# Optimizing a Trainium2 kernel written in Bass

```python
import numpy as np
import jax
import jax.numpy as jnp

def _softmax(x, axis=-1):
    return jax.nn.softmax(x, axis=axis)

def _gelu(x):
    return jax.nn.gelu(x, approximate=True)

def _silu(x):
    return jax.nn.silu(x)

def _sigmoid(x):
    return jax.nn.sigmoid(x)

def _layernorm(x, axis=-1, eps=1e-05):
    m = jnp.mean(x, axis=axis, keepdims=True)
    v = jnp.var(x, axis=axis, keepdims=True)
    return (x - m) / jnp.sqrt(v + eps)

def _scatter_add(tgt, idx, src, axis=0):
    return tgt.at[idx].add(src)

def _segment_sum(src, seg, n):
    return jax.ops.segment_sum(src, seg, n)
kernel_name = 'mk_adj_ffn_d2_adj_r2_08e925'

def setup_inputs(seed: int=0):
    np.random.seed(seed)
    _w = jnp.asarray

    def _rec_inputs():
        import jax
        import jax.numpy as jnp
        _gk = jax.random.key(seed)
        x = -0.0002928 + 1 * jax.random.normal(jax.random.fold_in(_gk, 1), (64, 128, 128), jnp.float32)
        _w = (1.0 + jnp.arange(128, dtype=jnp.float32)) ** (-0.5)
        _w = _w / _w.mean()
        _pij = jnp.clip(0.125 * _w[:, None] * _w[None, :], 0.0, 1.0)
        _a = jax.random.uniform(jax.random.fold_in(_gk, 2), (64, 128, 128)) < _pij
        adj = _a.astype(jnp.int32)
        _nm = jnp.ones((64, 128), dtype=bool)
        nodemask = jnp.where(_nm, 1.0, 0.0).astype(jnp.float32)
        return (x, adj, nodemask)
    x, adj, nodemask = _rec_inputs()

    def _L0_gnn_setup():
        import jax, jax.numpy as jnp
        import numpy as np
        key = jax.random.key(seed)
        k1, k2, k3, k4 = jax.random.split(key, 4)
        B, N, F, U = (8, 1024, 128, 128)
        x = jax.random.normal(k1, (B, N, F), dtype=jnp.float32)
        adj = jax.random.randint(k2, (B, N, N), 0, 2, dtype=jnp.int32)
        W_msg = jax.random.normal(k3, (F, U), dtype=jnp.float32) / np.sqrt(F)
        W_upd = jax.random.normal(k4, (F, U), dtype=jnp.float32) / np.sqrt(F)
        bias = jnp.zeros((U,), dtype=jnp.float32)
        return {'x': x, 'adj': adj, 'W_msg': W_msg, 'W_upd': W_upd, 'bias': bias}
    _L0_gnn_all = _L0_gnn_setup()
    _L0_gnn_in = {k: v for k, v in _L0_gnn_all.items() if k in ('W_msg', 'W_upd', 'bias')}
    del _L0_gnn_all

    def _L0_ffn_setup():
        import jax, jax.numpy as jnp
        import numpy as np
        BN_EPS = 0.001

        def _bn(h, g, b, m, v):
            return g * (h - m) * jax.lax.rsqrt(v + BN_EPS) + b
        key = jax.random.key(seed)
        ks = jax.random.split(key, 8)
        B, F, Df = (128, 64, 128)
        E, H, D = (8, 128, 128)
        s1 = 1.0 / np.sqrt(Df)
        s2 = 1.0 / np.sqrt(H)
        return {'x': jax.random.normal(ks[0], (B, F, Df), jnp.float32), 'Wr': jax.random.normal(ks[1], (Df, E), jnp.float32) * s1, 'br': jnp.zeros((E,), jnp.float32), 'W1': jax.random.normal(ks[2], (E, Df, H), jnp.float32) * s1, 'b1': jnp.zeros((E, H), jnp.float32), 'g1': jnp.ones((E, H), jnp.float32), 'be1': jnp.zeros((E, H), jnp.float32), 'm1': jnp.zeros((E, H), jnp.float32), 'v1': jnp.ones((E, H), jnp.float32), 'W2': jax.random.normal(ks[3], (E, H, H), jnp.float32) * s2, 'b2': jnp.zeros((E, H), jnp.float32), 'g2': jnp.ones((E, H), jnp.float32), 'be2': jnp.zeros((E, H), jnp.float32), 'm2': jnp.zeros((E, H), jnp.float32), 'v2': jnp.ones((E, H), jnp.float32), 'Wo': jax.random.normal(ks[4], (E, H, D), jnp.float32) * s2, 'bo': jnp.zeros((E, D), jnp.float32)}
    _L0_ffn_all = _L0_ffn_setup()
    _L0_ffn_in = {k: v for k, v in _L0_ffn_all.items() if k in ('Wr', 'br', 'W1', 'b1', 'g1', 'be1', 'm1', 'v1', 'W2', 'b2', 'g2', 'be2', 'm2', 'v2', 'Wo', 'bo')}
    del _L0_ffn_all

    def _L1_gnn_setup():
        import jax, jax.numpy as jnp
        import numpy as np
        D_MODEL = 128
        NUM_REL = 40

        def _direction(x, W, Wg, b, bg, adj, rel_ids):
            h = x @ W.T
            g = h @ Wg.T
            vals = (h[:, :, None, :] + b) * jax.nn.sigmoid(g[:, :, None, :] + bg)
            onehot = (adj[..., None] == rel_ids).astype(h.dtype)
            return jnp.einsum('bnmr,bmrd->bnd', onehot, vals)
        key = jax.random.key(seed)
        ks = jax.random.split(key, 16)
        B, N, d = (2, 256, D_MODEL)
        s = 0.02
        inp = {'node': jax.random.normal(ks[0], (B, N, d), dtype=jnp.float32), 'node_mask': jnp.ones((B, N), dtype=jnp.float32), 'adj_mat': jax.random.randint(ks[1], (B, N, N), 0, 41, dtype=jnp.int32), 'W_fwd': jax.random.normal(ks[2], (d, d), dtype=jnp.float32) * s, 'W_bwd': jax.random.normal(ks[3], (d, d), dtype=jnp.float32) * s, 'W_loop': jax.random.normal(ks[4], (d, d), dtype=jnp.float32) * s, 'Wg_fwd': jax.random.normal(ks[5], (d, d), dtype=jnp.float32) * s, 'Wg_bwd': jax.random.normal(ks[6], (d, d), dtype=jnp.float32) * s, 'Wg_loop': jax.random.normal(ks[7], (d, d), dtype=jnp.float32) * s, 'b_fwd': jax.random.normal(ks[8], (NUM_REL - 1, d), dtype=jnp.float32) * s, 'b_bwd': jax.random.normal(ks[9], (NUM_REL - 1, d), dtype=jnp.float32) * s, 'b_loop': jax.random.normal(ks[10], (1, d), dtype=jnp.float32) * s, 'bg_fwd': jax.random.normal(ks[11], (NUM_REL - 1, d), dtype=jnp.float32) * s, 'bg_bwd': jax.random.normal(ks[12], (NUM_REL - 1, d), dtype=jnp.float32) * s, 'bg_loop': jax.random.normal(ks[13], (1, d), dtype=jnp.float32) * s}
        return inp
    _L1_gnn_all = _L1_gnn_setup()
    _L1_gnn_in = {k: v for k, v in _L1_gnn_all.items() if k in ('W_fwd', 'W_bwd', 'W_loop', 'Wg_fwd', 'Wg_bwd', 'Wg_loop', 'b_fwd', 'b_bwd', 'b_loop', 'bg_fwd', 'bg_bwd', 'bg_loop')}
    del _L1_gnn_all

    def _L1_ffn_setup():
        import jax, jax.numpy as jnp
        import numpy as np
        B, S, D_MODEL, FFN, P = (8, 2048, 128, 512, 8)
        BLK = 128
        key = jax.random.key(seed)
        ks = jax.random.split(key, 12)
        x = jax.random.normal(ks[0], (B, S, D_MODEL), jnp.float32)
        Wt = 0.05 * jax.random.normal(ks[1], (FFN, D_MODEL), jnp.float32)
        bt = 0.05 * jax.random.normal(ks[2], (FFN,), jnp.float32)
        sl_cvx = 1.0 + 0.1 * jax.random.normal(ks[3], (FFN, P), jnp.float32)
        of_cvx = 0.1 * jax.random.normal(ks[4], (FFN, P), jnp.float32)
        sl_ccv = 1.0 + 0.1 * jax.random.normal(ks[5], (FFN, P), jnp.float32)
        of_ccv = 0.1 * jax.random.normal(ks[6], (FFN, P), jnp.float32)
        alpha = jnp.zeros((FFN,), jnp.float32)
        Wc = jax.random.normal(ks[7], (D_MODEL, FFN), jnp.float32) / np.sqrt(D_MODEL)
        bc = jnp.zeros((FFN,), jnp.float32)
        Wg = 0.01 * jax.random.normal(ks[8], (D_MODEL, FFN), jnp.float32)
        bg = 2.0 * jnp.ones((FFN,), jnp.float32)
        Wd = jax.random.normal(ks[9], (FFN, D_MODEL), jnp.float32) / np.sqrt(FFN)
        bd = jnp.zeros((D_MODEL,), jnp.float32)
        return {'x': x, 'Wt': Wt, 'bt': bt, 'sl_cvx': sl_cvx, 'of_cvx': of_cvx, 'sl_ccv': sl_ccv, 'of_ccv': of_ccv, 'alpha': alpha, 'Wc': Wc, 'bc': bc, 'Wg': Wg, 'bg': bg, 'Wd': Wd, 'bd': bd}
    _L1_ffn_all = _L1_ffn_setup()
    _L1_ffn_in = {k: v for k, v in _L1_ffn_all.items() if k in ('Wt', 'bt', 'sl_cvx', 'of_cvx', 'sl_ccv', 'of_ccv', 'alpha', 'Wc', 'bc', 'Wg', 'bg', 'Wd', 'bd')}
    del _L1_ffn_all
    return {'x': x, 'adj': adj, 'nodemask': nodemask, 'L0_gnn_W_msg': _L0_gnn_in['W_msg'], 'L0_gnn_W_upd': _L0_gnn_in['W_upd'], 'L0_gnn_bias': _L0_gnn_in['bias'], 'L0_ffn_Wr': _L0_ffn_in['Wr'], 'L0_ffn_br': _L0_ffn_in['br'], 'L0_ffn_W1': _L0_ffn_in['W1'], 'L0_ffn_b1': _L0_ffn_in['b1'], 'L0_ffn_g1': _L0_ffn_in['g1'], 'L0_ffn_be1': _L0_ffn_in['be1'], 'L0_ffn_m1': _L0_ffn_in['m1'], 'L0_ffn_v1': _L0_ffn_in['v1'], 'L0_ffn_W2': _L0_ffn_in['W2'], 'L0_ffn_b2': _L0_ffn_in['b2'], 'L0_ffn_g2': _L0_ffn_in['g2'], 'L0_ffn_be2': _L0_ffn_in['be2'], 'L0_ffn_m2': _L0_ffn_in['m2'], 'L0_ffn_v2': _L0_ffn_in['v2'], 'L0_ffn_Wo': _L0_ffn_in['Wo'], 'L0_ffn_bo': _L0_ffn_in['bo'], 'L1_gnn_W_fwd': _L1_gnn_in['W_fwd'], 'L1_gnn_W_bwd': _L1_gnn_in['W_bwd'], 'L1_gnn_W_loop': _L1_gnn_in['W_loop'], 'L1_gnn_Wg_fwd': _L1_gnn_in['Wg_fwd'], 'L1_gnn_Wg_bwd': _L1_gnn_in['Wg_bwd'], 'L1_gnn_Wg_loop': _L1_gnn_in['Wg_loop'], 'L1_gnn_b_fwd': _L1_gnn_in['b_fwd'], 'L1_gnn_b_bwd': _L1_gnn_in['b_bwd'], 'L1_gnn_b_loop': _L1_gnn_in['b_loop'], 'L1_gnn_bg_fwd': _L1_gnn_in['bg_fwd'], 'L1_gnn_bg_bwd': _L1_gnn_in['bg_bwd'], 'L1_gnn_bg_loop': _L1_gnn_in['bg_loop'], 'L1_ffn_Wt': _L1_ffn_in['Wt'], 'L1_ffn_bt': _L1_ffn_in['bt'], 'L1_ffn_sl_cvx': _L1_ffn_in['sl_cvx'], 'L1_ffn_of_cvx': _L1_ffn_in['of_cvx'], 'L1_ffn_sl_ccv': _L1_ffn_in['sl_ccv'], 'L1_ffn_of_ccv': _L1_ffn_in['of_ccv'], 'L1_ffn_alpha': _L1_ffn_in['alpha'], 'L1_ffn_Wc': _L1_ffn_in['Wc'], 'L1_ffn_bc': _L1_ffn_in['bc'], 'L1_ffn_Wg': _L1_ffn_in['Wg'], 'L1_ffn_bg': _L1_ffn_in['bg'], 'L1_ffn_Wd': _L1_ffn_in['Wd'], 'L1_ffn_bd': _L1_ffn_in['bd']}

def reference(x, adj, nodemask, L0_gnn_W_msg, L0_gnn_W_upd, L0_gnn_bias, L0_ffn_Wr, L0_ffn_br, L0_ffn_W1, L0_ffn_b1, L0_ffn_g1, L0_ffn_be1, L0_ffn_m1, L0_ffn_v1, L0_ffn_W2, L0_ffn_b2, L0_ffn_g2, L0_ffn_be2, L0_ffn_m2, L0_ffn_v2, L0_ffn_Wo, L0_ffn_bo, L1_gnn_W_fwd, L1_gnn_W_bwd, L1_gnn_W_loop, L1_gnn_Wg_fwd, L1_gnn_Wg_bwd, L1_gnn_Wg_loop, L1_gnn_b_fwd, L1_gnn_b_bwd, L1_gnn_b_loop, L1_gnn_bg_fwd, L1_gnn_bg_bwd, L1_gnn_bg_loop, L1_ffn_Wt, L1_ffn_bt, L1_ffn_sl_cvx, L1_ffn_of_cvx, L1_ffn_sl_ccv, L1_ffn_of_ccv, L1_ffn_alpha, L1_ffn_Wc, L1_ffn_bc, L1_ffn_Wg, L1_ffn_bg, L1_ffn_Wd, L1_ffn_bd):
    import jax
    import jax.numpy as jnp

    def _L0_gnn_ref(x, adj, W_msg, W_upd, bias):
        import jax, jax.numpy as jnp
        import numpy as np
        a = adj.astype(x.dtype)
        h = jnp.einsum('bnf,fu->bnu', x, W_msg)
        msg_sum = jnp.einsum('bij,biu->bju', a, h)
        deg = jnp.sum(a, axis=1)
        messages = jnp.where(deg[..., None] > 0, msg_sum / jnp.maximum(deg, 1.0)[..., None], 0.0)
        out = jnp.einsum('bnf,fu->bnu', x, W_upd) + messages + bias
        return jax.nn.relu(out)

    def _L0_ffn_ref(x, Wr, br, W1, b1, g1, be1, m1, v1, W2, b2, g2, be2, m2, v2, Wo, bo):
        import jax, jax.numpy as jnp
        import numpy as np
        BN_EPS = 0.001

        def _bn(h, g, b, m, v):
            return g * (h - m) * jax.lax.rsqrt(v + BN_EPS) + b
        feat = jnp.mean(x, axis=0)
        w = jax.nn.softmax(feat @ Wr + br, axis=-1)
        h = jnp.einsum('bfd,edh->bfeh', x, W1) + b1
        h = jax.nn.relu(_bn(h, g1, be1, m1, v1))
        h = jnp.einsum('bfeh,ehk->bfek', h, W2) + b2
        h = jax.nn.relu(_bn(h, g2, be2, m2, v2))
        y = jnp.einsum('bfeh,ehd->bfed', h, Wo) + bo
        return jnp.einsum('bfed,fe->bfd', y, w)

    def _L1_gnn_ref(node, node_mask, adj_mat, W_fwd, W_bwd, W_loop, Wg_fwd, Wg_bwd, Wg_loop, b_fwd, b_bwd, b_loop, bg_fwd, bg_bwd, bg_loop):
        import jax, jax.numpy as jnp
        import numpy as np
        D_MODEL = 128
        NUM_REL = 40

        def _direction(x, W, Wg, b, bg, adj, rel_ids):
            h = x @ W.T
            g = h @ Wg.T
            vals = (h[:, :, None, :] + b) * jax.nn.sigmoid(g[:, :, None, :] + bg)
            onehot = (adj[..., None] == rel_ids).astype(h.dtype)
            return jnp.einsum('bnmr,bmrd->bnd', onehot, vals)
        rels = jnp.arange(2, NUM_REL + 1, dtype=adj_mat.dtype)
        rel1 = jnp.array([1], dtype=adj_mat.dtype)
        adj_t = jnp.swapaxes(adj_mat, -1, -2)
        out = _direction(node, W_fwd, Wg_fwd, b_fwd, bg_fwd, adj_mat, rels)
        out = out + _direction(node, W_bwd, Wg_bwd, b_bwd, bg_bwd, adj_t, rels)
        out = out + _direction(node, W_loop, Wg_loop, b_loop, bg_loop, adj_t, rel1)
        return jax.nn.relu(out)

    def _L1_ffn_ref(x, Wt, bt, sl_cvx, of_cvx, sl_ccv, of_ccv, alpha, Wc, bc, Wg, bg, Wd, bd):
        import jax, jax.numpy as jnp
        import numpy as np
        B, S, D_MODEL, FFN, P = (8, 2048, 128, 512, 8)
        BLK = 128
        Bx, Sx, D = x.shape
        T = Bx * Sx
        xf = x.reshape(T, D)
        xb = xf.reshape(T // BLK, BLK, D)
        s = jax.nn.sigmoid(alpha)

        def blk_fn(xx):
            t = jnp.max(xx[:, None, :] + Wt[None, :, :], axis=-1) + bt
            z = t[:, :, None]
            cvx = jnp.max(z * sl_cvx[None] + of_cvx[None], axis=-1)
            ccv = jnp.min(z * sl_ccv[None] + of_ccv[None], axis=-1)
            return s * cvx + (1.0 - s) * ccv
        trop = jax.lax.map(blk_fn, xb).reshape(T, FFN)
        classical = jax.nn.gelu(xf @ Wc + bc, approximate=False)
        g = jax.nn.sigmoid(xf @ Wg + bg)
        fused = g * trop + (1.0 - g) * classical
        out = fused @ Wd + bd
        return out.reshape(Bx, Sx, D)
    x = x + _L0_gnn_ref(_layernorm(x, axis=-1), adj, L0_gnn_W_msg, L0_gnn_W_upd, L0_gnn_bias)
    x = x + _L0_ffn_ref(_layernorm(x, axis=-1), L0_ffn_Wr, L0_ffn_br, L0_ffn_W1, L0_ffn_b1, L0_ffn_g1, L0_ffn_be1, L0_ffn_m1, L0_ffn_v1, L0_ffn_W2, L0_ffn_b2, L0_ffn_g2, L0_ffn_be2, L0_ffn_m2, L0_ffn_v2, L0_ffn_Wo, L0_ffn_bo)
    x = x + _L1_gnn_ref(_layernorm(x, axis=-1), nodemask, adj, L1_gnn_W_fwd, L1_gnn_W_bwd, L1_gnn_W_loop, L1_gnn_Wg_fwd, L1_gnn_Wg_bwd, L1_gnn_Wg_loop, L1_gnn_b_fwd, L1_gnn_b_bwd, L1_gnn_b_loop, L1_gnn_bg_fwd, L1_gnn_bg_bwd, L1_gnn_bg_loop)
    x = x + _L1_ffn_ref(_layernorm(x, axis=-1), L1_ffn_Wt, L1_ffn_bt, L1_ffn_sl_cvx, L1_ffn_of_cvx, L1_ffn_sl_ccv, L1_ffn_of_ccv, L1_ffn_alpha, L1_ffn_Wc, L1_ffn_bc, L1_ffn_Wg, L1_ffn_bg, L1_ffn_Wd, L1_ffn_bd)
    return x

_drawn_inputs = setup_inputs


def setup_inputs(seed=0):
    import zlib

    import numpy as np

    out = dict(_drawn_inputs(seed))
    spreads = {'L0_gnn_bias': (0.0, 0.1),
     'L0_ffn_br': (0.0, 0.442),
     'L0_ffn_b1': (0.0, 0.768),
     'L0_ffn_g1': (1.0, 0.6),
     'L0_ffn_be1': (0.0, 0.783),
     'L0_ffn_m1': (0.0, 0.721),
     'L0_ffn_v1': (1.0, 0.6),
     'L0_ffn_b2': (0.0, 0.433),
     'L0_ffn_g2': (1.0, 0.6),
     'L0_ffn_be2': (0.0, 0.504),
     'L0_ffn_m2': (0.0, 0.462),
     'L0_ffn_v2': (1.0, 0.6),
     'L0_ffn_bo': (0.0, 0.329),
     'L1_ffn_alpha': (0.0, 0.8),
     'L1_ffn_bc': (0.0, 2.0),
     'L1_ffn_bg': (2.0, 0.2),
     'L1_ffn_bd': (0.0, 0.277)}
    factors = {'L0_ffn_Wr': 4.783,
     'L1_gnn_Wg_loop': 8.0,
     'L1_gnn_bg_loop': 8.0,
     'L1_ffn_Wt': 3.852,
     'L1_ffn_bt': 3.833,
     'L1_ffn_of_cvx': 4.127,
     'L1_ffn_of_ccv': 4.369,
     'L1_ffn_Wg': 4.777}
    for name, (base, spread) in spreads.items():
        noise = np.random.default_rng([zlib.crc32(name.encode()), seed]).standard_normal(out[name].shape)
        drawn = base * np.exp(spread * noise) if base else spread * noise
        out[name] = jnp.asarray(drawn.astype(out[name].dtype))
    for name, factor in factors.items():
        out[name] = (out[name] * factor).astype(out[name].dtype)
    return out
```

```python
from contextlib import ExitStack

import concourse.bass as bass
from concourse import mybir

ALU = mybir.AluOpType
ACT = mybir.ActivationFunctionType
AX = mybir.AxisListType
F32 = mybir.dt.float32
BF16 = mybir.dt.bfloat16
I32 = mybir.dt.int32
U32 = mybir.dt.uint32

P = 128
NT = 64
E = 8
NC = 4
NH = NC * P
G4 = 4
NG = NT // G4
GW = G4 * P
NL = 8
NREL = 39
LN_EPS = 1e-5
BN_EPS = 1e-3
LOWEST = -3.0e38
RING = 8
PWL_OPS = 18


def wait(eng, sem, value):
    if not (isinstance(value, int) and value <= 0):
        eng.wait_ge(sem, value)


def build(nc, a, out):
    with ExitStack() as ctx:
        def sb(name, shape, dt=F32):
            return ctx.enter_context(nc.sbuf_tensor(name, shape, dt))

        def sem(name):
            return ctx.enter_context(nc.semaphore(name))

        X = sb("X", [P, NT * P])
        M1 = sb("M1", [P, NT * P], BF16)
        EX = sb("EX", [P, NT * P])
        STATS = sb("STATS", [P, NT, 6])
        MEAN = sb("MEAN", [P, NT])
        RSTD = sb("RSTD", [P, NT])
        FLG = sb("FLG", [P, NT])
        ident = sb("ident", [P, P])
        ones = sb("ones", [P, P])
        pidx = sb("pidx", [P, P])
        PAR = sb("PAR", [96, P])
        PT = sb("PT", [P, 96])
        WMU = sb("WMU", [P, 2 * P])
        b0row = sb("b0row", [1, 2 * P])
        Wr = sb("Wr", [P, E])
        brrow = sb("brrow", [1, E])
        W1 = sb("W1", [P, E, P])
        W2 = sb("W2", [P, E, P])
        Wo = sb("Wo", [P, E, P])
        bo = sb("bo", [E, P])
        WG = sb("WG", [P, 6, P])
        WHG = sb("WHG", [P, 3, 2, P])
        b1row = sb("b1row", [1, 2 * P])
        B4 = sb("B4", [P, 4 * P])
        WtS = sb("WtS", [P, NC, P])
        SL = sb("SL", [P, NC, 2 * NL])
        OF = sb("OF", [P, NC, 2 * NL])
        Wc = sb("Wc", [P, NH])
        Wg = sb("Wg", [P, NH])
        Wd = sb("Wd", [P, NC, P])
        bdrow = sb("bdrow", [1, G4 * P])
        sc1 = sb("sc1", [P, E])
        c1 = sb("c1", [P, E])
        nc2 = sb("nc2", [P, E])
        bgh = sb("bgh", [P, NC])
        WB = sb("WB", [P, E, P])
        CW = sb("CW", [P, P])
        small = sb("small", [P, 16, NT])
        flag = sb("flag", [1, 2], I32)
        WORK = 13312
        work = sb("work", [P, WORK])

        PS = [ctx.enter_context(nc.psum_tensor(f"ps{i}", [P, 512], F32)) for i in range(8)]

        class Carve:
            def __init__(self):
                self.at = 0

            def __call__(self, n):
                v = work[:, self.at:self.at + n]
                self.at += n
                assert self.at <= WORK
                return v

        bt_at, al_at, bc_at, bg_at = 80, 84, 88, 92

        params_loaded, weights_loaded, x_loaded = sem("params_loaded"), sem("weights_loaded"), sem("x_loaded")
        pool_made, pe_setup, act_setup, dve_setup = sem("pool_made"), sem("pe_setup"), sem("act_setup"), sem("dve_setup")
        carve = Carve()
        bc_scale = carve(E * P)
        WgT = carve(3 * P)
        names = ["b1", "g1", "be1", "m1", "v1", "b2", "g2", "be2", "m2", "v2"]
        loads = [(WMU[:, 0:P], a["L0_gnn_W_msg"]), (WMU[:, P:2 * P], a["L0_gnn_W_upd"]),
                 (b0row[0:1, P:2 * P], a["L0_gnn_bias"].rearrange("(o d) -> o d", o=1)),
                 (Wr[:, :], a["L0_ffn_Wr"]), (brrow[:, :], a["L0_ffn_br"].rearrange("(o d) -> o d", o=1)),
                 (W1[:, :, :], a["L0_ffn_W1"].rearrange("e d h -> d e h")),
                 (W2[:, :, :], a["L0_ffn_W2"].rearrange("e d h -> d e h")),
                 (Wo[:, :, :], a["L0_ffn_Wo"].rearrange("e d h -> d e h")),
                 (bo[:, :], a["L0_ffn_bo"]),
                 (WG[:, 0, :], a["L1_gnn_W_fwd"]), (WG[:, 1, :], a["L1_gnn_W_bwd"]), (WG[:, 2, :], a["L1_gnn_W_loop"]),
                 (WG[:, 3, :], a["L1_gnn_Wg_fwd"]), (WG[:, 4, :], a["L1_gnn_Wg_bwd"]), (WG[:, 5, :], a["L1_gnn_Wg_loop"]),
                 (b1row[:, 0:P], a["L1_gnn_b_loop"]), (b1row[:, P:2 * P], a["L1_gnn_bg_loop"]),
                 (WtS[:, :, :], a["L1_ffn_Wt"].rearrange("(c f) d -> f c d", c=NC)),
                 (SL[:, :, 0:NL], a["L1_ffn_sl_cvx"].rearrange("(c f) l -> f c l", c=NC)),
                 (SL[:, :, NL:2 * NL], a["L1_ffn_sl_ccv"].rearrange("(c f) l -> f c l", c=NC)),
                 (OF[:, :, 0:NL], a["L1_ffn_of_cvx"].rearrange("(c f) l -> f c l", c=NC)),
                 (OF[:, :, NL:2 * NL], a["L1_ffn_of_ccv"].rearrange("(c f) l -> f c l", c=NC)),
                 (Wc[:, :], a["L1_ffn_Wc"]), (Wg[:, :], a["L1_ffn_Wg"]),
                 (Wd[:, :, :], a["L1_ffn_Wd"].rearrange("(c f) d -> f c d", c=NC))]
        loads += [(bdrow[:, j * P:(j + 1) * P], a["L1_ffn_bd"].rearrange("(o d) -> o d", o=1)) for j in range(G4)]
        relation_rows = ["L1_gnn_b_fwd", "L1_gnn_bg_fwd", "L1_gnn_b_bwd", "L1_gnn_bg_bwd"]

        class Chain:
            def __init__(self, eng, sem, base=0):
                self.eng, self.sem, self.n = eng, sem, base

            def __call__(self, ins):
                ins.then_inc(self.sem, 1)
                self.n += 1
                self.eng.wait_ge(self.sem, self.n)

        def rsqrt_after_sqrt(link, dve, v, root, r, t):
            link(dve.reciprocal(r, root))
            link(dve.tensor_tensor(t, r, r, ALU.mult))
            link(dve.tensor_tensor(t, t, v, ALU.mult))
            link(dve.tensor_scalar(t, t, -0.5, 1.5, ALU.mult, ALU.add))
            link(dve.tensor_tensor(r, r, t, ALU.mult))

        S = [small[:, i, :] for i in range(16)]

        def variance(link, dve):
            ev, od = STATS[:, :, 1], STATS[:, :, 4]
            link(dve.tensor_tensor(S[1], ev, od, ALU.add))
            link(dve.tensor_scalar(MEAN[:, :], S[1], 0.5, None, ALU.mult))
            link(dve.tensor_tensor(S[1], ev, od, ALU.subtract))
            link(dve.tensor_tensor(S[1], S[1], S[1], ALU.mult))
            link(dve.tensor_tensor(S[2], STATS[:, :, 2], STATS[:, :, 5], ALU.add))
            link(dve.tensor_scalar(S[2], S[2], 1.0 / P, LN_EPS, ALU.mult, ALU.add))
            link(dve.scalar_tensor_tensor(S[0], S[1], 0.25, S[2], ALU.mult, ALU.add))

        def layer_norm_scales(name):
            steps, rooted = sem(name + "_dve"), sem(name + "_root")
            with nc.Block() as block:
                @block.vector
                def _(dve):
                    link = Chain(dve, steps)
                    variance(link, dve)
                    dve.wait_ge(rooted, 1)
                    rsqrt_after_sqrt(link, dve, S[0], S[3], RSTD[:, :], S[1])

                @block.scalar
                def _(act):
                    act.wait_ge(steps, 7)
                    act.activation(S[3], S[0], ACT.Sqrt).then_inc(rooted, 1)

        with nc.Block() as block:
            @block.sync
            def _(sp):
                for i, n in enumerate(names):
                    sp.dma_start(PAR[8 * i:8 * i + 8, :], a["L0_ffn_" + n]).then_inc(params_loaded, 16)
                for at, n in ((bt_at, "bt"), (al_at, "alpha"), (bc_at, "bc"), (bg_at, "bg")):
                    sp.dma_start(PAR[at:at + NC, :], a["L1_ffn_" + n].rearrange("(c f) -> c f", c=NC)).then_inc(params_loaded, 16)
                for dst, src in loads:
                    sp.dma_start(dst, src).then_inc(weights_loaded, 16)
                sp.wait_ge(pool_made, 5)
                for i, n in enumerate(relation_rows):
                    sp.dma_start(B4[0:NREL, i * P:(i + 1) * P], a[n]).then_inc(weights_loaded, 16)

            N_WEIGHTS = 16 * (len(loads) + len(relation_rows))

            @block.scalar
            def _(act):
                for i in range(4):
                    n = NT // 4
                    act.dma_start(X[:, i * n * P:(i + 1) * n * P].rearrange("p (t d) -> p t d", d=P),
                                  a["x"][i * n:(i + 1) * n].rearrange("t p d -> p t d")).then_inc(x_loaded, 16)
                act.wait_ge(pe_setup, 1)
                act.copy(PT[:, :], PS[0][:, 0:96]).then_inc(act_setup, 1)
                act.wait_ge(dve_setup, 2)
                act.activation(S[3][:, 0:16], S[0][:, 0:16], ACT.Sqrt).then_inc(act_setup, 1)
                act.activation(S[4][:, 0:NC], PT[:, al_at:al_at + NC], ACT.Sigmoid).then_inc(act_setup, 1)
                act.wait_ge(pe_setup, 3)
                act.copy(WHG[:, :, 0, :], PS[2][:, 0:3 * P].rearrange("p (i d) -> p i d", i=3)).then_inc(act_setup, 1)
                act.copy(WgT, PS[3][:, 0:3 * P]).then_inc(act_setup, 1)
                act.wait_ge(pe_setup, 4)
                act.copy(WHG[:, :, 1, :], PS[4][:, 0:3 * P].rearrange("p (i d) -> p i d", i=3)).then_inc(act_setup, 1)

            @block.gpsimd
            def _(pool):
                pool.memset(ones[:, :], 1.0).then_inc(pool_made, 1)
                pool.memset(ident[:, :], 0.0).then_inc(pool_made, 1)
                pool.wait_ge(pool_made, 2)
                pool.affine_select(out=ident[:, :], in_=ident[:, :], compare_op=ALU.not_equal, fill=1.0, base=0,
                                   pattern=[[-1, P]], channel_multiplier=1).then_inc(pool_made, 1)
                pool.iota(pidx[:, :], [[0, P]], base=0, channel_multiplier=1,
                          allow_small_or_imprecise_dtypes=True).then_inc(pool_made, 1)
                pool.memset(B4[:, :], 0.0).then_inc(pool_made, 1)
                pool.memset(b0row[:, 0:P], 0.0).then_inc(pool_made, 1)
                pool.memset(EX[:, :], 0.0).then_inc(pool_made, 1)

            @block.tensor
            def _(pe):
                pe.wait_ge(pool_made, 4)
                pe.wait_ge(params_loaded, 16 * 14)
                pe.transpose(PS[0][:, 0:96], PAR[:, :], ident[0:96, 0:96]).then_inc(pe_setup, 1)
                pe.wait_ge(weights_loaded, N_WEIGHTS)
                for i in range(6):
                    bank = PS[2 + i // 3]
                    last = pe.transpose(bank[:, (i % 3) * P:(i % 3 + 1) * P], WG[:, i, :], ident[:, :])
                    if i % 3 == 2:
                        last.then_inc(pe_setup, 1)
                pe.wait_ge(act_setup, 5)
                for i in range(3):
                    last = pe.matmul(PS[4][:, i * P:(i + 1) * P], WG[:, i, :], WgT[:, i * P:(i + 1) * P],
                                     start=True, stop=True)
                last.then_inc(pe_setup, 1)
                pe.wait_ge(dve_setup, 3)
                for e in range(E):
                    last = pe.matmul(PS[5 + e // 4][:, (e % 4) * P:(e % 4 + 1) * P],
                                     bc_scale[:, e * P:(e + 1) * P], ident[:, :], start=True, stop=True)
                last.then_inc(pe_setup, 1)

            dve_chain, x_stats = sem("dve_chain"), sem("x_stats")

            @block.vector
            def _(dve):
                link = Chain(dve, dve_chain)

                def col(name, n=E):
                    at = 8 * names.index(name)
                    return PT[:, at:at + n]

                dve.wait_ge(act_setup, 1)
                dve.tensor_scalar(S[0][:, 0:8], col("v1"), BN_EPS, None, ALU.add).then_inc(dve_setup, 1)
                dve.tensor_scalar(S[0][:, 8:16], col("v2"), BN_EPS, None, ALU.add).then_inc(dve_setup, 1)
                dve.wait_ge(act_setup, 3)
                dve.wait_ge(dve_setup, 2)
                rsqrt_after_sqrt(link, dve, S[0][:, 0:16], S[3][:, 0:16], S[5][:, 0:16], S[1][:, 0:16])
                link(dve.tensor_tensor(sc1[:, :], col("g1"), S[5][:, 0:8], ALU.mult))
                link(dve.tensor_tensor(c1[:, :], col("b1"), col("m1"), ALU.subtract))
                link(dve.tensor_tensor(c1[:, :], c1[:, :], sc1[:, :], ALU.mult))
                link(dve.tensor_tensor(c1[:, :], c1[:, :], col("be1"), ALU.add))
                sc2 = S[6][:, 0:8]
                link(dve.tensor_tensor(sc2, col("g2"), S[5][:, 8:16], ALU.mult))
                link(dve.tensor_tensor(nc2[:, :], col("m2"), col("b2"), ALU.subtract))
                link(dve.tensor_tensor(nc2[:, :], nc2[:, :], sc2, ALU.mult))
                link(dve.tensor_tensor(nc2[:, :], nc2[:, :], col("be2"), ALU.subtract))
                dve.tensor_copy(bc_scale.rearrange("p (e k) -> p e k", e=E),
                                sc2.unsqueeze(2).to_broadcast([P, E, P])).then_inc(dve_setup, 1)
                link(dve.tensor_scalar(S[7][:, 0:NC], S[4][:, 0:NC], -1.0, 1.0, ALU.mult, ALU.add))
                link(dve.tensor_scalar(bgh[:, :], PT[:, bg_at:bg_at + NC], 0.5, None, ALU.mult))
                dve.wait_ge(weights_loaded, N_WEIGHTS)
                for c in range(NC):
                    link(dve.scalar_tensor_tensor(OF[:, c, :], SL[:, c, :], PT[:, bt_at + c:bt_at + c + 1], OF[:, c, :],
                                                  ALU.mult, ALU.add))
                    for t in (SL, OF):
                        link(dve.tensor_scalar(t[:, c, 0:NL], t[:, c, 0:NL], S[4][:, c:c + 1], None, ALU.mult))
                        link(dve.tensor_scalar(t[:, c, NL:2 * NL], t[:, c, NL:2 * NL], S[7][:, c:c + 1], None, ALU.mult))
                dve.wait_ge(pe_setup, 5)
                for h in range(2):
                    w = W2[:, 4 * h:4 * h + 4, :].rearrange("p e k -> p (e k)")
                    link(dve.tensor_tensor(w, PS[5 + h][:, :], w, ALU.mult))
                dve.wait_ge(x_loaded, 64)
                with dve.Fori(0, NT) as t:
                    dve.bn_stats(STATS[:, bass.ds(t, 1), :].rearrange("p o s -> p (o s)"),
                                 X[:, bass.ds(t * P, P)]).then_inc(x_stats, 1)

        layer_norm_scales("ln1")

        def normalise(dve, dst, t):
            return dve.tensor_scalar(dst, X[:, bass.ds(t * P, P)], MEAN[:, bass.ds(t, 1)], RSTD[:, bass.ds(t, 1)],
                                     ALU.subtract, ALU.mult)

        def tile_stats(dve, t):
            return dve.bn_stats(STATS[:, bass.ds(t, 1), :].rearrange("p o s -> p (o s)"), X[:, bass.ds(t * P, P)])

        carve = Carve()
        adj_i = [carve(P).bitcast(I32) for _ in range(2)]
        adj_f = [carve(P) for _ in range(2)]
        xn = [carve(P) for _ in range(2)]
        xT = [carve(P) for _ in range(2)]
        hu = [carve(2 * (P + 1)) for _ in range(2)]
        tmp = [carve(P) for _ in range(2)]
        deg = [carve(4) for _ in range(2)]
        with nc.Block() as block:
            adj_loaded = [sem("adj_loaded0"), sem("adj_loaded1")]
            adj_cast, adj_masked = sem("adj_cast"), sem("adj_masked")
            xn_ready, xn_turned, xT_ready = sem("p1_xn_ready"), sem("p1_xn_turned"), sem("p1_xT_ready")
            hu_summed, hu_ready, msg_summed, msg_used = sem("hu_summed"), sem("hu_ready"), sem("msg_summed"), sem("msg_used")
            back_steps, x1_ready = sem("p1_back_steps"), sem("x1_ready")
            ones_set = sem("ones_set")

            @block.sync
            def _(sp):
                for p in range(2):
                    sp.dma_start(adj_i[p], a["adj"][p]).then_inc(adj_loaded[p], 16)
                with sp.Fori(0, NT // 2 - 1) as i:
                    for p in range(2):
                        t = i * 2 + p
                        sp.wait_ge(adj_cast, t + 1)
                        sp.wait_ge(adj_masked, t + 1)
                        sp.dma_start(adj_i[p], a["adj"][bass.ds(t + 2, 1)].rearrange("o p j -> (o p) j")).then_inc(adj_loaded[p], 16)

            @block.gpsimd
            def _(pool):
                for p in range(2):
                    pool.memset(hu[p][:, P:P + 1], 1.0).then_inc(ones_set, 1)

            @block.tensor
            def _(pe):
                def turn(t, p):
                    pe.wait_ge(xn_ready, t + 1)
                    wait(pe, xT_ready, t - 1)
                    pe.transpose(PS[p][:, 0:P], xn[p], ident[:, :]).then_inc(xn_turned, 1)

                def project(t, p):
                    pe.wait_ge(xT_ready, t + 1)
                    wait(pe, hu_ready, t - 1)
                    pe.matmul(PS[2 + p][:, 0:2 * P], ones[0:1, :], b0row[:, :], start=True, stop=False)
                    pe.matmul(PS[2 + p][:, 0:2 * P], xT[p], WMU[:, :], start=False, stop=True).then_inc(hu_summed, 1)

                def gather(t, p):
                    pe.wait_ge(hu_ready, t + 1)
                    pe.wait_ge(adj_cast, t + 1)
                    wait(pe, msg_used, t - 1)
                    pe.matmul(PS[4 + p][:, 0:P + 1], adj_f[p], hu[p][:, 0:P + 1], start=True, stop=True).then_inc(msg_summed, 1)

                pe.wait_ge(ones_set, 2)
                turn(0, 0)
                project(0, 0)
                turn(1, 1)
                gather(0, 0)
                project(1, 1)
                with pe.Fori(1, NT // 2) as i:
                    for p in range(2):
                        t = i * 2 + p
                        turn(t, p)
                        gather(t - 1, 1 - p)
                        project(t, p)
                gather(NT - 1, 1)

            @block.scalar
            def _(act):
                def tile(i, p):
                    t = i * 2 + p
                    act.wait_ge(adj_loaded[p], i * 16 + 16)
                    wait(act, msg_summed, t - 1)
                    act.copy(adj_f[p], adj_i[p]).then_inc(adj_cast, 1)
                    act.wait_ge(xn_turned, t + 1)
                    wait(act, hu_summed, t - 1)
                    act.copy(xT[p], PS[p][:, 0:P]).then_inc(xT_ready, 1)
                    act.wait_ge(hu_summed, t + 1)
                    wait(act, msg_used, t - 1)
                    act.copy(hu[p].rearrange("p (s d) -> p s d", s=2)[:, :, 0:P],
                             PS[2 + p][:, 0:2 * P].rearrange("p (s d) -> p s d", s=2)).then_inc(hu_ready, 1)

                for p in range(2):
                    tile(0, p)
                with act.Fori(1, NT // 2) as i:
                    for p in range(2):
                        tile(i, p)

            @block.vector
            def _(dve):
                def front(i, p):
                    t = i * 2 + p
                    wait(dve, xn_turned, t - 1)
                    normalise(dve, xn[p], t).then_inc(xn_ready, 1)
                    dve.wait_ge(adj_loaded[p], i * 16 + 16)
                    dve.tensor_scalar(M1[:, bass.ds(t * P, P)], adj_i[p], 1.0, None, ALU.is_equal)
                    dve.tensor_reduce(FLG[:, bass.ds(t, 1)], adj_i[p], AX.X, ALU.max).then_inc(adj_masked, 1)

                def back(t, p):
                    m, d = PS[4 + p], deg[p]
                    dve.wait_ge(msg_summed, t + 1)
                    dve.tensor_scalar(d[:, 0:1], m[:, P:P + 1], 1.0, None, ALU.max).then_inc(back_steps, 1)
                    dve.wait_ge(back_steps, t * 4 + 1)
                    dve.reciprocal(d[:, 1:2], d[:, 0:1]).then_inc(back_steps, 1)
                    dve.wait_ge(back_steps, t * 4 + 2)
                    dve.scalar_tensor_tensor(d[:, 2:3], m[:, P:P + 1], 0.0, d[:, 1:2], ALU.is_gt, ALU.mult).then_inc(back_steps, 1)
                    dve.wait_ge(back_steps, t * 4 + 3)
                    dve.scalar_tensor_tensor(tmp[p], m[:, 0:P], d[:, 2:3], hu[p][:, P + 1:2 * P + 1],
                                             ALU.mult, ALU.add).then_inc(msg_used, 1)
                    x = X[:, bass.ds(t * P, P)]
                    dve.wait_ge(msg_used, t + 1)
                    dve.scalar_tensor_tensor(x, tmp[p], 0.0, x, ALU.max, ALU.add).then_inc(back_steps, 1)
                    dve.wait_ge(back_steps, t * 4 + 4)
                    tile_stats(dve, t).then_inc(x1_ready, 1)

                front(0, 0)
                front(0, 1)
                back(0, 0)
                with dve.Fori(1, NT // 2) as i:
                    front(i, 0)
                    back(i * 2 - 1, 1)
                    front(i, 1)
                    back(i * 2, 0)
                back(NT - 1, 1)

        layer_norm_scales("ln2")

        carve = Carve()
        feat = [carve(P) for _ in range(2)]
        featT = carve(P)
        route = carve(64)
        spread = carve(E * P)
        c2diag = carve(E * E)
        wT = carve(P)
        C8 = carve(P)
        with nc.Block() as block:
            f_steps, f_sum = sem("f_steps"), [sem("f_sum0"), sem("f_sum1")]
            r_pe, r_act, r_dve = sem("r_pe"), sem("r_act"), sem("r_dve")

            @block.vector
            def _(dve):
                link = Chain(dve, f_steps)
                for p in range(2):
                    dve.memset(feat[p], 0.0).then_inc(f_sum[p], 1)
                with dve.Fori(0, NT // 2) as i:
                    for p in range(2):
                        t = i * 2 + p
                        dve.wait_ge(f_sum[p], i + 1)
                        dve.scalar_tensor_tensor(feat[p], X[:, bass.ds(t * P, P)], RSTD[:, bass.ds(t, 1)], feat[p],
                                                 ALU.mult, ALU.add).then_inc(f_sum[p], 1)
                for p in range(2):
                    dve.wait_ge(f_sum[p], NT // 2 + 1)
                link(dve.tensor_tensor(S[1], MEAN[:, :], RSTD[:, :], ALU.mult))
                link(dve.tensor_reduce(S[2][:, 0:1], S[1], AX.X, ALU.add))
                link(dve.tensor_tensor(feat[0], feat[0], feat[1], ALU.add))
                link(dve.tensor_scalar(feat[0], feat[0], S[2][:, 0:1], 1.0 / NT, ALU.subtract, ALU.mult))
                dve.sem_inc(r_dve, 1)
                dve.wait_ge(r_pe, 2)
                logits, shifted, ex, w = (route[:, 8 * i:8 * i + 8] for i in range(4))
                link(dve.tensor_copy(logits, PS[1][:, 0:E]))
                link(dve.tensor_reduce(route[:, 40:41], logits, AX.X, ALU.max))
                link(dve.tensor_scalar(shifted, logits, route[:, 40:41], None, ALU.subtract))
                dve.sem_inc(r_dve, 1)
                dve.wait_ge(r_act, 2)
                link(dve.reciprocal(route[:, 42:43], route[:, 41:42]))
                link(dve.tensor_scalar(w, ex, route[:, 42:43], None, ALU.mult))
                link(dve.tensor_copy(spread.rearrange("p (e k) -> p e k", e=E), w.unsqueeze(2).to_broadcast([P, E, P])))
                link(dve.memset(c2diag, 0.0))
                link(dve.tensor_scalar(c2diag[:, 0:E * E:E + 1], nc2[:, :], -1.0, None, ALU.mult))
                dve.sem_inc(r_dve, 1)
                dve.wait_ge(r_pe, 5)
                for h in range(2):
                    link(dve.tensor_copy(WB[:, 4 * h:4 * h + 4, :].rearrange("p e k -> p (e k)"), PS[2 + h][:, :]))
                dve.wait_ge(r_pe, 6)
                link(dve.tensor_copy(CW[:, :], PS[6][:, 0:P]))
                link(dve.tensor_reduce(S[1][:, 0:1], FLG[:, :], AX.X, ALU.max))
                dve.sem_inc(r_dve, 1)
                dve.wait_ge(r_pe, 7)
                link(dve.tensor_reduce(S[2][0:1, 0:1], PS[7][0:1, 0:P], AX.X, ALU.max))
                link(dve.tensor_scalar(flag[0:1, 0:1], S[2][0:1, 0:1], 2.0, None, ALU.is_ge))

            @block.scalar
            def _(act):
                act.wait_ge(r_pe, 1)
                act.copy(featT, PS[0][:, 0:P]).then_inc(r_act, 1)
                act.wait_ge(r_dve, 2)
                act.activation(route[:, 16:24], route[:, 8:16], ACT.Exp, accum_out=route[:, 41:42]).then_inc(r_act, 1)
                act.wait_ge(r_pe, 3)
                act.copy(wT[0:E, :], PS[4][0:E, 0:P]).then_inc(r_act, 1)
                act.wait_ge(r_pe, 4)
                act.copy(C8[0:E, :], PS[5][0:E, 0:P]).then_inc(r_act, 1)

            @block.tensor
            def _(pe):
                pe.wait_ge(r_dve, 1)
                pe.transpose(PS[0][:, 0:P], feat[0], ident[:, :]).then_inc(r_pe, 1)
                pe.wait_ge(r_act, 1)
                pe.matmul(PS[1][:, 0:E], ones[0:1, :], brrow[:, :], start=True, stop=False)
                pe.matmul(PS[1][:, 0:E], featT, Wr[:, :], start=False, stop=True).then_inc(r_pe, 1)
                pe.wait_ge(r_dve, 3)
                pe.transpose(PS[4][0:E, 0:P], route[:, 24:32], ident[:, :]).then_inc(r_pe, 1)
                pe.matmul(PS[5][0:E, 0:P], ident[0:E, 0:E], bo[:, :], start=True, stop=False)
                for e in range(E):
                    last = pe.matmul(PS[5][0:E, 0:P], c2diag[:, e * E:(e + 1) * E], Wo[:, e, :], start=False, stop=(e == E - 1))
                last.then_inc(r_pe, 1)
                for e in range(E):
                    last = pe.matmul(PS[2 + e // 4][:, (e % 4) * P:(e % 4 + 1) * P], spread[:, e * P:(e + 1) * P], ident[:, :],
                                     start=True, stop=True)
                last.then_inc(r_pe, 1)
                pe.wait_ge(r_act, 4)
                pe.matmul(PS[6][:, 0:P], wT[0:E, :], C8[0:E, :], start=True, stop=True).then_inc(r_pe, 1)
                pe.wait_ge(r_dve, 4)
                pe.matmul(PS[7][0:1, 0:P], S[1][:, 0:1], ident[:, :], start=True, stop=True).then_inc(r_pe, 1)

        carve = Carve()
        xn4 = [carve(GW) for _ in range(2)]
        xT4 = [carve(GW) for _ in range(2)]
        h1 = [carve(GW) for _ in range(2)]
        h2 = [carve(GW) for _ in range(2)]
        with nc.Block() as block:
            xn_ready, xn_turned, xT_ready = sem("p2_xn_ready"), sem("p2_xn_turned"), sem("p2_xT_ready")
            h1_summed, h1_ready, h2_summed, h2_ready = sem("h1_summed"), sem("h1_ready"), sem("h2_summed"), sem("h2_ready")
            h2_used, y_summed = sem("h2_used"), sem("y_summed")
            cw_added, y_used, x2_ready = sem("cw_added"), sem("y_used"), sem("x2_ready")

            @block.gpsimd
            def _(pool):
                with pool.Fori(0, NG) as g:
                    pool.wait_ge(xn_ready, g * 4 + 4)
                    x = X[:, bass.ds(g * GW, GW)].rearrange("p (t d) -> p t d", d=P)
                    pool.tensor_tensor(x, x, CW[:, :].unsqueeze(1).to_broadcast([P, G4, P]), ALU.add).then_inc(cw_added, 1)

            @block.tensor
            def _(pe):
                def turn(g, p):
                    pe.wait_ge(xn_ready, g * 4 + 4)
                    wait(pe, xT_ready, g)
                    for j in range(G4):
                        last = pe.transpose(PS[0][:, j * P:(j + 1) * P], xn4[p][:, j * P:(j + 1) * P], ident[:, :])
                    last.then_inc(xn_turned, 1)

                def group(g, p, nxt):
                    def first(e):
                        if e == 0:
                            pe.wait_ge(xT_ready, g + 1)
                        wait(pe, h1_ready, g * E + e - 1)
                        pe.matmul(PS[1 + e % 2][:, :], W1[:, e, :], xT4[p], start=True, stop=True).then_inc(h1_summed, 1)

                    def second(e):
                        pe.wait_ge(h1_ready, g * E + e + 1)
                        wait(pe, h2_ready, g * E + e - 1)
                        pe.matmul(PS[3 + e % 2][:, :], W2[:, e, :], h1[e % 2], start=True, stop=True).then_inc(h2_summed, 1)

                    def third(e):
                        pe.wait_ge(h2_ready, g * E + e + 1)
                        if e == 0:
                            wait(pe, y_used, g)
                        for j in range(G4):
                            last = pe.matmul(PS[5 + p][:, j * P:(j + 1) * P], h2[e % 2][:, j * P:(j + 1) * P], Wo[:, e, :],
                                             start=(e == 0 and j == 0), stop=(e == E - 1), skip_group_check=True)
                        last.then_inc(h2_used, 1)

                    for e in range(E + 2):
                        if e < E:
                            first(e)
                        if e == 5 and nxt:
                            turn(*nxt)
                        if 1 <= e <= E:
                            second(e - 1)
                        if e >= 2:
                            third(e - 2)

                turn(0, 0)
                group(0, 0, (1, 1))
                with pe.Fori(0, NG // 2 - 1) as i:
                    group(i * 2 + 1, 1, (i * 2 + 2, 0))
                    group(i * 2 + 2, 0, (i * 2 + 3, 1))
                group(NG - 1, 1, None)

            @block.scalar
            def _(act):
                def copy_xT(g, p):
                    act.wait_ge(xn_turned, g + 1)
                    wait(act, h1_summed, (g - 1) * E)
                    act.copy(xT4[p], PS[0][:, :]).then_inc(xT_ready, 1)

                def group(g, p, nxt):
                    for e in range(E):
                        act.wait_ge(h1_summed, g * E + e + 1)
                        wait(act, h2_summed, g * E + e - 1)
                        act.activation(h1[e % 2], PS[1 + e % 2][:, :], ACT.Relu, bias=c1[:, e:e + 1],
                                       scale=sc1[:, e:e + 1]).then_inc(h1_ready, 1)
                        if e == 5 and nxt:
                            copy_xT(*nxt)

                copy_xT(0, 0)
                group(0, 0, (1, 1))
                with act.Fori(0, NG // 2 - 1) as i:
                    group(i * 2 + 1, 1, (i * 2 + 2, 0))
                    group(i * 2 + 2, 0, (i * 2 + 3, 1))
                group(NG - 1, 1, None)

            @block.vector
            def _(dve):
                def norms(g, p):
                    wait(dve, xn_turned, g - 1)
                    for j in range(G4):
                        normalise(dve, xn4[p][:, j * P:(j + 1) * P], g * G4 + j).then_inc(xn_ready, 1)

                def group(g, p, nxt):
                    for e in range(E):
                        dve.wait_ge(h2_summed, g * E + e + 1)
                        wait(dve, h2_used, g * E + e - 1)
                        dve.scalar_tensor_tensor(h2[e % 2].rearrange("p (t n) -> p t n", n=P),
                                                 PS[3 + e % 2][:, :].rearrange("p (t n) -> p t n", n=P),
                                                 nc2[:, e:e + 1], WB[:, e:e + 1, :].to_broadcast([P, G4, P]),
                                                 ALU.max, ALU.mult).then_inc(h2_ready, 1)
                        if e == 2 and nxt:
                            norms(*nxt)

                def finish(g, p):
                    dve.wait_ge(h2_used, g * E + E)
                    dve.wait_ge(cw_added, g + 1)
                    x = X[:, bass.ds(g * GW, GW)]
                    dve.tensor_tensor(x, PS[5 + p][:, :], x, ALU.add).then_inc(y_used, 1)
                    dve.wait_ge(y_used, g + 2)
                    for j in range(G4):
                        tile_stats(dve, g * G4 + j).then_inc(x2_ready, 1)

                dve.sem_inc(y_used, 1)
                norms(0, 0)
                group(0, 0, (1, 1))
                finish(0, 0)
                with dve.Fori(0, NG // 2 - 1) as i:
                    group(i * 2 + 1, 1, (i * 2 + 2, 0))
                    finish(i * 2 + 1, 1)
                    group(i * 2 + 2, 0, (i * 2 + 3, 1))
                    finish(i * 2 + 2, 0)
                group(NG - 1, 1, None)
                finish(NG - 1, 1)

        layer_norm_scales("ln3")

        carve = Carve()
        g_adj = carve(P).bitcast(I32)
        g_adjf, g_adjT, g_xn, g_xT = carve(P), carve(P), carve(P), carve(P)
        g_hg = carve(4 * P)
        g_rel = carve(1)
        g_sel, g_mf, g_mb = carve(P), carve(P), carve(P)
        g_sig, g_val = carve(2 * P), carve(2 * P)
        with nc.Block() as block:
            ga_loaded, ga_free, g_in = sem("ga_loaded"), sem("ga_free"), sem("g_in")
            g_turned, g_copied, g_proj, g_hgready = sem("g_turned"), sem("g_copied"), sem("g_proj"), sem("g_hgready")
            g_rset, g_mask, g_vsum, g_sigready, g_valready, g_acc, g_added = (
                sem("g_rset"), sem("g_mask"), sem("g_vsum"), sem("g_sigready"), sem("g_valready"), sem("g_acc"), sem("g_added"))

            def if_relations(eng):
                return eng.If(eng.value_load(flag[0:1, 0:1]) > 0)

            @block.sync
            def _(sp):
                with if_relations(sp):
                    with sp.Fori(0, NT) as t:
                        sp.wait_ge(ga_free, t + 1)
                        sp.dma_start(g_adj, a["adj"][bass.ds(t, 1)].rearrange("o p j -> (o p) j")).then_inc(ga_loaded, 16)

            @block.vector
            def _(dve):
                with if_relations(dve):
                    dve.sem_inc(ga_free, 1)
                    with dve.Fori(0, NT) as t:
                        dve.wait_ge(ga_loaded, t * 16 + 16)
                        dve.tensor_copy(g_adjf, g_adj).then_inc(ga_free, 1)
                        dve.memset(g_rel, 1.0).then_inc(g_rset, 1)
                        normalise(dve, g_xn, t).then_inc(g_in, 1)
                        with dve.Fori(0, NREL) as r:
                            n = t * NREL + r
                            dve.wait_ge(g_hgready, t + 1)
                            dve.wait_ge(ga_free, t + 2)
                            dve.wait_ge(g_rset, t * (NREL + 1) + r + 1)
                            dve.tensor_scalar(g_rel, g_rel, 1.0, None, ALU.add).then_inc(g_rset, 1)
                            dve.wait_ge(g_rset, t * (NREL + 1) + r + 2)
                            dve.tensor_scalar(g_sel, pidx[:, :], 2.0, g_rel, ALU.add, ALU.is_equal).then_inc(g_mask, 1)
                            dve.tensor_scalar(g_mf, g_adjT, g_rel, None, ALU.is_equal).then_inc(g_mask, 1)
                            dve.tensor_scalar(g_mb, g_adjf, g_rel, None, ALU.is_equal).then_inc(g_mask, 1)
                            dve.wait_ge(g_sigready, n * 2 + 2)
                            for h in range(2):
                                dve.tensor_tensor(g_val[:, h * P:(h + 1) * P], PS[2][:, 2 * h * P:(2 * h + 1) * P],
                                                  g_sig[:, h * P:(h + 1) * P], ALU.mult).then_inc(g_valready, 1)
                            dve.wait_ge(g_acc, n + 1)
                            ex = EX[:, bass.ds(t * P, P)]
                            dve.tensor_tensor(ex, PS[3][:, 0:P], ex, ALU.add).then_inc(g_added, 1)
                            dve.wait_ge(g_added, n + 1)

            @block.scalar
            def _(act):
                with if_relations(act):
                    with act.Fori(0, NT) as t:
                        act.wait_ge(g_turned, t + 1)
                        act.copy(g_adjT, PS[0][:, 0:P]).then_inc(g_copied, 1)
                        act.copy(g_xT, PS[0][:, P:2 * P]).then_inc(g_copied, 1)
                        act.wait_ge(g_proj, t + 1)
                        act.wait_ge(g_copied, t * 2 + 2)
                        act.copy(g_hg, PS[1][:, :]).then_inc(g_hgready, 1)
                        with act.Fori(0, NREL) as r:
                            act.wait_ge(g_vsum, t * NREL + r + 1)
                            for h in range(2):
                                act.activation(g_sig[:, h * P:(h + 1) * P], PS[2][:, (2 * h + 1) * P:(2 * h + 2) * P],
                                               ACT.Sigmoid).then_inc(g_sigready, 1)

            @block.tensor
            def _(pe):
                with if_relations(pe):
                    with pe.Fori(0, NT) as t:
                        pe.wait_ge(g_in, t + 1)
                        pe.wait_ge(ga_free, t + 2)
                        pe.transpose(PS[0][:, 0:P], g_adjf, ident[:, :])
                        pe.transpose(PS[0][:, P:2 * P], g_xn, ident[:, :]).then_inc(g_turned, 1)
                        pe.wait_ge(g_copied, t * 2 + 2)
                        pe.matmul(PS[1][:, :], g_xT, WHG[:, 0:2, :, :].rearrange("p i s d -> p (i s d)"),
                                  start=True, stop=True).then_inc(g_proj, 1)
                        with pe.Fori(0, NREL) as r:
                            n = t * NREL + r
                            pe.wait_ge(g_hgready, t + 1)
                            pe.wait_ge(g_mask, n * 3 + 3)
                            pe.matmul(PS[2][:, :], ident[:, :], g_hg, start=True, stop=False)
                            pe.matmul(PS[2][:, :], g_sel, B4[:, :], start=False, stop=True).then_inc(g_vsum, 1)
                            pe.wait_ge(g_valready, n * 2 + 2)
                            pe.matmul(PS[3][:, 0:P], g_mf, g_val[:, 0:P], start=True, stop=False)
                            pe.matmul(PS[3][:, 0:P], g_mb, g_val[:, P:2 * P], start=False, stop=True).then_inc(g_acc, 1)

        carve = Carve()
        xn = [carve(P) for _ in range(2)]
        xT = [carve(P) for _ in range(2)]
        m1f = [carve(P) for _ in range(2)]
        sig = [carve(P) for _ in range(2)]
        val = [carve(P) for _ in range(2)]
        tmp = [carve(P) for _ in range(2)]
        with nc.Block() as block:
            xn_ready, xn_turned, xT_ready = sem("p3_xn_ready"), sem("p3_xn_turned"), sem("p3_xT_ready")
            hg_summed, sig_ready, val_ready = sem("hg_summed"), sem("sig_ready"), sem("val_ready")
            m1_ready, agg_summed, agg_used, relu_done, x3_ready = (
                sem("m1_ready"), sem("agg_summed"), sem("agg_used"), sem("relu_done"), sem("x3_ready"))

            @block.gpsimd
            def _(pool):
                def tile(t, p):
                    wait(pool, agg_summed, t - 1)
                    pool.tensor_copy(m1f[p], M1[:, bass.ds(t * P, P)]).then_inc(m1_ready, 1)

                tile(0, 0)
                tile(1, 1)
                with pool.Fori(1, NT // 2) as i:
                    for p in range(2):
                        tile(i * 2 + p, p)

            @block.tensor
            def _(pe):
                def turn(t, p):
                    pe.wait_ge(xn_ready, t + 1)
                    wait(pe, xT_ready, t - 1)
                    pe.transpose(PS[p][:, 0:P], xn[p], ident[:, :]).then_inc(xn_turned, 1)

                def project(t, p):
                    pe.wait_ge(xT_ready, t + 1)
                    wait(pe, val_ready, t - 1)
                    pe.matmul(PS[2 + p][:, 0:2 * P], ones[0:1, :], b1row[:, :], start=True, stop=False)
                    pe.matmul(PS[2 + p][:, 0:2 * P], xT[p], WHG[:, 2, :, :].rearrange("p s d -> p (s d)"),
                              start=False, stop=True).then_inc(hg_summed, 1)

                def gather(t, p):
                    pe.wait_ge(val_ready, t + 1)
                    pe.wait_ge(m1_ready, t + 1)
                    wait(pe, agg_used, t - 1)
                    pe.matmul(PS[4 + p][:, 0:P], m1f[p], val[p], start=True, stop=True).then_inc(agg_summed, 1)

                turn(0, 0)
                project(0, 0)
                turn(1, 1)
                project(1, 1)
                gather(0, 0)
                with pe.Fori(1, NT // 2) as i:
                    for p in range(2):
                        t = i * 2 + p
                        turn(t, p)
                        project(t, p)
                        gather(t - 1, 1 - p)
                gather(NT - 1, 1)

            @block.scalar
            def _(act):
                def tile(t, p):
                    act.wait_ge(xn_turned, t + 1)
                    wait(act, hg_summed, t - 1)
                    act.copy(xT[p], PS[p][:, 0:P]).then_inc(xT_ready, 1)
                    act.wait_ge(hg_summed, t + 1)
                    wait(act, val_ready, t - 1)
                    act.activation(sig[p], PS[2 + p][:, P:2 * P], ACT.Sigmoid).then_inc(sig_ready, 1)

                tile(0, 0)
                tile(1, 1)
                with act.Fori(1, NT // 2) as i:
                    for p in range(2):
                        tile(i * 2 + p, p)

            @block.vector
            def _(dve):
                def front(t, p):
                    wait(dve, xn_turned, t - 1)
                    normalise(dve, xn[p], t).then_inc(xn_ready, 1)

                def middle(t, p):
                    dve.wait_ge(sig_ready, t + 1)
                    wait(dve, agg_summed, t - 1)
                    dve.tensor_tensor(val[p], PS[2 + p][:, 0:P], sig[p], ALU.mult).then_inc(val_ready, 1)

                def back(t, p):
                    x = X[:, bass.ds(t * P, P)]
                    dve.wait_ge(agg_summed, t + 1)
                    dve.tensor_tensor(tmp[p], PS[4 + p][:, 0:P], EX[:, bass.ds(t * P, P)], ALU.add).then_inc(agg_used, 1)
                    dve.wait_ge(agg_used, t + 1)
                    dve.scalar_tensor_tensor(x, tmp[p], 0.0, x, ALU.max, ALU.add).then_inc(relu_done, 1)
                    dve.wait_ge(relu_done, t + 1)
                    tile_stats(dve, t).then_inc(x3_ready, 1)

                front(0, 0)
                front(1, 1)
                middle(0, 0)
                middle(1, 1)
                back(0, 0)
                with dve.Fori(1, NT // 2) as i:
                    for p in range(2):
                        t = i * 2 + p
                        front(t, p)
                        middle(t, p)
                        back(t - 1, 1 - p)
                back(NT - 1, 1)

        layer_norm_scales("ln4")

        carve = Carve()
        xn4 = carve(GW)
        xT4 = carve(GW)
        Z = [carve(GW) for _ in range(NC)]
        sel = [carve(P) for _ in range(2)]
        dcount = carve(1)
        ring = [carve(GW) for _ in range(RING)]
        gelu, gate = carve(GW), carve(GW)
        cv, cc, tr = carve(GW), carve(GW), carve(GW)
        F = [carve(GW) for _ in range(2)]
        outs = carve(GW)
        BCLS, BGATE, BOUT = PS[5], PS[6], PS[7]
        lines_ready, chunk_in, pwl_done = sem("lines_ready"), sem("chunk_in"), sem("pwl_done")
        chunk_summed, out_summed, out_made, out_stored = sem("chunk_summed"), sem("out_summed"), sem("out_made"), sem("out_stored")

        def consumer(i):
            return max(i - 1, 0) if i < NL else max(i - 2, NL - 1)

        def act_chunk(act, m, c):
            act.wait_ge(chunk_summed, m + 1)
            wait(act, pwl_done, m * PWL_OPS)
            act.activation(gelu, BCLS[:, :], ACT.Gelu, bias=PT[:, bc_at + c:bc_at + c + 1]).then_inc(chunk_in, 1)
            act.activation(gate, BGATE[:, :], ACT.Tanh, bias=bgh[:, c:c + 1], scale=0.5).then_inc(chunk_in, 1)
            for i in range(2 * NL):
                if i >= RING:
                    wait(act, pwl_done, m * PWL_OPS + consumer(i - RING) + 1)
                act.activation(ring[i % RING], Z[c], ACT.Identity, bias=OF[:, c, i:i + 1],
                               scale=SL[:, c, i:i + 1]).then_inc(lines_ready, 1)

        def dve_chunk(dve, m, c):
            n = [0]

            def step(ins):
                ins.then_inc(pwl_done, 1)
                n[0] += 1

            def after(k):
                dve.wait_ge(pwl_done, m * PWL_OPS + k)

            for i in range(2 * NL):
                if i in (0, NL):
                    continue
                acc, op = (cv, ALU.max) if i < NL else (cc, ALU.min)
                dve.wait_ge(lines_ready, m * 2 * NL + i + 1)
                if i in (1, NL + 1):
                    step(dve.tensor_tensor(acc, ring[(i - 1) % RING], ring[i % RING], op))
                else:
                    after(n[0])
                    step(dve.tensor_tensor(acc, acc, ring[i % RING], op))
            after(n[0])
            step(dve.tensor_tensor(tr, cv, cc, ALU.add))
            dve.wait_ge(chunk_in, m * 2 + 2)
            after(n[0])
            step(dve.tensor_tensor(tr, tr, gelu, ALU.subtract))
            after(n[0])
            step(dve.scalar_tensor_tensor(tr, gate, 1.0, tr, ALU.add, ALU.mult))
            after(n[0])
            wait(dve, out_summed, m - 1)
            step(dve.scalar_tensor_tensor(F[c % 2], tr, 0.5, gelu, ALU.mult, ALU.add))
            assert n[0] == PWL_OPS

        def pe_chunk(pe, m, c):
            wait(pe, chunk_in, m * 2)
            cols = slice(c * P, (c + 1) * P)
            pe.matmul(BCLS[:, :], Wc[:, cols], xT4, start=True, stop=True)
            pe.matmul(BGATE[:, :], Wg[:, cols], xT4, start=True, stop=True).then_inc(chunk_summed, 1)

        def pe_out(pe, m, c, g):
            pe.wait_ge(pwl_done, m * PWL_OPS + PWL_OPS)
            if c == 0:
                wait(pe, out_made, g)
                pe.matmul(BOUT[:, :], ones[0:1, :], bdrow[:, :], start=True, stop=False, skip_group_check=True)
            for j in range(G4):
                last = pe.matmul(BOUT[:, j * P:(j + 1) * P], F[c % 2][:, j * P:(j + 1) * P], Wd[:, c, :],
                                 start=False, stop=(c == NC - 1), skip_group_check=True)
            last.then_inc(out_summed, 1)

        with nc.Block() as block:
            d_xn, d_turned, d_xT = sem("d_xn"), sem("d_turned"), sem("d_xT")
            z_set, d_sel, d_row, d_max = sem("z_set"), sem("d_sel"), sem("d_row"), sem("d_max")
            d_cnt = sem("d_cnt")

            @block.sync
            def _(sp):
                with sp.Fori(0, NG) as g:
                    sp.wait_ge(out_made, g + 1)
                    sp.dma_start(out[bass.ds(g * G4, G4)].rearrange("t p d -> p t d"),
                                 outs.rearrange("p (t d) -> p t d", d=P)).then_inc(out_stored, 16)
                sp.wait_ge(out_stored, NG * 16)

            @block.tensor
            def _(pe):
                def group(g):
                    pe.wait_ge(d_xn, g * 4 + 4)
                    for j in range(G4):
                        last = pe.transpose(PS[0][:, j * P:(j + 1) * P], xn4[:, j * P:(j + 1) * P], ident[:, :])
                    last.then_inc(d_turned, 1)
                    with pe.Fori(0, P // 2) as d:
                        for p in range(2):
                            n = g * P + d * 2 + p
                            pe.wait_ge(d_xT, g + 1)
                            pe.wait_ge(d_sel, n + 1)
                            pe.matmul(PS[1 + p][:, :], sel[p], xT4, start=True, stop=True).then_inc(d_row, 1)
                    for c in range(NC):
                        m = g * NC + c
                        pe_chunk(pe, m, c)
                        if c:
                            pe_out(pe, m - 1, c - 1, g)
                    pe_out(pe, g * NC + NC - 1, NC - 1, g)

                group(0)
                with pe.Fori(1, NG) as g:
                    group(g)

            @block.scalar
            def _(act):
                def group(g):
                    act.wait_ge(d_turned, g + 1)
                    act.copy(xT4, PS[0][:, :]).then_inc(d_xT, 1)
                    act.wait_ge(d_max, (g * P + P) * NC + NC)
                    for c in range(NC):
                        act_chunk(act, g * NC + c, c)

                group(0)
                with act.Fori(1, NG) as g:
                    group(g)

            @block.vector
            def _(dve):
                def group(g):
                    for j in range(G4):
                        normalise(dve, xn4[:, j * P:(j + 1) * P], g * G4 + j).then_inc(d_xn, 1)
                    dve.memset(dcount, -1.0).then_inc(z_set, 1)
                    for c in range(NC):
                        dve.memset(Z[c], LOWEST).then_inc(z_set, 1)
                    def select(n, p):
                        dve.tensor_scalar(dcount, dcount, 1.0, None, ALU.add).then_inc(d_cnt, 1)
                        dve.wait_ge(d_cnt, n + 1)
                        dve.tensor_scalar(sel[p], pidx[:, :], dcount, None, ALU.is_equal).then_inc(d_sel, 1)

                    with dve.Fori(0, P // 2) as d:
                        for p in range(2):
                            n = g * P + d * 2 + p
                            dve.wait_ge(z_set, g * (NC + 1) + NC + 1)
                            select(n, p)
                        for p in range(2):
                            n = g * P + d * 2 + p
                            dve.wait_ge(d_row, n + 1)
                            for c in range(NC):
                                dve.wait_ge(d_max, n * NC + c + 1)
                                dve.scalar_tensor_tensor(Z[c], PS[1 + p][:, :], WtS[:, c, bass.ds(d * 2 + p, 1)], Z[c],
                                                         ALU.add, ALU.max).then_inc(d_max, 1)
                    for c in range(NC):
                        dve_chunk(dve, g * NC + c, c)
                    dve.wait_ge(out_summed, g * NC + NC)
                    wait(dve, out_stored, g * 16)
                    dve.tensor_tensor(outs, BOUT[:, :], X[:, bass.ds(g * GW, GW)], ALU.add).then_inc(out_made, 1)

                dve.sem_inc(d_max, NC)
                group(0)
                with dve.Fori(1, NG) as g:
                    group(g)


_INS = ['x', 'adj', 'L0_gnn_W_msg', 'L0_gnn_W_upd', 'L0_gnn_bias', 'L0_ffn_Wr', 'L0_ffn_br', 'L0_ffn_W1', 'L0_ffn_b1',
        'L0_ffn_g1', 'L0_ffn_be1', 'L0_ffn_m1', 'L0_ffn_v1', 'L0_ffn_W2', 'L0_ffn_b2', 'L0_ffn_g2', 'L0_ffn_be2',
        'L0_ffn_m2', 'L0_ffn_v2', 'L0_ffn_Wo', 'L0_ffn_bo', 'L1_gnn_W_fwd', 'L1_gnn_W_bwd', 'L1_gnn_W_loop',
        'L1_gnn_Wg_fwd', 'L1_gnn_Wg_bwd', 'L1_gnn_Wg_loop', 'L1_gnn_b_fwd', 'L1_gnn_b_bwd', 'L1_gnn_b_loop',
        'L1_gnn_bg_fwd', 'L1_gnn_bg_bwd', 'L1_gnn_bg_loop', 'L1_ffn_Wt', 'L1_ffn_bt', 'L1_ffn_sl_cvx', 'L1_ffn_of_cvx',
        'L1_ffn_sl_ccv', 'L1_ffn_of_ccv', 'L1_ffn_alpha', 'L1_ffn_Wc', 'L1_ffn_bc', 'L1_ffn_Wg', 'L1_ffn_bg',
        'L1_ffn_Wd', 'L1_ffn_bd']


def kernel(**inputs):
    import numpy as _np
    import concourse.bacc as _bacc
    from concourse import mybir as _mybir
    from concourse.bass_utils import run_bass_kernel_spmd as _run

    nc = _bacc.Bacc("TRN2", target_bir_lowering=False, num_devices=1)
    arrays, args = {}, {}
    for name in _INS:
        arr = _np.ascontiguousarray(inputs[name])
        arrays[f"in_{name}_dram"] = arr
        args[name] = nc.dram_tensor(f"in_{name}_dram", arr.shape, _mybir.dt.from_np(arr.dtype), kind="ExternalInput").ap()
    out = nc.dram_tensor("out_0_dram", (NT, P, P), _mybir.dt.float32, kind="ExternalOutput").ap()
    build(nc, args, out)
    r = _run(nc, [arrays], core_ids=[0])
    return r.results[0]["out_0_dram"]
```

```python
from contextlib import ExitStack

import concourse.bass as bass
from concourse import mybir

ALU = mybir.AluOpType
ACT = mybir.ActivationFunctionType
AX = mybir.AxisListType
F32 = mybir.dt.float32
BF16 = mybir.dt.bfloat16
I32 = mybir.dt.int32
U32 = mybir.dt.uint32

P = 128
NT = 64
E = 8
NC = 4
NH = NC * P
G4 = 4
NG = NT // G4
GW = G4 * P
NL = 8
NREL = 39
LN_EPS = 1e-5
BN_EPS = 1e-3
LOWEST = -3.0e38
R1 = 8
R2 = 16
USES = G4 * R1 + R2 + G4
FILLS = 4 + NC
ROUNDS = G4 + R2 // 8
YW = P + 2
FAR = -1.0e30
PAIRS = NL
STEPS = 18


def wait(eng, sem, value):
    if not (isinstance(value, int) and value <= 0):
        eng.wait_ge(sem, value)


def build(nc, a, out):
    with ExitStack() as ctx:
        def sb(name, shape, dt=F32):
            return ctx.enter_context(nc.sbuf_tensor(name, shape, dt))

        def sem(name):
            return ctx.enter_context(nc.semaphore(name))

        X = sb("X", [P, NT * P])
        M1 = sb("M1", [P, NT * P], BF16)
        EX = sb("EX", [P, NT * P])
        STATS = sb("STATS", [P, NT, 6])
        MEAN = sb("MEAN", [P, NT])
        RSTD = sb("RSTD", [P, NT])
        FLG = sb("FLG", [P, NT])
        ident = sb("ident", [P, P])
        ones = sb("ones", [P, P])
        pidx = sb("pidx", [P, P])
        PAR = sb("PAR", [96, P])
        PT = sb("PT", [P, 96])
        WMU = sb("WMU", [P, 2 * P])
        b0row = sb("b0row", [1, 2 * P])
        Wr = sb("Wr", [P, E])
        brrow = sb("brrow", [1, E])
        W1 = sb("W1", [P, E, P])
        W2 = sb("W2", [P, E, P])
        Wo = sb("Wo", [P, E, P])
        bo = sb("bo", [E, P])
        WG = sb("WG", [P, 6, P])
        WHG = sb("WHG", [P, 3, 2, P])
        b1row = sb("b1row", [1, 2 * P])
        B4 = sb("B4", [P, 4 * P])
        WtS = sb("WtS", [P, NC, P])
        SL = sb("SL", [P, NC, 2 * NL])
        OF = sb("OF", [P, NC, 2 * NL])
        Wc = sb("Wc", [P, NH])
        Wg = sb("Wg", [P, NH])
        Wd = sb("Wd", [P, NC, P])
        bdrow = sb("bdrow", [1, G4 * P])
        sc1 = sb("sc1", [P, E])
        c1 = sb("c1", [P, E])
        nc2 = sb("nc2", [P, E])
        bgh = sb("bgh", [P, NC])
        OFA = sb("OFA", [P, NC, PAIRS])
        OFM = sb("OFM", [P, NC, PAIRS - 1])
        OFK = sb("OFK", [P, NC])
        NMR = sb("NMR", [P, NT])
        WP = sb("WP", [P, 3, NH], BF16)
        mwrow = sb("mwrow", [P, P])
        coli = sb("coli", [P, P])
        colb = sb("colb", [P, P], BF16)
        identb = sb("identb", [P, P], BF16)
        onesb = sb("onesb", [P, P], BF16)
        tri = sb("tri", [P, P], BF16)
        PMALL = sb("PMALL", [P, NT])
        OPEN = sb("OPEN", [P, NG])
        flag2 = sb("flag2", [1, 2], I32)
        WB = sb("WB", [P, E, P])
        CW = sb("CW", [P, P])
        small = sb("small", [P, 16, NT])
        flag = sb("flag", [1, 2], I32)
        WORK = 13312
        work = sb("work", [P, WORK])

        PS = [ctx.enter_context(nc.psum_tensor(f"ps{i}", [P, 512], F32)) for i in range(8)]

        class Carve:
            def __init__(self):
                self.at = 0

            def __call__(self, n):
                v = work[:, self.at:self.at + n]
                self.at += n
                assert self.at <= WORK
                return v

        bt_at, al_at, bc_at, bg_at = 80, 84, 88, 92

        params_loaded, weights_loaded, x_loaded = sem("params_loaded"), sem("weights_loaded"), sem("x_loaded")
        pool_made, pe_setup, act_setup, dve_setup = sem("pool_made"), sem("pe_setup"), sem("act_setup"), sem("dve_setup")
        carve = Carve()
        bc_scale = carve(E * P)
        WgT = carve(3 * P)
        wtT, wres = carve(NH), carve(NH)
        mw_spread = carve(P)
        names = ["b1", "g1", "be1", "m1", "v1", "b2", "g2", "be2", "m2", "v2"]
        loads = [(WMU[:, 0:P], a["L0_gnn_W_msg"]), (WMU[:, P:2 * P], a["L0_gnn_W_upd"]),
                 (b0row[0:1, P:2 * P], a["L0_gnn_bias"].rearrange("(o d) -> o d", o=1)),
                 (Wr[:, :], a["L0_ffn_Wr"]), (brrow[:, :], a["L0_ffn_br"].rearrange("(o d) -> o d", o=1)),
                 (W1[:, :, :], a["L0_ffn_W1"].rearrange("e d h -> d e h")),
                 (W2[:, :, :], a["L0_ffn_W2"].rearrange("e d h -> d e h")),
                 (Wo[:, :, :], a["L0_ffn_Wo"].rearrange("e d h -> d e h")),
                 (bo[:, :], a["L0_ffn_bo"]),
                 (WG[:, 0, :], a["L1_gnn_W_fwd"]), (WG[:, 1, :], a["L1_gnn_W_bwd"]), (WG[:, 2, :], a["L1_gnn_W_loop"]),
                 (WG[:, 3, :], a["L1_gnn_Wg_fwd"]), (WG[:, 4, :], a["L1_gnn_Wg_bwd"]), (WG[:, 5, :], a["L1_gnn_Wg_loop"]),
                 (b1row[:, 0:P], a["L1_gnn_b_loop"]), (b1row[:, P:2 * P], a["L1_gnn_bg_loop"]),
                 (WtS[:, :, :], a["L1_ffn_Wt"].rearrange("(c f) d -> f c d", c=NC)),
                 (SL[:, :, 0:NL], a["L1_ffn_sl_cvx"].rearrange("(c f) l -> f c l", c=NC)),
                 (SL[:, :, NL:2 * NL], a["L1_ffn_sl_ccv"].rearrange("(c f) l -> f c l", c=NC)),
                 (OF[:, :, 0:NL], a["L1_ffn_of_cvx"].rearrange("(c f) l -> f c l", c=NC)),
                 (OF[:, :, NL:2 * NL], a["L1_ffn_of_ccv"].rearrange("(c f) l -> f c l", c=NC)),
                 (Wc[:, :], a["L1_ffn_Wc"]), (Wg[:, :], a["L1_ffn_Wg"]),
                 (Wd[:, :, :], a["L1_ffn_Wd"].rearrange("(c f) d -> f c d", c=NC))]
        loads += [(bdrow[:, j * P:(j + 1) * P], a["L1_ffn_bd"].rearrange("(o d) -> o d", o=1)) for j in range(G4)]
        relation_rows = ["L1_gnn_b_fwd", "L1_gnn_bg_fwd", "L1_gnn_b_bwd", "L1_gnn_bg_bwd"]

        class Chain:
            def __init__(self, eng, sem, base=0):
                self.eng, self.sem, self.n = eng, sem, base

            def __call__(self, ins):
                ins.then_inc(self.sem, 1)
                self.n += 1
                self.eng.wait_ge(self.sem, self.n)

        def rsqrt_after_sqrt(link, dve, v, root, r, t):
            link(dve.reciprocal(r, root))
            link(dve.tensor_tensor(t, r, r, ALU.mult))
            link(dve.tensor_tensor(t, t, v, ALU.mult))
            link(dve.tensor_scalar(t, t, -0.5, 1.5, ALU.mult, ALU.add))
            link(dve.tensor_tensor(r, r, t, ALU.mult))

        S = [small[:, i, :] for i in range(16)]

        def variance(link, dve):
            ev, od = STATS[:, :, 1], STATS[:, :, 4]
            link(dve.tensor_tensor(S[1], ev, od, ALU.add))
            link(dve.tensor_scalar(MEAN[:, :], S[1], 0.5, None, ALU.mult))
            link(dve.tensor_tensor(S[1], ev, od, ALU.subtract))
            link(dve.tensor_tensor(S[1], S[1], S[1], ALU.mult))
            link(dve.tensor_tensor(S[2], STATS[:, :, 2], STATS[:, :, 5], ALU.add))
            link(dve.tensor_scalar(S[2], S[2], 1.0 / P, LN_EPS, ALU.mult, ALU.add))
            link(dve.scalar_tensor_tensor(S[0], S[1], 0.25, S[2], ALU.mult, ALU.add))

        def layer_norm_scales(name):
            steps, rooted = sem(name + "_dve"), sem(name + "_root")
            with nc.Block() as block:
                @block.vector
                def _(dve):
                    link = Chain(dve, steps)
                    variance(link, dve)
                    dve.wait_ge(rooted, 1)
                    rsqrt_after_sqrt(link, dve, S[0], S[3], RSTD[:, :], S[1])
                    link(dve.scalar_tensor_tensor(NMR[:, :], MEAN[:, :], -1.0, RSTD[:, :], ALU.mult, ALU.mult))

                @block.scalar
                def _(act):
                    act.wait_ge(steps, 7)
                    act.activation(S[3], S[0], ACT.Sqrt).then_inc(rooted, 1)

        with nc.Block() as block:
            @block.sync
            def _(sp):
                for i, n in enumerate(names):
                    sp.dma_start(PAR[8 * i:8 * i + 8, :], a["L0_ffn_" + n]).then_inc(params_loaded, 16)
                for at, n in ((bt_at, "bt"), (al_at, "alpha"), (bc_at, "bc"), (bg_at, "bg")):
                    sp.dma_start(PAR[at:at + NC, :], a["L1_ffn_" + n].rearrange("(c f) -> c f", c=NC)).then_inc(params_loaded, 16)
                for dst, src in loads:
                    sp.dma_start(dst, src).then_inc(weights_loaded, 16)
                sp.wait_ge(pool_made, 5)
                for i, n in enumerate(relation_rows):
                    sp.dma_start(B4[0:NREL, i * P:(i + 1) * P], a[n]).then_inc(weights_loaded, 16)

            N_WEIGHTS = 16 * (len(loads) + len(relation_rows))

            @block.scalar
            def _(act):
                for i in range(4):
                    n = NT // 4
                    act.dma_start(X[:, i * n * P:(i + 1) * n * P].rearrange("p (t d) -> p t d", d=P),
                                  a["x"][i * n:(i + 1) * n].rearrange("t p d -> p t d")).then_inc(x_loaded, 16)
                act.wait_ge(pe_setup, 1)
                act.copy(PT[:, :], PS[0][:, 0:96]).then_inc(act_setup, 1)
                act.wait_ge(dve_setup, 2)
                act.activation(S[3][:, 0:16], S[0][:, 0:16], ACT.Sqrt).then_inc(act_setup, 1)
                act.activation(S[4][:, 0:NC], PT[:, al_at:al_at + NC], ACT.Sigmoid).then_inc(act_setup, 1)
                act.wait_ge(pe_setup, 3)
                act.copy(WHG[:, :, 0, :], PS[2][:, 0:3 * P].rearrange("p (i d) -> p i d", i=3)).then_inc(act_setup, 1)
                act.copy(WgT, PS[3][:, 0:3 * P]).then_inc(act_setup, 1)
                act.wait_ge(pe_setup, 4)
                act.copy(WHG[:, :, 1, :], PS[4][:, 0:3 * P].rearrange("p (i d) -> p i d", i=3)).then_inc(act_setup, 1)

            @block.gpsimd
            def _(pool):
                pool.memset(ones[:, :], 1.0).then_inc(pool_made, 1)
                pool.memset(ident[:, :], 0.0).then_inc(pool_made, 1)
                pool.wait_ge(pool_made, 2)
                pool.affine_select(out=ident[:, :], in_=ident[:, :], compare_op=ALU.not_equal, fill=1.0, base=0,
                                   pattern=[[-1, P]], channel_multiplier=1).then_inc(pool_made, 1)
                pool.iota(pidx[:, :], [[0, P]], base=0, channel_multiplier=1,
                          allow_small_or_imprecise_dtypes=True).then_inc(pool_made, 1)
                pool.memset(B4[:, :], 0.0).then_inc(pool_made, 1)
                pool.memset(b0row[:, 0:P], 0.0).then_inc(pool_made, 1)
                pool.iota(coli[:, :], [[1, P]], base=1, channel_multiplier=0,
                          allow_small_or_imprecise_dtypes=True).then_inc(pool_made, 1)
                pool.memset(EX[:, :], 0.0).then_inc(pool_made, 1)

            @block.tensor
            def _(pe):
                pe.wait_ge(pool_made, 4)
                pe.wait_ge(params_loaded, 16 * 14)
                pe.transpose(PS[0][:, 0:96], PAR[:, :], ident[0:96, 0:96]).then_inc(pe_setup, 1)
                pe.wait_ge(weights_loaded, N_WEIGHTS)
                for i in range(6):
                    bank = PS[2 + i // 3]
                    last = pe.transpose(bank[:, (i % 3) * P:(i % 3 + 1) * P], WG[:, i, :], ident[:, :])
                    if i % 3 == 2:
                        last.then_inc(pe_setup, 1)
                pe.wait_ge(act_setup, 5)
                for i in range(3):
                    last = pe.matmul(PS[4][:, i * P:(i + 1) * P], WG[:, i, :], WgT[:, i * P:(i + 1) * P],
                                     start=True, stop=True)
                last.then_inc(pe_setup, 1)
                for c in range(NC):
                    last = pe.transpose(PS[1][:, c * P:(c + 1) * P], WtS[:, c, :], ident[:, :])
                last.then_inc(pe_setup, 1)
                pe.wait_ge(dve_setup, 3)
                for e in range(E):
                    last = pe.matmul(PS[5 + e // 4][:, (e % 4) * P:(e % 4 + 1) * P],
                                     bc_scale[:, e * P:(e + 1) * P], ident[:, :], start=True, stop=True)
                last.then_inc(pe_setup, 1)
                pe.wait_ge(dve_setup, 4)
                pe.matmul(PS[7][:, 0:P], mw_spread, ident[:, :], start=True, stop=True).then_inc(pe_setup, 1)

            dve_chain, x_stats = sem("dve_chain"), sem("x_stats")

            @block.vector
            def _(dve):
                link = Chain(dve, dve_chain)

                def col(name, n=E):
                    at = 8 * names.index(name)
                    return PT[:, at:at + n]

                dve.wait_ge(act_setup, 1)
                dve.tensor_scalar(S[0][:, 0:8], col("v1"), BN_EPS, None, ALU.add).then_inc(dve_setup, 1)
                dve.tensor_scalar(S[0][:, 8:16], col("v2"), BN_EPS, None, ALU.add).then_inc(dve_setup, 1)
                dve.wait_ge(act_setup, 3)
                dve.wait_ge(dve_setup, 2)
                rsqrt_after_sqrt(link, dve, S[0][:, 0:16], S[3][:, 0:16], S[5][:, 0:16], S[1][:, 0:16])
                link(dve.tensor_tensor(sc1[:, :], col("g1"), S[5][:, 0:8], ALU.mult))
                link(dve.tensor_tensor(c1[:, :], col("b1"), col("m1"), ALU.subtract))
                link(dve.tensor_tensor(c1[:, :], c1[:, :], sc1[:, :], ALU.mult))
                link(dve.tensor_tensor(c1[:, :], c1[:, :], col("be1"), ALU.add))
                sc2 = S[6][:, 0:8]
                link(dve.tensor_tensor(sc2, col("g2"), S[5][:, 8:16], ALU.mult))
                link(dve.tensor_tensor(nc2[:, :], col("m2"), col("b2"), ALU.subtract))
                link(dve.tensor_tensor(nc2[:, :], nc2[:, :], sc2, ALU.mult))
                link(dve.tensor_tensor(nc2[:, :], nc2[:, :], col("be2"), ALU.subtract))
                dve.tensor_copy(bc_scale.rearrange("p (e k) -> p e k", e=E),
                                sc2.unsqueeze(2).to_broadcast([P, E, P])).then_inc(dve_setup, 1)
                link(dve.tensor_scalar(S[7][:, 0:NC], S[4][:, 0:NC], -1.0, 1.0, ALU.mult, ALU.add))
                link(dve.tensor_scalar(bgh[:, :], PT[:, bg_at:bg_at + NC], 0.5, None, ALU.mult))
                dve.wait_ge(weights_loaded, N_WEIGHTS)
                for c in range(NC):
                    link(dve.scalar_tensor_tensor(OF[:, c, :], SL[:, c, :], PT[:, bt_at + c:bt_at + c + 1], OF[:, c, :],
                                                  ALU.mult, ALU.add))
                    for t in (SL, OF):
                        link(dve.tensor_scalar(t[:, c, 0:NL], t[:, c, 0:NL], S[4][:, c:c + 1], None, ALU.mult))
                        link(dve.tensor_scalar(t[:, c, NL:2 * NL], t[:, c, NL:2 * NL], S[7][:, c:c + 1], None, ALU.mult))
                link(dve.tensor_tensor(OFA[:, :, :], OF[:, :, 0:2 * NL:2], OF[:, :, 1:2 * NL:2], ALU.subtract))
                link(dve.tensor_tensor(OFM[:, :, :], OF[:, :, 1:2 * NL - 1:2], OF[:, :, 3:2 * NL:2], ALU.subtract))
                link(dve.tensor_tensor(OFK[:, :], OF[:, :, NL - 1], OF[:, :, 2 * NL - 1], ALU.add))
                dve.wait_ge(pe_setup, 5)
                link(dve.tensor_copy(wtT, PS[1][:, :]))
                mw = S[8][:, 0:1]
                link(dve.tensor_reduce(mw, wtT, AX.X, ALU.max))
                dve.tensor_copy(mw_spread, mw.to_broadcast([P, P])).then_inc(dve_setup, 1)
                link(dve.tensor_scalar(wtT, wtT, mw, None, ALU.subtract))
                link(dve.tensor_copy(WP[:, 0, :], wtT))
                link(dve.tensor_tensor(wres, wtT, WP[:, 0, :], ALU.subtract))
                link(dve.tensor_copy(WP[:, 1, :], wres))
                link(dve.tensor_tensor(wres, wres, WP[:, 1, :], ALU.subtract))
                link(dve.tensor_copy(WP[:, 2, :], wres))
                dve.wait_ge(pool_made, 7)
                link(dve.tensor_copy(identb[:, :], ident[:, :]))
                link(dve.tensor_copy(onesb[:, :], ones[:, :]))
                link(dve.tensor_scalar(colb[:, :], coli[:, :], 1.0, None, ALU.subtract))
                link(dve.tensor_tensor(tri[:, :], pidx[:, :], colb[:, :], ALU.is_lt))
                dve.wait_ge(pe_setup, 7)
                link(dve.tensor_copy(mwrow[:, :], PS[7][:, 0:P]))
                for h in range(2):
                    w = W2[:, 4 * h:4 * h + 4, :].rearrange("p e k -> p (e k)")
                    link(dve.tensor_tensor(w, PS[5 + h][:, :], w, ALU.mult))
                dve.wait_ge(x_loaded, 64)
                with dve.Fori(0, NT) as t:
                    dve.bn_stats(STATS[:, bass.ds(t, 1), :].rearrange("p o s -> p (o s)"),
                                 X[:, bass.ds(t * P, P)]).then_inc(x_stats, 1)

        layer_norm_scales("ln1")

        def normalise(dve, dst, t):
            return dve.tensor_scalar(dst, X[:, bass.ds(t * P, P)], MEAN[:, bass.ds(t, 1)], RSTD[:, bass.ds(t, 1)],
                                     ALU.subtract, ALU.mult)

        def tile_stats(dve, t):
            return dve.bn_stats(STATS[:, bass.ds(t, 1), :].rearrange("p o s -> p (o s)"), X[:, bass.ds(t * P, P)])

        carve = Carve()
        adj_i = [carve(P).bitcast(I32) for _ in range(2)]
        adj_f = [carve(P) for _ in range(2)]
        xn = [carve(P) for _ in range(2)]
        xT = [carve(P) for _ in range(2)]
        hu = [carve(2 * (P + 1)) for _ in range(2)]
        tmp = [carve(P) for _ in range(2)]
        deg = [carve(4) for _ in range(2)]
        with nc.Block() as block:
            adj_loaded = [sem("adj_loaded0"), sem("adj_loaded1")]
            adj_cast, adj_masked = sem("adj_cast"), sem("adj_masked")
            xn_ready, xn_turned, xT_ready = sem("p1_xn_ready"), sem("p1_xn_turned"), sem("p1_xT_ready")
            hu_summed, hu_ready, msg_summed, msg_used = sem("hu_summed"), sem("hu_ready"), sem("msg_summed"), sem("msg_used")
            back_steps, x1_ready = sem("p1_back_steps"), sem("x1_ready")
            ones_set = sem("ones_set")

            @block.sync
            def _(sp):
                for p in range(2):
                    sp.dma_start(adj_i[p], a["adj"][p]).then_inc(adj_loaded[p], 16)
                with sp.Fori(0, NT // 2 - 1) as i:
                    for p in range(2):
                        t = i * 2 + p
                        sp.wait_ge(adj_cast, t + 1)
                        sp.wait_ge(adj_masked, t + 1)
                        sp.dma_start(adj_i[p], a["adj"][bass.ds(t + 2, 1)].rearrange("o p j -> (o p) j")).then_inc(adj_loaded[p], 16)

            @block.gpsimd
            def _(pool):
                for p in range(2):
                    pool.memset(hu[p][:, P:P + 1], 1.0).then_inc(ones_set, 1)

            @block.tensor
            def _(pe):
                def turn(t, p):
                    pe.wait_ge(xn_ready, t + 1)
                    wait(pe, xT_ready, t - 1)
                    pe.transpose(PS[p][:, 0:P], xn[p], ident[:, :]).then_inc(xn_turned, 1)

                def project(t, p):
                    pe.wait_ge(xT_ready, t + 1)
                    wait(pe, hu_ready, t - 1)
                    pe.matmul(PS[2 + p][:, 0:2 * P], ones[0:1, :], b0row[:, :], start=True, stop=False)
                    pe.matmul(PS[2 + p][:, 0:2 * P], xT[p], WMU[:, :], start=False, stop=True).then_inc(hu_summed, 1)

                def gather(t, p):
                    pe.wait_ge(hu_ready, t + 1)
                    pe.wait_ge(adj_cast, t + 1)
                    wait(pe, msg_used, t - 1)
                    pe.matmul(PS[4 + p][:, 0:P + 1], adj_f[p], hu[p][:, 0:P + 1], start=True, stop=True).then_inc(msg_summed, 1)

                pe.wait_ge(ones_set, 2)
                turn(0, 0)
                project(0, 0)
                turn(1, 1)
                gather(0, 0)
                project(1, 1)
                with pe.Fori(1, NT // 2) as i:
                    for p in range(2):
                        t = i * 2 + p
                        turn(t, p)
                        gather(t - 1, 1 - p)
                        project(t, p)
                gather(NT - 1, 1)

            @block.scalar
            def _(act):
                def tile(i, p):
                    t = i * 2 + p
                    act.wait_ge(adj_loaded[p], i * 16 + 16)
                    wait(act, msg_summed, t - 1)
                    act.copy(adj_f[p], adj_i[p]).then_inc(adj_cast, 1)
                    act.wait_ge(xn_turned, t + 1)
                    wait(act, hu_summed, t - 1)
                    act.copy(xT[p], PS[p][:, 0:P]).then_inc(xT_ready, 1)
                    act.wait_ge(hu_summed, t + 1)
                    wait(act, msg_used, t - 1)
                    act.copy(hu[p].rearrange("p (s d) -> p s d", s=2)[:, :, 0:P],
                             PS[2 + p][:, 0:2 * P].rearrange("p (s d) -> p s d", s=2)).then_inc(hu_ready, 1)

                for p in range(2):
                    tile(0, p)
                with act.Fori(1, NT // 2) as i:
                    for p in range(2):
                        tile(i, p)

            @block.vector
            def _(dve):
                def front(i, p):
                    t = i * 2 + p
                    wait(dve, xn_turned, t - 1)
                    normalise(dve, xn[p], t).then_inc(xn_ready, 1)
                    dve.wait_ge(adj_loaded[p], i * 16 + 16)
                    dve.tensor_scalar(M1[:, bass.ds(t * P, P)], adj_i[p], 1.0, None, ALU.is_equal)
                    dve.tensor_reduce(FLG[:, bass.ds(t, 1)], adj_i[p], AX.X, ALU.max).then_inc(adj_masked, 1)

                def back(t, p):
                    m, d = PS[4 + p], deg[p]
                    dve.wait_ge(msg_summed, t + 1)
                    dve.tensor_scalar(d[:, 0:1], m[:, P:P + 1], 1.0, None, ALU.max).then_inc(back_steps, 1)
                    dve.wait_ge(back_steps, t * 4 + 1)
                    dve.reciprocal(d[:, 1:2], d[:, 0:1]).then_inc(back_steps, 1)
                    dve.wait_ge(back_steps, t * 4 + 2)
                    dve.scalar_tensor_tensor(d[:, 2:3], m[:, P:P + 1], 0.0, d[:, 1:2], ALU.is_gt, ALU.mult).then_inc(back_steps, 1)
                    dve.wait_ge(back_steps, t * 4 + 3)
                    dve.scalar_tensor_tensor(tmp[p], m[:, 0:P], d[:, 2:3], hu[p][:, P + 1:2 * P + 1],
                                             ALU.mult, ALU.add).then_inc(msg_used, 1)
                    x = X[:, bass.ds(t * P, P)]
                    dve.wait_ge(msg_used, t + 1)
                    dve.scalar_tensor_tensor(x, tmp[p], 0.0, x, ALU.max, ALU.add).then_inc(back_steps, 1)
                    dve.wait_ge(back_steps, t * 4 + 4)
                    tile_stats(dve, t).then_inc(x1_ready, 1)

                front(0, 0)
                front(0, 1)
                back(0, 0)
                with dve.Fori(1, NT // 2) as i:
                    front(i, 0)
                    back(i * 2 - 1, 1)
                    front(i, 1)
                    back(i * 2, 0)
                back(NT - 1, 1)

        layer_norm_scales("ln2")

        carve = Carve()
        feat = [carve(P) for _ in range(2)]
        featT = carve(P)
        route = carve(64)
        spread = carve(E * P)
        c2diag = carve(E * E)
        wT = carve(P)
        C8 = carve(P)
        with nc.Block() as block:
            f_steps, f_sum = sem("f_steps"), [sem("f_sum0"), sem("f_sum1")]
            r_pe, r_act, r_dve = sem("r_pe"), sem("r_act"), sem("r_dve")

            @block.vector
            def _(dve):
                link = Chain(dve, f_steps)
                for p in range(2):
                    dve.memset(feat[p], 0.0).then_inc(f_sum[p], 1)
                with dve.Fori(0, NT // 2) as i:
                    for p in range(2):
                        t = i * 2 + p
                        dve.wait_ge(f_sum[p], i + 1)
                        dve.scalar_tensor_tensor(feat[p], X[:, bass.ds(t * P, P)], RSTD[:, bass.ds(t, 1)], feat[p],
                                                 ALU.mult, ALU.add).then_inc(f_sum[p], 1)
                for p in range(2):
                    dve.wait_ge(f_sum[p], NT // 2 + 1)
                link(dve.tensor_tensor(S[1], MEAN[:, :], RSTD[:, :], ALU.mult))
                link(dve.tensor_reduce(S[2][:, 0:1], S[1], AX.X, ALU.add))
                link(dve.tensor_tensor(feat[0], feat[0], feat[1], ALU.add))
                link(dve.tensor_scalar(feat[0], feat[0], S[2][:, 0:1], 1.0 / NT, ALU.subtract, ALU.mult))
                dve.sem_inc(r_dve, 1)
                dve.wait_ge(r_pe, 2)
                logits, shifted, ex, w = (route[:, 8 * i:8 * i + 8] for i in range(4))
                link(dve.tensor_copy(logits, PS[1][:, 0:E]))
                link(dve.tensor_reduce(route[:, 40:41], logits, AX.X, ALU.max))
                link(dve.tensor_scalar(shifted, logits, route[:, 40:41], None, ALU.subtract))
                dve.sem_inc(r_dve, 1)
                dve.wait_ge(r_act, 2)
                link(dve.reciprocal(route[:, 42:43], route[:, 41:42]))
                link(dve.tensor_scalar(w, ex, route[:, 42:43], None, ALU.mult))
                link(dve.tensor_copy(spread.rearrange("p (e k) -> p e k", e=E), w.unsqueeze(2).to_broadcast([P, E, P])))
                link(dve.memset(c2diag, 0.0))
                link(dve.tensor_scalar(c2diag[:, 0:E * E:E + 1], nc2[:, :], -1.0, None, ALU.mult))
                dve.sem_inc(r_dve, 1)
                dve.wait_ge(r_pe, 5)
                for h in range(2):
                    link(dve.tensor_copy(WB[:, 4 * h:4 * h + 4, :].rearrange("p e k -> p (e k)"), PS[2 + h][:, :]))
                dve.wait_ge(r_pe, 6)
                link(dve.tensor_copy(CW[:, :], PS[6][:, 0:P]))
                link(dve.tensor_reduce(S[1][:, 0:1], FLG[:, :], AX.X, ALU.max))
                dve.sem_inc(r_dve, 1)
                dve.wait_ge(r_pe, 7)
                link(dve.tensor_reduce(S[2][0:1, 0:1], PS[7][0:1, 0:P], AX.X, ALU.max))
                link(dve.tensor_scalar(flag[0:1, 0:1], S[2][0:1, 0:1], 2.0, None, ALU.is_ge))

            @block.scalar
            def _(act):
                act.wait_ge(r_pe, 1)
                act.copy(featT, PS[0][:, 0:P]).then_inc(r_act, 1)
                act.wait_ge(r_dve, 2)
                act.activation(route[:, 16:24], route[:, 8:16], ACT.Exp, accum_out=route[:, 41:42]).then_inc(r_act, 1)
                act.wait_ge(r_pe, 3)
                act.copy(wT[0:E, :], PS[4][0:E, 0:P]).then_inc(r_act, 1)
                act.wait_ge(r_pe, 4)
                act.copy(C8[0:E, :], PS[5][0:E, 0:P]).then_inc(r_act, 1)

            @block.tensor
            def _(pe):
                pe.wait_ge(r_dve, 1)
                pe.transpose(PS[0][:, 0:P], feat[0], ident[:, :]).then_inc(r_pe, 1)
                pe.wait_ge(r_act, 1)
                pe.matmul(PS[1][:, 0:E], ones[0:1, :], brrow[:, :], start=True, stop=False)
                pe.matmul(PS[1][:, 0:E], featT, Wr[:, :], start=False, stop=True).then_inc(r_pe, 1)
                pe.wait_ge(r_dve, 3)
                pe.transpose(PS[4][0:E, 0:P], route[:, 24:32], ident[:, :]).then_inc(r_pe, 1)
                pe.matmul(PS[5][0:E, 0:P], ident[0:E, 0:E], bo[:, :], start=True, stop=False)
                for e in range(E):
                    last = pe.matmul(PS[5][0:E, 0:P], c2diag[:, e * E:(e + 1) * E], Wo[:, e, :], start=False, stop=(e == E - 1))
                last.then_inc(r_pe, 1)
                for e in range(E):
                    last = pe.matmul(PS[2 + e // 4][:, (e % 4) * P:(e % 4 + 1) * P], spread[:, e * P:(e + 1) * P], ident[:, :],
                                     start=True, stop=True)
                last.then_inc(r_pe, 1)
                pe.wait_ge(r_act, 4)
                pe.matmul(PS[6][:, 0:P], wT[0:E, :], C8[0:E, :], start=True, stop=True).then_inc(r_pe, 1)
                pe.wait_ge(r_dve, 4)
                pe.matmul(PS[7][0:1, 0:P], S[1][:, 0:1], ident[:, :], start=True, stop=True).then_inc(r_pe, 1)

        carve = Carve()
        xn4 = [carve(GW) for _ in range(2)]
        xT4 = [carve(GW) for _ in range(2)]
        h1 = [carve(GW) for _ in range(2)]
        h2 = [carve(GW) for _ in range(2)]
        with nc.Block() as block:
            xn_ready, xn_turned, xT_ready = sem("p2_xn_ready"), sem("p2_xn_turned"), sem("p2_xT_ready")
            h1_summed, h1_ready, h2_summed, h2_ready = sem("h1_summed"), sem("h1_ready"), sem("h2_summed"), sem("h2_ready")
            h2_used, y_summed = sem("h2_used"), sem("y_summed")
            cw_added, y_used, x2_ready = sem("cw_added"), sem("y_used"), sem("x2_ready")

            @block.gpsimd
            def _(pool):
                with pool.Fori(0, NG) as g:
                    pool.wait_ge(xn_ready, g * 4 + 4)
                    x = X[:, bass.ds(g * GW, GW)].rearrange("p (t d) -> p t d", d=P)
                    pool.tensor_tensor(x, x, CW[:, :].unsqueeze(1).to_broadcast([P, G4, P]), ALU.add).then_inc(cw_added, 1)

            @block.tensor
            def _(pe):
                def turn(g, p):
                    pe.wait_ge(xn_ready, g * 4 + 4)
                    wait(pe, xT_ready, g)
                    for j in range(G4):
                        last = pe.transpose(PS[0][:, j * P:(j + 1) * P], xn4[p][:, j * P:(j + 1) * P], ident[:, :])
                    last.then_inc(xn_turned, 1)

                def group(g, p, nxt):
                    def first(e):
                        if e == 0:
                            pe.wait_ge(xT_ready, g + 1)
                        wait(pe, h1_ready, g * E + e - 1)
                        pe.matmul(PS[1 + e % 2][:, :], W1[:, e, :], xT4[p], start=True, stop=True).then_inc(h1_summed, 1)

                    def second(e):
                        pe.wait_ge(h1_ready, g * E + e + 1)
                        wait(pe, h2_ready, g * E + e - 1)
                        pe.matmul(PS[3 + e % 2][:, :], W2[:, e, :], h1[e % 2], start=True, stop=True).then_inc(h2_summed, 1)

                    def third(e):
                        pe.wait_ge(h2_ready, g * E + e + 1)
                        if e == 0:
                            wait(pe, y_used, g)
                        for j in range(G4):
                            last = pe.matmul(PS[5 + p][:, j * P:(j + 1) * P], h2[e % 2][:, j * P:(j + 1) * P], Wo[:, e, :],
                                             start=(e == 0 and j == 0), stop=(e == E - 1), skip_group_check=True)
                        last.then_inc(h2_used, 1)

                    for e in range(E + 2):
                        if e < E:
                            first(e)
                        if e == 5 and nxt:
                            turn(*nxt)
                        if 1 <= e <= E:
                            second(e - 1)
                        if e >= 2:
                            third(e - 2)

                turn(0, 0)
                group(0, 0, (1, 1))
                with pe.Fori(0, NG // 2 - 1) as i:
                    group(i * 2 + 1, 1, (i * 2 + 2, 0))
                    group(i * 2 + 2, 0, (i * 2 + 3, 1))
                group(NG - 1, 1, None)

            @block.scalar
            def _(act):
                def copy_xT(g, p):
                    act.wait_ge(xn_turned, g + 1)
                    wait(act, h1_summed, (g - 1) * E)
                    act.copy(xT4[p], PS[0][:, :]).then_inc(xT_ready, 1)

                def group(g, p, nxt):
                    for e in range(E):
                        act.wait_ge(h1_summed, g * E + e + 1)
                        wait(act, h2_summed, g * E + e - 1)
                        act.activation(h1[e % 2], PS[1 + e % 2][:, :], ACT.Relu, bias=c1[:, e:e + 1],
                                       scale=sc1[:, e:e + 1]).then_inc(h1_ready, 1)
                        if e == 5 and nxt:
                            copy_xT(*nxt)

                copy_xT(0, 0)
                group(0, 0, (1, 1))
                with act.Fori(0, NG // 2 - 1) as i:
                    group(i * 2 + 1, 1, (i * 2 + 2, 0))
                    group(i * 2 + 2, 0, (i * 2 + 3, 1))
                group(NG - 1, 1, None)

            @block.vector
            def _(dve):
                def norms(g, p):
                    wait(dve, xn_turned, g - 1)
                    for j in range(G4):
                        normalise(dve, xn4[p][:, j * P:(j + 1) * P], g * G4 + j).then_inc(xn_ready, 1)

                def group(g, p, nxt):
                    for e in range(E):
                        dve.wait_ge(h2_summed, g * E + e + 1)
                        wait(dve, h2_used, g * E + e - 1)
                        dve.scalar_tensor_tensor(h2[e % 2].rearrange("p (t n) -> p t n", n=P),
                                                 PS[3 + e % 2][:, :].rearrange("p (t n) -> p t n", n=P),
                                                 nc2[:, e:e + 1], WB[:, e:e + 1, :].to_broadcast([P, G4, P]),
                                                 ALU.max, ALU.mult).then_inc(h2_ready, 1)
                        if e == 2 and nxt:
                            norms(*nxt)

                def finish(g, p):
                    dve.wait_ge(h2_used, g * E + E)
                    dve.wait_ge(cw_added, g + 1)
                    x = X[:, bass.ds(g * GW, GW)]
                    dve.tensor_tensor(x, PS[5 + p][:, :], x, ALU.add).then_inc(y_used, 1)
                    dve.wait_ge(y_used, g + 2)
                    for j in range(G4):
                        tile_stats(dve, g * G4 + j).then_inc(x2_ready, 1)

                dve.sem_inc(y_used, 1)
                norms(0, 0)
                group(0, 0, (1, 1))
                finish(0, 0)
                with dve.Fori(0, NG // 2 - 1) as i:
                    group(i * 2 + 1, 1, (i * 2 + 2, 0))
                    finish(i * 2 + 1, 1)
                    group(i * 2 + 2, 0, (i * 2 + 3, 1))
                    finish(i * 2 + 2, 0)
                group(NG - 1, 1, None)
                finish(NG - 1, 1)

        layer_norm_scales("ln3")

        carve = Carve()
        g_adj = carve(P).bitcast(I32)
        g_adjf, g_adjT, g_xn, g_xT = carve(P), carve(P), carve(P), carve(P)
        g_hg = carve(4 * P)
        g_rel = carve(1)
        g_sel, g_mf, g_mb = carve(P), carve(P), carve(P)
        g_sig, g_val = carve(2 * P), carve(2 * P)
        with nc.Block() as block:
            ga_loaded, ga_free, g_in = sem("ga_loaded"), sem("ga_free"), sem("g_in")
            g_turned, g_copied, g_proj, g_hgready = sem("g_turned"), sem("g_copied"), sem("g_proj"), sem("g_hgready")
            g_rset, g_mask, g_vsum, g_sigready, g_valready, g_acc, g_added = (
                sem("g_rset"), sem("g_mask"), sem("g_vsum"), sem("g_sigready"), sem("g_valready"), sem("g_acc"), sem("g_added"))

            def if_relations(eng):
                return eng.If(eng.value_load(flag[0:1, 0:1]) > 0)

            @block.sync
            def _(sp):
                with if_relations(sp):
                    with sp.Fori(0, NT) as t:
                        sp.wait_ge(ga_free, t + 1)
                        sp.dma_start(g_adj, a["adj"][bass.ds(t, 1)].rearrange("o p j -> (o p) j")).then_inc(ga_loaded, 16)

            @block.vector
            def _(dve):
                with if_relations(dve):
                    dve.sem_inc(ga_free, 1)
                    with dve.Fori(0, NT) as t:
                        dve.wait_ge(ga_loaded, t * 16 + 16)
                        dve.tensor_copy(g_adjf, g_adj).then_inc(ga_free, 1)
                        dve.memset(g_rel, 1.0).then_inc(g_rset, 1)
                        normalise(dve, g_xn, t).then_inc(g_in, 1)
                        with dve.Fori(0, NREL) as r:
                            n = t * NREL + r
                            dve.wait_ge(g_hgready, t + 1)
                            dve.wait_ge(ga_free, t + 2)
                            dve.wait_ge(g_rset, t * (NREL + 1) + r + 1)
                            dve.tensor_scalar(g_rel, g_rel, 1.0, None, ALU.add).then_inc(g_rset, 1)
                            dve.wait_ge(g_rset, t * (NREL + 1) + r + 2)
                            dve.tensor_scalar(g_sel, pidx[:, :], 2.0, g_rel, ALU.add, ALU.is_equal).then_inc(g_mask, 1)
                            dve.tensor_scalar(g_mf, g_adjT, g_rel, None, ALU.is_equal).then_inc(g_mask, 1)
                            dve.tensor_scalar(g_mb, g_adjf, g_rel, None, ALU.is_equal).then_inc(g_mask, 1)
                            dve.wait_ge(g_sigready, n * 2 + 2)
                            for h in range(2):
                                dve.tensor_tensor(g_val[:, h * P:(h + 1) * P], PS[2][:, 2 * h * P:(2 * h + 1) * P],
                                                  g_sig[:, h * P:(h + 1) * P], ALU.mult).then_inc(g_valready, 1)
                            dve.wait_ge(g_acc, n + 1)
                            ex = EX[:, bass.ds(t * P, P)]
                            dve.tensor_tensor(ex, PS[3][:, 0:P], ex, ALU.add).then_inc(g_added, 1)
                            dve.wait_ge(g_added, n + 1)

            @block.scalar
            def _(act):
                with if_relations(act):
                    with act.Fori(0, NT) as t:
                        act.wait_ge(g_turned, t + 1)
                        act.copy(g_adjT, PS[0][:, 0:P]).then_inc(g_copied, 1)
                        act.copy(g_xT, PS[0][:, P:2 * P]).then_inc(g_copied, 1)
                        act.wait_ge(g_proj, t + 1)
                        act.wait_ge(g_copied, t * 2 + 2)
                        act.copy(g_hg, PS[1][:, :]).then_inc(g_hgready, 1)
                        with act.Fori(0, NREL) as r:
                            act.wait_ge(g_vsum, t * NREL + r + 1)
                            for h in range(2):
                                act.activation(g_sig[:, h * P:(h + 1) * P], PS[2][:, (2 * h + 1) * P:(2 * h + 2) * P],
                                               ACT.Sigmoid).then_inc(g_sigready, 1)

            @block.tensor
            def _(pe):
                with if_relations(pe):
                    with pe.Fori(0, NT) as t:
                        pe.wait_ge(g_in, t + 1)
                        pe.wait_ge(ga_free, t + 2)
                        pe.transpose(PS[0][:, 0:P], g_adjf, ident[:, :])
                        pe.transpose(PS[0][:, P:2 * P], g_xn, ident[:, :]).then_inc(g_turned, 1)
                        pe.wait_ge(g_copied, t * 2 + 2)
                        pe.matmul(PS[1][:, :], g_xT, WHG[:, 0:2, :, :].rearrange("p i s d -> p (i s d)"),
                                  start=True, stop=True).then_inc(g_proj, 1)
                        with pe.Fori(0, NREL) as r:
                            n = t * NREL + r
                            pe.wait_ge(g_hgready, t + 1)
                            pe.wait_ge(g_mask, n * 3 + 3)
                            pe.matmul(PS[2][:, :], ident[:, :], g_hg, start=True, stop=False)
                            pe.matmul(PS[2][:, :], g_sel, B4[:, :], start=False, stop=True).then_inc(g_vsum, 1)
                            pe.wait_ge(g_valready, n * 2 + 2)
                            pe.matmul(PS[3][:, 0:P], g_mf, g_val[:, 0:P], start=True, stop=False)
                            pe.matmul(PS[3][:, 0:P], g_mb, g_val[:, P:2 * P], start=False, stop=True).then_inc(g_acc, 1)

        carve = Carve()
        xn = [carve(P) for _ in range(2)]
        xT = [carve(P) for _ in range(2)]
        m1f = [carve(P) for _ in range(2)]
        sig = [carve(P) for _ in range(2)]
        val = [carve(P) for _ in range(2)]
        tmp = [carve(P) for _ in range(2)]
        with nc.Block() as block:
            xn_ready, xn_turned, xT_ready = sem("p3_xn_ready"), sem("p3_xn_turned"), sem("p3_xT_ready")
            hg_summed, sig_ready, val_ready = sem("hg_summed"), sem("sig_ready"), sem("val_ready")
            m1_ready, agg_summed, agg_used, relu_done, x3_ready = (
                sem("m1_ready"), sem("agg_summed"), sem("agg_used"), sem("relu_done"), sem("x3_ready"))

            @block.gpsimd
            def _(pool):
                def tile(t, p):
                    wait(pool, agg_summed, t - 1)
                    pool.tensor_copy(m1f[p], M1[:, bass.ds(t * P, P)]).then_inc(m1_ready, 1)

                tile(0, 0)
                tile(1, 1)
                with pool.Fori(1, NT // 2) as i:
                    for p in range(2):
                        tile(i * 2 + p, p)

            @block.tensor
            def _(pe):
                def turn(t, p):
                    pe.wait_ge(xn_ready, t + 1)
                    wait(pe, xT_ready, t - 1)
                    pe.transpose(PS[p][:, 0:P], xn[p], ident[:, :]).then_inc(xn_turned, 1)

                def project(t, p):
                    pe.wait_ge(xT_ready, t + 1)
                    wait(pe, val_ready, t - 1)
                    pe.matmul(PS[2 + p][:, 0:2 * P], ones[0:1, :], b1row[:, :], start=True, stop=False)
                    pe.matmul(PS[2 + p][:, 0:2 * P], xT[p], WHG[:, 2, :, :].rearrange("p s d -> p (s d)"),
                              start=False, stop=True).then_inc(hg_summed, 1)

                def gather(t, p):
                    pe.wait_ge(val_ready, t + 1)
                    pe.wait_ge(m1_ready, t + 1)
                    wait(pe, agg_used, t - 1)
                    pe.matmul(PS[4 + p][:, 0:P], m1f[p], val[p], start=True, stop=True).then_inc(agg_summed, 1)

                turn(0, 0)
                project(0, 0)
                turn(1, 1)
                project(1, 1)
                gather(0, 0)
                with pe.Fori(1, NT // 2) as i:
                    for p in range(2):
                        t = i * 2 + p
                        turn(t, p)
                        project(t, p)
                        gather(t - 1, 1 - p)
                gather(NT - 1, 1)

            @block.scalar
            def _(act):
                def tile(t, p):
                    act.wait_ge(xn_turned, t + 1)
                    wait(act, hg_summed, t - 1)
                    act.copy(xT[p], PS[p][:, 0:P]).then_inc(xT_ready, 1)
                    act.wait_ge(hg_summed, t + 1)
                    wait(act, val_ready, t - 1)
                    act.activation(sig[p], PS[2 + p][:, P:2 * P], ACT.Sigmoid).then_inc(sig_ready, 1)

                tile(0, 0)
                tile(1, 1)
                with act.Fori(1, NT // 2) as i:
                    for p in range(2):
                        tile(i * 2 + p, p)

            @block.vector
            def _(dve):
                def front(t, p):
                    wait(dve, xn_turned, t - 1)
                    normalise(dve, xn[p], t).then_inc(xn_ready, 1)

                def middle(t, p):
                    dve.wait_ge(sig_ready, t + 1)
                    wait(dve, agg_summed, t - 1)
                    dve.tensor_tensor(val[p], PS[2 + p][:, 0:P], sig[p], ALU.mult).then_inc(val_ready, 1)

                def back(t, p):
                    x = X[:, bass.ds(t * P, P)]
                    dve.wait_ge(agg_summed, t + 1)
                    dve.tensor_tensor(tmp[p], PS[4 + p][:, 0:P], EX[:, bass.ds(t * P, P)], ALU.add).then_inc(agg_used, 1)
                    dve.wait_ge(agg_used, t + 1)
                    dve.scalar_tensor_tensor(x, tmp[p], 0.0, x, ALU.max, ALU.add).then_inc(relu_done, 1)
                    dve.wait_ge(relu_done, t + 1)
                    tile_stats(dve, t).then_inc(x3_ready, 1)

                front(0, 0)
                front(1, 1)
                middle(0, 0)
                middle(1, 1)
                back(0, 0)
                with dve.Fori(1, NT // 2) as i:
                    for p in range(2):
                        t = i * 2 + p
                        front(t, p)
                        middle(t, p)
                        back(t - 1, 1 - p)
                back(NT - 1, 1)

        layer_norm_scales("ln4")

        class Pwl:
            def __init__(self, tag):
                self.lines_ready, self.acts_ready = sem(tag + "_lines_ready"), sem(tag + "_acts_ready")
                self.stepped, self.chunk_summed = sem(tag + "_stepped"), sem(tag + "_chunk_summed")
                self.out_summed, self.out_made, self.out_stored = (
                    sem(tag + "_out_summed"), sem(tag + "_out_made"), sem(tag + "_out_stored"))

        at_ex = [0]

        def carve_ex(n):
            v = EX[:, at_ex[0]:at_ex[0] + n]
            at_ex[0] += n
            assert at_ex[0] <= NT * P
            return v

        carve = Carve()
        Z = [carve_ex(GW) for _ in range(NC)]
        T = [carve_ex(NH) for _ in range(G4)]
        ring = [carve_ex(GW) for _ in range(PAIRS)]
        TO = carve(NH)
        YE = carve(G4 * YW).rearrange("p (j w) -> p j w", j=G4)
        YO = carve(YW)
        slotm = [carve(P) for _ in range(G4)]
        slotT = carve(G4 * P)
        xna, xT4 = carve(GW), carve(GW)
        OH = [carve(8 * P // 2).bitcast(BF16) for _ in range(2)]
        OHT = [carve(8 * P // 2).bitcast(BF16) for _ in range(2)]
        gelu, gate, cv, cc, tr = (carve(GW) for _ in range(5))
        F = [carve(GW) for _ in range(2)]
        outs = carve(GW)
        top = [carve(8) for _ in range(2)]
        topo = carve(R2)
        rest = carve(8 * G4)
        resto = carve(8)
        taken = carve(2)
        index = carve(8).bitcast(U32)
        padded = carve(4).bitcast(BF16)
        opened = padded[:, G4 - 1:2 * G4 - 1]
        closed = carve(G4)
        slot = carve(G4)
        sel = [carve(P) for _ in range(2)]
        dcount = carve(1)
        BT, BM, BCLS, BGATE, BOUT = PS[3], PS[4], PS[5], PS[6], PS[7]
        RELEASE = [0, 1, 4, 5, 8, 9, 12, 13]

        def act_pair(act, s, m, c, i):
            k = i // 2 + (i % 2) * (NL // 2)
            wait(act, s.stepped, (m - 1) * STEPS + RELEASE[i] + 1)
            act.activation(ring[i], Z[c], ACT.Identity, bias=OFA[:, c, k:k + 1],
                           scale=SL[:, c, 2 * k:2 * k + 1]).then_inc(s.lines_ready, 1)

        def act_functions(act, s, m, c):
            act.wait_ge(s.chunk_summed, m + 1)
            wait(act, s.stepped, m * STEPS)
            act.activation(gelu, BCLS[:, :], ACT.Gelu, bias=PT[:, bc_at + c:bc_at + c + 1]).then_inc(s.acts_ready, 1)
            act.activation(gate, BGATE[:, :], ACT.Tanh, bias=bgh[:, c:c + 1], scale=0.5).then_inc(s.acts_ready, 1)

        def dve_step(dve, s, m, c, n):
            after = m * STEPS + n
            if n < 14:
                side = n % 2
                acc, op = ((cv, ALU.max), (cc, ALU.min))[side]
                pair = 0 if n < 2 else (n - 2) // 4 + 1
                k = pair + side * (NL // 2)
                i = 2 * pair + side
                if n < 2 or (n - 2) % 4 < 2:
                    dve.wait_ge(s.lines_ready, m * PAIRS + i + 1)
                    wait(dve, s.stepped, after - 1)
                    dve.scalar_tensor_tensor(acc if n < 2 else ring[i], Z[c], SL[:, c, 2 * k + 1:2 * k + 2], ring[i],
                                             ALU.mult, op).then_inc(s.stepped, 1)
                else:
                    dve.wait_ge(s.stepped, after - 1)
                    dve.scalar_tensor_tensor(acc, acc, OFM[:, c, k - 1:k], ring[i], ALU.add, op).then_inc(s.stepped, 1)
            else:
                dve.wait_ge(s.stepped, after)
                if n == 14:
                    dve.scalar_tensor_tensor(tr, cv, OFK[:, c:c + 1], cc, ALU.add, ALU.add).then_inc(s.stepped, 1)
                elif n == 15:
                    dve.wait_ge(s.acts_ready, m * 2 + 2)
                    dve.tensor_tensor(tr, tr, gelu, ALU.subtract).then_inc(s.stepped, 1)
                elif n == 16:
                    dve.scalar_tensor_tensor(tr, gate, 1.0, tr, ALU.add, ALU.mult).then_inc(s.stepped, 1)
                else:
                    wait(dve, s.out_summed, m - 1)
                    dve.scalar_tensor_tensor(F[c % 2], tr, 0.5, gelu, ALU.mult, ALU.add).then_inc(s.stepped, 1)

        def pe_chunk(pe, s, m, c):
            wait(pe, s.acts_ready, m * 2)
            cols = slice(c * P, (c + 1) * P)
            pe.matmul(BCLS[:, :], Wc[:, cols], xT4, start=True, stop=True)
            pe.matmul(BGATE[:, :], Wg[:, cols], xT4, start=True, stop=True).then_inc(s.chunk_summed, 1)

        def pe_out(pe, s, m, c, g):
            pe.wait_ge(s.stepped, m * STEPS + STEPS)
            if c == 0:
                wait(pe, s.out_made, g)
                pe.matmul(BOUT[:, :], ones[0:1, :], bdrow[:, :], start=True, stop=False, skip_group_check=True)
            for j in range(G4):
                last = pe.matmul(BOUT[:, j * P:(j + 1) * P], F[c % 2][:, j * P:(j + 1) * P], Wd[:, c, :],
                                 start=False, stop=(c == NC - 1), skip_group_check=True)
            last.then_inc(s.out_summed, 1)

        def dve_finish(dve, s, g):
            dve.wait_ge(s.out_summed, g * NC + NC)
            dve.wait_ge(s.out_stored, g * 16 + 16)
            dve.tensor_tensor(outs, BOUT[:, :], X[:, bass.ds(g * GW, GW)], ALU.add).then_inc(s.out_made, 1)

        def store_groups(sp, s):
            sp.sem_inc(s.out_stored, 16)
            with sp.Fori(0, NG) as g:
                sp.wait_ge(s.out_made, g + 1)
                sp.dma_start(out[bass.ds(g * G4, G4)].rearrange("t p d -> p t d"),
                             outs.rearrange("p (t d) -> p t d", d=P)).then_inc(s.out_stored, 16)
            sp.wait_ge(s.out_stored, NG * 16 + 16)

        def all_groups(eng, iteration):
            iteration(0)
            iteration(1)
            with eng.Fori(2, NG - 1) as g:
                iteration(g)
            iteration(NG - 1)
            iteration(NG)

        def has_tiles(g):
            return not isinstance(g, int) or g < NG

        def has_next(g):
            return not isinstance(g, int) or g < NG - 1

        def has_pwl(g):
            return not isinstance(g, int) or g >= 1

        def has_finish(g):
            return not isinstance(g, int) or g >= 2

        s4 = Pwl("p4")
        ones_made, y_steps, oh_ready, oh_turned, oht_ready = (
            sem("ones_made"), sem("y_steps"), sem("oh_ready"), sem("oh_turned"), sem("oht_ready"))
        cand_summed, cand_used = sem("cand_summed"), sem("cand_used")
        min_ready, open_ready, slots_given, slotm_ready = sem("min_ready"), sem("open_ready"), sem("slots_given"), sem("slotm_ready")
        bm_filled, bm_read = sem("bm_filled"), sem("bm_read")
        xna_ready = sem("xna_ready")
        F_SLOT, F_ROWS, F_SLOTT, F_XT, F_Z = 0, 1, 2, 3, 4
        with nc.Block() as block:
            @block.sync
            def _(sp):
                store_groups(sp, s4)

            @block.tensor
            def _(pe):
                def turn_onehots(q, slot_):
                    pe.wait_ge(oh_ready, q + 1)
                    wait(pe, oht_ready, q)
                    for k in range(8):
                        last = pe.transpose(BT[:, :].bitcast(BF16)[:, k * P:(k + 1) * P], OH[slot_][:, k * P:(k + 1) * P],
                                            identb[:, :])
                    last.then_inc(oh_turned, 1)

                def candidates(q, slot_, g, u0):
                    pe.wait_ge(oht_ready, q + 1)
                    for k in range(8):
                        u = u0 + k
                        before = {0: 51, 1: 49, 2: 50}[u] - USES if u < 3 else u - 3
                        wait(pe, cand_used, g * USES + before + 1)
                        for part in range(3):
                            last = pe.matmul(PS[u % 3][:, :], OHT[slot_][:, k * P:(k + 1) * P], WP[:, part, :],
                                             start=(part == 0), stop=(part == 2))
                        last.then_inc(cand_summed, 1)

                def fill(g, f):
                    wait(pe, bm_read, g * FILLS + f)

                def iteration(g):
                    q0, m0 = g * ROUNDS, (g - 1) * NC
                    for j in range(G4):
                        if has_tiles(g):
                            if j + 1 < G4:
                                turn_onehots(q0 + j + 1, (j + 1) % 2)
                            candidates(q0 + j, j % 2, g, j * R1)
                        if j in (0, 2) and has_pwl(g):
                            pe_chunk(pe, s4, m0 + j // 2, j // 2)
                        if j == 1 and has_finish(g):
                            pe_out(pe, s4, m0 - 1, NC - 1, g - 2)
                        if j == 3 and has_pwl(g):
                            pe_out(pe, s4, m0, 0, g - 1)
                    if has_tiles(g):
                        fill(g, F_SLOT)
                        pe.wait_ge(open_ready, g + 1)
                        pe.matmul(BM[:, 0:G4], tri[:, :], opened, start=True, stop=False)
                        for j in range(1, G4):
                            last = pe.matmul(BM[:, 0:G4], onesb[:, :], padded[:, G4 - 1 - j:2 * G4 - 1 - j],
                                             start=False, stop=(j == G4 - 1))
                        last.then_inc(bm_filled, 1)
                    if has_pwl(g):
                        pe_chunk(pe, s4, m0 + 2, 2)
                    if has_tiles(g):
                        fill(g, F_ROWS)
                        pe.wait_ge(slotm_ready, g * G4 + G4)
                        for j in range(G4):
                            last = pe.matmul(BM[:, 0:YW], slotm[j], YE[:, j, :], start=(j == 0), stop=(j == G4 - 1))
                        last.then_inc(bm_filled, 1)
                        fill(g, F_SLOTT)
                        for j in range(G4):
                            last = pe.transpose(BM[:, j * P:(j + 1) * P], slotm[j], ident[:, :])
                        last.then_inc(bm_filled, 1)
                        turn_onehots(q0 + 4, 0)
                    if has_pwl(g):
                        pe_out(pe, s4, m0 + 1, 1, g - 1)
                    if has_tiles(g):
                        turn_onehots(q0 + 5, 1)
                        candidates(q0 + 4, 0, g, G4 * R1)
                    if has_pwl(g):
                        pe_chunk(pe, s4, m0 + 3, 3)
                    if has_tiles(g):
                        candidates(q0 + 5, 1, g, G4 * R1 + 8)
                        if has_next(g):
                            turn_onehots(q0 + ROUNDS, 0)
                    if has_pwl(g):
                        pe_out(pe, s4, m0 + 2, 2, g - 1)
                    if has_tiles(g):
                        pe.wait_ge(bm_read, g * FILLS + F_SLOTT + 1)
                        pe.wait_ge(cand_used, g * USES + G4 * R1 + R2)
                        for j in range(G4):
                            u = G4 * R1 + R2 + j
                            pe.wait_ge(cand_used, g * USES + u - 2)
                            pe.matmul(PS[u % 3][:, :], slotT[:, j * P:(j + 1) * P], TO, start=True, stop=True).then_inc(cand_summed, 1)
                        fill(g, F_XT)
                        pe.wait_ge(xna_ready, g * G4 + G4)
                        for j in range(G4):
                            last = pe.transpose(BM[:, j * P:(j + 1) * P], xna[:, j * P:(j + 1) * P], ident[:, :])
                        last.then_inc(bm_filled, 1)
                        pe.wait_ge(cand_used, (g + 1) * USES)
                        for c in range(NC):
                            fill(g, F_Z + c)
                            for j in range(G4):
                                last = pe.transpose(BM[:, j * P:(j + 1) * P], T[j][:, c * P:(c + 1) * P], ident[:, :])
                            last.then_inc(bm_filled, 1)
                    elif True:
                        pe_out(pe, s4, m0 + 3, 3, g - 1)

                turn_onehots(0, 0)
                all_groups(pe, iteration)

            @block.scalar
            def _(act):
                def copy_onehots(q, slot_):
                    act.wait_ge(oh_turned, q + 1)
                    act.copy(OHT[slot_], BT[:, :].bitcast(BF16)).then_inc(oht_ready, 1)

                def onehot_free(g, j):
                    wait(act, cand_summed, g * USES + (j - 1) * 8 if j >= 2 else (g - 1) * USES + G4 * R1 + (j + 1) * 8)

                def chunk_part(g, part):
                    m, c = (g - 1) * NC + part // 2, part // 2
                    for i in (range(6), range(6, PAIRS))[part % 2]:
                        act_pair(act, s4, m, c, i)
                    if part % 2:
                        act_functions(act, s4, m, c)

                def iteration(g):
                    q0 = g * ROUNDS
                    for j in range(G4):
                        if j + 1 < G4 and has_tiles(g):
                            onehot_free(g, j + 1)
                            copy_onehots(q0 + j + 1, (j + 1) % 2)
                        if has_pwl(g):
                            chunk_part(g, j)
                    if has_pwl(g):
                        chunk_part(g, 4)
                    if has_tiles(g):
                        act.wait_ge(bm_filled, g * FILLS + F_ROWS + 1)
                        act.copy(YO, BM[:, 0:YW]).then_inc(bm_read, 1)
                        act.wait_ge(bm_filled, g * FILLS + F_SLOTT + 1)
                        act.copy(slotT, BM[:, :]).then_inc(bm_read, 1)
                        onehot_free(g, 4)
                        copy_onehots(q0 + 4, 0)
                    if has_pwl(g):
                        chunk_part(g, 5)
                    if has_tiles(g):
                        onehot_free(g, 5)
                        copy_onehots(q0 + 5, 1)
                    if has_pwl(g):
                        chunk_part(g, 6)
                        chunk_part(g, 7)
                    if has_tiles(g):
                        if has_next(g):
                            onehot_free(g + 1, 0)
                            copy_onehots(q0 + ROUNDS, 0)
                        wait(act, bm_filled, g * FILLS - FILLS + F_XT + 1)
                        for j in range(G4):
                            t = g * G4 + j
                            act.activation(xna[:, j * P:(j + 1) * P], X[:, bass.ds(t * P, P)], ACT.Identity,
                                           bias=NMR[:, bass.ds(t, 1)], scale=RSTD[:, bass.ds(t, 1)]).then_inc(xna_ready, 1)
                        act.wait_ge(bm_filled, g * FILLS + F_XT + 1)
                        wait(act, s4.chunk_summed, g * NC)
                        act.copy(xT4, BM[:, :]).then_inc(bm_read, 1)
                        for c in range(NC):
                            act.wait_ge(bm_filled, g * FILLS + F_Z + c + 1)
                            wait(act, s4.stepped, ((g - 1) * NC + c + 1) * STEPS)
                            act.copy(Z[c], BM[:, :]).then_inc(bm_read, 1)

                copy_onehots(0, 0)
                all_groups(act, iteration)

            @block.vector
            def _(dve):
                def top8(src, dst, q, slot_):
                    dve.drain()
                    dve.max(dst, src)
                    dve.drain()
                    dve.max_index(index, dst, src)
                    dve.match_replace(src, dst, src, FAR)
                    dve.drain()
                    wait(dve, oh_turned, q - 1)
                    for k in range(8):
                        last = dve.tensor_scalar(OH[slot_][:, k * P:(k + 1) * P], colb[:, :], index[:, k:k + 1], None,
                                                 ALU.is_equal)
                    last.then_inc(oh_ready, 1)

                def select(g, j):
                    t = g * G4 + j
                    y = YE[:, j, 0:P]
                    wait(dve, bm_filled, (g - 1) * FILLS + F_ROWS + 1)
                    dve.tensor_scalar(y, X[:, bass.ds(t * P, P)], MEAN[:, bass.ds(t, 1)], RSTD[:, bass.ds(t, 1)],
                                      ALU.subtract, ALU.mult).then_inc(y_steps, 1)
                    dve.wait_ge(y_steps, t + 1)
                    dve.tensor_tensor(y, y, mwrow[:, :], ALU.add)
                    top8(y, top[j % 2], g * ROUNDS + j, j % 2)
                    dve.max(rest[:, 8 * j:8 * j + 8], y)

                def maximum(g, u, dst, bound, first=False):
                    dve.wait_ge(cand_summed, g * USES + u + 1)
                    if first:
                        dve.tensor_scalar(dst, PS[u % 3][:, :], bound, None, ALU.add).then_inc(cand_used, 1)
                    else:
                        dve.wait_ge(cand_used, g * USES + u)
                        dve.scalar_tensor_tensor(dst, PS[u % 3][:, :], bound, dst, ALU.add, ALU.max).then_inc(cand_used, 1)

                def steps(g, first, count):
                    if has_pwl(g):
                        for w in range(first, first + count):
                            dve_step(dve, s4, (g - 1) * NC + w // STEPS, w // STEPS, w % STEPS)

                def iteration(g):
                    if not has_tiles(g):
                        steps(g, 0, 20)
                        dve_finish(dve, s4, g - 2)
                        steps(g, 20, 4 * STEPS - 20)
                        dve_finish(dve, s4, g - 1)
                        return
                    for j in range(G4):
                        if j + 1 < G4:
                            select(g, j + 1)
                        wait(dve, bm_filled, g * FILLS)
                        for k in range(R1):
                            maximum(g, j * R1 + k, T[j], top[j % 2][:, k:k + 1], first=(k == 0))
                            steps(g, 9 * j + k, 1)
                        steps(g, 9 * j + 8, 1)
                        dve.wait_ge(cand_used, g * USES + (j + 1) * R1)
                        dve.tensor_reduce(YE[:, j, P + 1:P + 2], T[j], AX.X, ALU.min).then_inc(min_ready, 1)
                        if j == 2 and has_finish(g):
                            dve_finish(dve, s4, g - 2)
                    dve.wait_ge(min_ready, g * G4 + G4)
                    dve.tensor_tensor(opened, rest.rearrange("p (j k) -> p j k", j=G4)[:, :, 0], YE[:, :, P + 1],
                                      ALU.is_gt).then_inc(open_ready, 1)
                    dve.wait_ge(open_ready, g + 1)
                    dve.tensor_scalar(closed, opened, 1.0, -FAR, ALU.subtract, ALU.mult)
                    steps(g, 36, 2)
                    dve.wait_ge(bm_filled, g * FILLS + F_SLOT + 1)
                    dve.scalar_tensor_tensor(slot, BM[:, 0:G4], 1.0, opened, ALU.add, ALU.mult).then_inc(bm_read, 1)
                    dve.wait_ge(bm_read, g * FILLS + F_SLOT + 1)
                    dve.tensor_copy(PMALL[:, bass.ds(g * G4, G4)], slot)
                    for j in range(G4):
                        dve.tensor_scalar(slotm[j], coli[:, :], slot[:, j:j + 1], None, ALU.is_equal).then_inc(slotm_ready, 1)
                    steps(g, 38, 4)
                    dve.wait_ge(bm_read, g * FILLS + F_ROWS + 1)
                    dve.tensor_copy(taken, YO[:, P:P + 2])
                    for r in range(R2 // 8):
                        top8(YO[:, 0:P], topo[:, 8 * r:8 * r + 8], g * ROUNDS + G4 + r, r)
                    dve.max(resto, YO[:, 0:P])
                    dve.drain()
                    dve.scalar_tensor_tensor(OPEN[:, bass.ds(g, 1)], resto[:, 0:1], taken[:, 1:2], taken[:, 0:1],
                                             ALU.is_gt, ALU.mult)
                    if has_next(g):
                        select(g + 1, 0)
                    for k in range(R2):
                        maximum(g, G4 * R1 + k, TO, topo[:, k:k + 1], first=(k == 0))
                        steps(g, 42 + k, 1)
                    steps(g, 58, 6)
                    for j in range(G4):
                        maximum(g, G4 * R1 + R2 + j, T[j], closed[:, j:j + 1])
                        steps(g, 64 + 2 * j, 2)

                dve.memset(YE[:, :, P], 1.0).then_inc(ones_made, 1)
                dve.memset(padded, 0.0).then_inc(ones_made, 1)
                dve.wait_ge(ones_made, 2)
                select(0, 0)
                all_groups(dve, iteration)

        with nc.Block() as block:
            o_steps, o_sum = sem("o_steps"), sem("o_sum")

            @block.vector
            def _(dve):
                link = Chain(dve, o_steps)
                link(dve.tensor_scalar(S[0], PMALL[:, :], float(P), None, ALU.is_gt))
                link(dve.tensor_reduce(S[1][:, 0:1], S[0], AX.X, ALU.max))
                link(dve.tensor_reduce(S[1][:, 1:2], OPEN[:, :], AX.X, ALU.max))
                link(dve.tensor_tensor(S[2][:, 0:1], S[1][:, 0:1], S[1][:, 1:2], ALU.max))
                dve.wait_ge(o_sum, 1)
                link(dve.tensor_reduce(S[3][0:1, 0:1], PS[0][0:1, 0:P], AX.X, ALU.max))
                link(dve.tensor_scalar(flag2[0:1, 0:1], S[3][0:1, 0:1], 0.0, None, ALU.is_gt))

            @block.tensor
            def _(pe):
                pe.wait_ge(o_steps, 4)
                pe.matmul(PS[0][0:1, 0:P], S[2][:, 0:1], ident[:, :], start=True, stop=True).then_inc(o_sum, 1)

        s5 = Pwl("p5")
        xn4 = xna
        with nc.Block() as block:
            d_xn, d_turned, d_xT = sem("d_xn"), sem("d_turned"), sem("d_xT")
            z_set, d_sel, d_row, d_max = sem("z_set"), sem("d_sel"), sem("d_row"), sem("d_max")
            d_cnt = sem("d_cnt")

            def if_open(eng):
                return eng.If(eng.value_load(flag2[0:1, 0:1]) > 0)

            @block.sync
            def _(sp):
                with if_open(sp):
                    store_groups(sp, s5)

            @block.tensor
            def _(pe):
                def group(g):
                    pe.wait_ge(d_xn, g * 4 + 4)
                    for j in range(G4):
                        last = pe.transpose(PS[0][:, j * P:(j + 1) * P], xn4[:, j * P:(j + 1) * P], ident[:, :])
                    last.then_inc(d_turned, 1)
                    with pe.Fori(0, P // 2) as d:
                        for p in range(2):
                            n = g * P + d * 2 + p
                            pe.wait_ge(d_xT, g + 1)
                            pe.wait_ge(d_sel, n + 1)
                            pe.matmul(PS[1 + p][:, :], sel[p], xT4, start=True, stop=True).then_inc(d_row, 1)
                    for c in range(NC):
                        m = g * NC + c
                        pe_chunk(pe, s5, m, c)
                        if c:
                            pe_out(pe, s5, m - 1, c - 1, g)
                    pe_out(pe, s5, g * NC + NC - 1, NC - 1, g)

                with if_open(pe):
                    group(0)
                    with pe.Fori(1, NG) as g:
                        group(g)

            @block.scalar
            def _(act):
                def group(g):
                    act.wait_ge(d_turned, g + 1)
                    act.copy(xT4, PS[0][:, :]).then_inc(d_xT, 1)
                    act.wait_ge(d_max, (g * P + P) * NC + NC)
                    for c in range(NC):
                        for i in range(PAIRS):
                            act_pair(act, s5, g * NC + c, c, i)
                        act_functions(act, s5, g * NC + c, c)

                with if_open(act):
                    group(0)
                    with act.Fori(1, NG) as g:
                        group(g)

            @block.vector
            def _(dve):
                def group(g):
                    for j in range(G4):
                        normalise(dve, xn4[:, j * P:(j + 1) * P], g * G4 + j).then_inc(d_xn, 1)
                    dve.memset(dcount, -1.0).then_inc(z_set, 1)
                    for c in range(NC):
                        dve.memset(Z[c], LOWEST).then_inc(z_set, 1)
                    with dve.Fori(0, P // 2) as d:
                        for p in range(2):
                            n = g * P + d * 2 + p
                            dve.wait_ge(z_set, g * (NC + 1) + NC + 1)
                            dve.tensor_scalar(dcount, dcount, 1.0, None, ALU.add).then_inc(d_cnt, 1)
                            dve.wait_ge(d_cnt, n + 1)
                            dve.tensor_scalar(sel[p], pidx[:, :], dcount, None, ALU.is_equal).then_inc(d_sel, 1)
                        for p in range(2):
                            n = g * P + d * 2 + p
                            dve.wait_ge(d_row, n + 1)
                            for c in range(NC):
                                dve.wait_ge(d_max, n * NC + c + 1)
                                dve.scalar_tensor_tensor(Z[c], PS[1 + p][:, :], WtS[:, c, bass.ds(d * 2 + p, 1)], Z[c],
                                                         ALU.add, ALU.max).then_inc(d_max, 1)
                    for c in range(NC):
                        for n in range(STEPS):
                            dve_step(dve, s5, g * NC + c, c, n)
                    dve_finish(dve, s5, g)

                with if_open(dve):
                    dve.sem_inc(d_max, NC)
                    group(0)
                    with dve.Fori(1, NG) as g:
                        group(g)


_INS = ['x', 'adj', 'L0_gnn_W_msg', 'L0_gnn_W_upd', 'L0_gnn_bias', 'L0_ffn_Wr', 'L0_ffn_br', 'L0_ffn_W1', 'L0_ffn_b1',
        'L0_ffn_g1', 'L0_ffn_be1', 'L0_ffn_m1', 'L0_ffn_v1', 'L0_ffn_W2', 'L0_ffn_b2', 'L0_ffn_g2', 'L0_ffn_be2',
        'L0_ffn_m2', 'L0_ffn_v2', 'L0_ffn_Wo', 'L0_ffn_bo', 'L1_gnn_W_fwd', 'L1_gnn_W_bwd', 'L1_gnn_W_loop',
        'L1_gnn_Wg_fwd', 'L1_gnn_Wg_bwd', 'L1_gnn_Wg_loop', 'L1_gnn_b_fwd', 'L1_gnn_b_bwd', 'L1_gnn_b_loop',
        'L1_gnn_bg_fwd', 'L1_gnn_bg_bwd', 'L1_gnn_bg_loop', 'L1_ffn_Wt', 'L1_ffn_bt', 'L1_ffn_sl_cvx', 'L1_ffn_of_cvx',
        'L1_ffn_sl_ccv', 'L1_ffn_of_ccv', 'L1_ffn_alpha', 'L1_ffn_Wc', 'L1_ffn_bc', 'L1_ffn_Wg', 'L1_ffn_bg',
        'L1_ffn_Wd', 'L1_ffn_bd']


def kernel(**inputs):
    import numpy as _np
    import concourse.bacc as _bacc
    from concourse import mybir as _mybir
    from concourse.bass_utils import run_bass_kernel_spmd as _run

    nc = _bacc.Bacc("TRN2", target_bir_lowering=False, num_devices=1)
    arrays, args = {}, {}
    for name in _INS:
        arr = _np.ascontiguousarray(inputs[name])
        arrays[f"in_{name}_dram"] = arr
        args[name] = nc.dram_tensor(f"in_{name}_dram", arr.shape, _mybir.dt.from_np(arr.dtype), kind="ExternalInput").ap()
    out = nc.dram_tensor("out_0_dram", (NT, P, P), _mybir.dt.float32, kind="ExternalOutput").ap()
    build(nc, args, out)
    r = _run(nc, [arrays], core_ids=[0])
    return r.results[0]["out_0_dram"]
```

```python
from contextlib import ExitStack

import concourse.bass as bass
from concourse import mybir

ALU = mybir.AluOpType
ACT = mybir.ActivationFunctionType
AX = mybir.AxisListType
F32 = mybir.dt.float32
BF16 = mybir.dt.bfloat16
I32 = mybir.dt.int32
U32 = mybir.dt.uint32

P = 128
NT = 64
E = 8
NC = 4
NH = NC * P
G4 = 4
NG = NT // G4
GW = G4 * P
NL = 8
NREL = 39
LN_EPS = 1e-5
BN_EPS = 1e-3
LOWEST = -3.0e38
R1 = 8
R2 = 16
CB4 = 4
USES = G4 * R1 + R2 + G4
FILLS = 4
ROUNDS = G4 + R2 // 8
YW = P + 2
FAR = -1.0e30
BENDS = NL - 1
DVE_TERMS = BENDS + 1
PE_TERMS = BENDS - 1
STEPS = DVE_TERMS + 3
RING_D, RING_P = 4, 3


def wait(eng, sem, value):
    if not (isinstance(value, int) and value <= 0):
        eng.wait_ge(sem, value)


def build(nc, a, out):
    with ExitStack() as ctx:
        def sb(name, shape, dt=F32):
            return ctx.enter_context(nc.sbuf_tensor(name, shape, dt))

        def sem(name):
            return ctx.enter_context(nc.semaphore(name))

        X = sb("X", [P, NT * P])
        M1 = sb("M1", [P, NT * P], BF16)
        EX = sb("EX", [P, NT * P])
        STATS = sb("STATS", [P, NT, 6])
        MEAN = sb("MEAN", [P, NT])
        RSTD = sb("RSTD", [P, NT])
        FLG = sb("FLG", [P, NT])
        ident = sb("ident", [P, P])
        ones = sb("ones", [P, P])
        pidx = sb("pidx", [P, P])
        PAR = sb("PAR", [96, P])
        PT = sb("PT", [P, 96])
        WMU = sb("WMU", [P, 2 * P])
        Wr = sb("Wr", [P, E])
        brrow = sb("brrow", [1, E])
        W1 = sb("W1", [P, E, P])
        W2 = sb("W2", [P, E, P])
        Wo = sb("Wo", [P, E, P])
        bo = sb("bo", [E, P])
        WG = sb("WG", [P, 6, P])
        WHG = sb("WHG", [P, 3, 2, P])
        brows = sb("brows", [3, 2, GW], BF16)
        B4 = sb("B4", [P, 4 * P])
        WtS = sb("WtS", [P, NC, P])
        SL = sb("SL", [P, NC, 2 * NL])
        OF = sb("OF", [P, NC, 2 * NL])
        Wc = sb("Wc", [P, NH])
        Wg = sb("Wg", [P, NH])
        Wd = sb("Wd", [P, NC, P])
        bdrow = sb("bdrow", [1, G4 * P])
        sc1 = sb("sc1", [P, E])
        c1 = sb("c1", [P, E])
        nc2 = sb("nc2", [P, E])
        bgh = sb("bgh", [P, NC])
        CA = sb("CA", [P, NL, 2 * NC])
        CB = sb("CB", [P, NL, 2 * NC])
        BW = sb("BW", [P, BENDS, 2 * NC])
        BO = sb("BO", [P, BENDS, 2 * NC])
        A0 = sb("A0", [P, NC])
        K0 = sb("K0", [P, NC])
        Wdh = sb("Wdh", [P, NC, P])
        NMR = sb("NMR", [P, NT])
        WP = sb("WP", [P, 3, NH], BF16)
        mwrow = sb("mwrow", [P, P])
        coli = sb("coli", [P, P])
        colb = sb("colb", [P, P], BF16)
        identb = sb("identb", [P, P], BF16)
        onesb = sb("onesb", [P, P], BF16)
        tri = sb("tri", [P, P], BF16)
        PMALL = sb("PMALL", [P, NT])
        OPEN = sb("OPEN", [P, NG])
        flag2 = sb("flag2", [1, 2], I32)
        WB = sb("WB", [P, E, P])
        CW = sb("CW", [P, P])
        small = sb("small", [P, 16, NT])
        flag = sb("flag", [1, 2], I32)
        WORK = 13312
        work = sb("work", [P, WORK])

        PS = [ctx.enter_context(nc.psum_tensor(f"ps{i}", [P, 512], F32)) for i in range(8)]

        class Carve:
            def __init__(self):
                self.at = 0

            def __call__(self, n):
                v = work[:, self.at:self.at + n]
                self.at += n
                assert self.at <= WORK
                return v

        bt_at, al_at, bc_at, bg_at = 80, 84, 88, 92

        params_loaded, weights_loaded = sem("params_loaded"), sem("weights_loaded")
        x_loaded = [sem(f"x_loaded{i}") for i in range(4)]
        pool_made, pe_setup, act_setup, dve_setup = sem("pool_made"), sem("pe_setup"), sem("act_setup"), sem("dve_setup")
        carve = Carve()
        bc_scale = carve(E * P)
        WgT = carve(3 * P)
        wtT, wres = carve(NH), carve(NH)
        mw_spread = carve(P)
        b3, b3sum = carve(4 * P)[0:3, :], carve(4 * P)[0:3, :]
        b3p = [carve(2 * P).bitcast(BF16)[0:3, :] for _ in range(3)]
        third = carve(3)[0:3, :]
        names = ["b1", "g1", "be1", "m1", "v1", "b2", "g2", "be2", "m2", "v2"]
        loads = [(WMU[:, 0:P], a["L0_gnn_W_msg"]), (WMU[:, P:2 * P], a["L0_gnn_W_upd"]),
                 (Wr[:, :], a["L0_ffn_Wr"]), (brrow[:, :], a["L0_ffn_br"].rearrange("(o d) -> o d", o=1)),
                 (W1[:, :, :], a["L0_ffn_W1"].rearrange("e d h -> d e h")),
                 (W2[:, :, :], a["L0_ffn_W2"].rearrange("e d h -> d e h")),
                 (Wo[:, :, :], a["L0_ffn_Wo"].rearrange("e d h -> d e h")),
                 (bo[:, :], a["L0_ffn_bo"]),
                 (WG[:, 0, :], a["L1_gnn_W_fwd"]), (WG[:, 1, :], a["L1_gnn_W_bwd"]), (WG[:, 2, :], a["L1_gnn_W_loop"]),
                 (WG[:, 3, :], a["L1_gnn_Wg_fwd"]), (WG[:, 4, :], a["L1_gnn_Wg_bwd"]), (WG[:, 5, :], a["L1_gnn_Wg_loop"]),
                 (WtS[:, :, :], a["L1_ffn_Wt"].rearrange("(c f) d -> f c d", c=NC)),
                 (SL[:, :, 0:NL], a["L1_ffn_sl_cvx"].rearrange("(c f) l -> f c l", c=NC)),
                 (SL[:, :, NL:2 * NL], a["L1_ffn_sl_ccv"].rearrange("(c f) l -> f c l", c=NC)),
                 (OF[:, :, 0:NL], a["L1_ffn_of_cvx"].rearrange("(c f) l -> f c l", c=NC)),
                 (OF[:, :, NL:2 * NL], a["L1_ffn_of_ccv"].rearrange("(c f) l -> f c l", c=NC)),
                 (Wc[:, :], a["L1_ffn_Wc"]), (Wg[:, :], a["L1_ffn_Wg"]),
                 (Wd[:, :, :], a["L1_ffn_Wd"].rearrange("(c f) d -> f c d", c=NC))]
        loads += [(bdrow[:, j * P:(j + 1) * P], a["L1_ffn_bd"].rearrange("(o d) -> o d", o=1)) for j in range(G4)]
        loads += [(b3[i:i + 1, (1 + j) * P:(2 + j) * P], a[n].rearrange("(o d) -> o d", o=1) if j == 0 else a[n])
                  for i in range(3) for j, n in enumerate(["L0_gnn_bias", "L1_gnn_b_loop", "L1_gnn_bg_loop"])]
        relation_rows = ["L1_gnn_b_fwd", "L1_gnn_bg_fwd", "L1_gnn_b_bwd", "L1_gnn_bg_bwd"]

        class Chain:
            def __init__(self, eng, sem, base=0):
                self.eng, self.sem, self.base, self.n = eng, sem, base, 0

            def __call__(self, ins):
                ins.then_inc(self.sem, 1)
                self.n += 1
                self.eng.wait_ge(self.sem, self.base + self.n)

        def rsqrt_after_sqrt(link, dve, v, root, r, t):
            link(dve.reciprocal(r, root))
            link(dve.tensor_tensor(t, r, r, ALU.mult))
            link(dve.tensor_tensor(t, t, v, ALU.mult))
            link(dve.tensor_scalar(t, t, -0.5, 1.5, ALU.mult, ALU.add))
            link(dve.tensor_tensor(r, r, t, ALU.mult))

        S = [small[:, i, :] for i in range(16)]

        def variance(link, dve):
            ev, od = STATS[:, :, 1], STATS[:, :, 4]
            link(dve.tensor_tensor(S[1], ev, od, ALU.add))
            link(dve.tensor_scalar(MEAN[:, :], S[1], 0.5, None, ALU.mult))
            link(dve.tensor_tensor(S[1], ev, od, ALU.subtract))
            link(dve.tensor_tensor(S[1], S[1], S[1], ALU.mult))
            link(dve.tensor_tensor(S[2], STATS[:, :, 2], STATS[:, :, 5], ALU.add))
            link(dve.tensor_scalar(S[2], S[2], 1.0 / P, LN_EPS, ALU.mult, ALU.add))
            link(dve.scalar_tensor_tensor(S[0], S[1], 0.25, S[2], ALU.mult, ALU.add))

        def layer_norm_scales(name):
            steps, rooted = sem(name + "_dve"), sem(name + "_root")
            with nc.Block() as block:
                @block.vector
                def _(dve):
                    link = Chain(dve, steps)
                    variance(link, dve)
                    dve.wait_ge(rooted, 1)
                    rsqrt_after_sqrt(link, dve, S[0], S[3], RSTD[:, :], S[1])
                    link(dve.scalar_tensor_tensor(NMR[:, :], MEAN[:, :], -1.0, RSTD[:, :], ALU.mult, ALU.mult))

                @block.scalar
                def _(act):
                    act.wait_ge(steps, 7)
                    act.activation(S[3], S[0], ACT.Sqrt).then_inc(rooted, 1)

        with nc.Block() as block:
            @block.sync
            def _(sp):
                for i, n in enumerate(names):
                    sp.dma_start(PAR[8 * i:8 * i + 8, :], a["L0_ffn_" + n]).then_inc(params_loaded, 16)
                for at, n in ((bt_at, "bt"), (al_at, "alpha"), (bc_at, "bc"), (bg_at, "bg")):
                    sp.dma_start(PAR[at:at + NC, :], a["L1_ffn_" + n].rearrange("(c f) -> c f", c=NC)).then_inc(params_loaded, 16)
                for dst, src in loads:
                    sp.dma_start(dst, src).then_inc(weights_loaded, 16)
                sp.wait_ge(pool_made, 5)
                for i, n in enumerate(relation_rows):
                    sp.dma_start(B4[0:NREL, i * P:(i + 1) * P], a[n]).then_inc(weights_loaded, 16)

            N_WEIGHTS = 16 * (len(loads) + len(relation_rows))

            @block.scalar
            def _(act):
                for i in range(4):
                    n = NT // 4
                    act.dma_start(X[:, i * n * P:(i + 1) * n * P].rearrange("p (t d) -> p t d", d=P),
                                  a["x"][i * n:(i + 1) * n].rearrange("t p d -> p t d")).then_inc(x_loaded[i], 16)
                act.wait_ge(pe_setup, 1)
                act.copy(PT[:, :], PS[0][:, 0:96]).then_inc(act_setup, 1)
                act.wait_ge(dve_setup, 2)
                act.activation(S[3][:, 0:16], S[0][:, 0:16], ACT.Sqrt).then_inc(act_setup, 1)
                act.activation(S[4][:, 0:NC], PT[:, al_at:al_at + NC], ACT.Sigmoid).then_inc(act_setup, 1)
                act.wait_ge(pe_setup, 3)
                act.copy(WHG[:, :, 0, :], PS[2][:, 0:3 * P].rearrange("p (i d) -> p i d", i=3)).then_inc(act_setup, 1)
                act.copy(WgT, PS[3][:, 0:3 * P]).then_inc(act_setup, 1)
                act.wait_ge(pe_setup, 4)
                act.copy(WHG[:, :, 1, :], PS[4][:, 0:3 * P].rearrange("p (i d) -> p i d", i=3)).then_inc(act_setup, 1)

            @block.gpsimd
            def _(pool):
                pool.memset(ones[:, :], 1.0).then_inc(pool_made, 1)
                pool.memset(ident[:, :], 0.0).then_inc(pool_made, 1)
                pool.wait_ge(pool_made, 2)
                pool.affine_select(out=ident[:, :], in_=ident[:, :], compare_op=ALU.not_equal, fill=1.0, base=0,
                                   pattern=[[-1, P]], channel_multiplier=1).then_inc(pool_made, 1)
                pool.iota(pidx[:, :], [[0, P]], base=0, channel_multiplier=1,
                          allow_small_or_imprecise_dtypes=True).then_inc(pool_made, 1)
                pool.memset(B4[:, :], 0.0).then_inc(pool_made, 1)
                pool.memset(b3[:, 0:P], 0.0).then_inc(pool_made, 1)
                pool.iota(coli[:, :], [[1, P]], base=1, channel_multiplier=0,
                          allow_small_or_imprecise_dtypes=True).then_inc(pool_made, 1)
                pool.memset(EX[:, :], 0.0).then_inc(pool_made, 1)

            @block.tensor
            def _(pe):
                pe.wait_ge(pool_made, 4)
                pe.wait_ge(params_loaded, 16 * 14)
                pe.transpose(PS[0][:, 0:96], PAR[:, :], ident[0:96, 0:96]).then_inc(pe_setup, 1)
                pe.wait_ge(weights_loaded, N_WEIGHTS)
                for i in range(6):
                    bank = PS[2 + i // 3]
                    last = pe.transpose(bank[:, (i % 3) * P:(i % 3 + 1) * P], WG[:, i, :], ident[:, :])
                    if i % 3 == 2:
                        last.then_inc(pe_setup, 1)
                pe.wait_ge(act_setup, 5)
                for i in range(3):
                    last = pe.matmul(PS[4][:, i * P:(i + 1) * P], WG[:, i, :], WgT[:, i * P:(i + 1) * P],
                                     start=True, stop=True)
                last.then_inc(pe_setup, 1)
                for c in range(NC):
                    last = pe.transpose(PS[1][:, c * P:(c + 1) * P], WtS[:, c, :], ident[:, :])
                last.then_inc(pe_setup, 1)
                pe.wait_ge(dve_setup, 3)
                for e in range(E):
                    last = pe.matmul(PS[5 + e // 4][:, (e % 4) * P:(e % 4 + 1) * P],
                                     bc_scale[:, e * P:(e + 1) * P], ident[:, :], start=True, stop=True)
                last.then_inc(pe_setup, 1)
                pe.wait_ge(dve_setup, 4)
                pe.matmul(PS[7][:, 0:P], mw_spread, ident[:, :], start=True, stop=True).then_inc(pe_setup, 1)

            dve_chain, x_stats = sem("dve_chain"), sem("x_stats")

            @block.vector
            def _(dve):
                link = Chain(dve, dve_chain)

                def col(name, n=E):
                    at = 8 * names.index(name)
                    return PT[:, at:at + n]

                for i in range(4):
                    dve.wait_ge(x_loaded[i], 16)
                    with dve.Fori(i * NT // 32, (i + 1) * NT // 32) as h:
                        for j in range(8):
                            t = h * 8 + j
                            dve.bn_stats(STATS[:, bass.ds(t, 1), :].rearrange("p o s -> p (o s)"),
                                         X[:, bass.ds(t * P, P)]).then_inc(x_stats, 1)
                dve.wait_ge(act_setup, 1)
                dve.tensor_scalar(S[0][:, 0:8], col("v1"), BN_EPS, None, ALU.add).then_inc(dve_setup, 1)
                dve.tensor_scalar(S[0][:, 8:16], col("v2"), BN_EPS, None, ALU.add).then_inc(dve_setup, 1)
                dve.wait_ge(act_setup, 3)
                dve.wait_ge(dve_setup, 2)
                rsqrt_after_sqrt(link, dve, S[0][:, 0:16], S[3][:, 0:16], S[5][:, 0:16], S[1][:, 0:16])
                link(dve.tensor_tensor(sc1[:, :], col("g1"), S[5][:, 0:8], ALU.mult))
                link(dve.tensor_tensor(c1[:, :], col("b1"), col("m1"), ALU.subtract))
                link(dve.tensor_tensor(c1[:, :], c1[:, :], sc1[:, :], ALU.mult))
                link(dve.tensor_tensor(c1[:, :], c1[:, :], col("be1"), ALU.add))
                sc2 = S[6][:, 0:8]
                link(dve.tensor_tensor(sc2, col("g2"), S[5][:, 8:16], ALU.mult))
                link(dve.tensor_tensor(nc2[:, :], col("m2"), col("b2"), ALU.subtract))
                link(dve.tensor_tensor(nc2[:, :], nc2[:, :], sc2, ALU.mult))
                link(dve.tensor_tensor(nc2[:, :], nc2[:, :], col("be2"), ALU.subtract))
                dve.tensor_copy(bc_scale.rearrange("p (e k) -> p e k", e=E),
                                sc2.unsqueeze(2).to_broadcast([P, E, P])).then_inc(dve_setup, 1)
                link(dve.tensor_scalar(S[7][:, 0:NC], S[4][:, 0:NC], -1.0, 1.0, ALU.mult, ALU.add))
                link(dve.tensor_scalar(bgh[:, :], PT[:, bg_at:bg_at + NC], 0.5, None, ALU.mult))
                dve.wait_ge(weights_loaded, N_WEIGHTS)
                for c in range(NC):
                    link(dve.scalar_tensor_tensor(OF[:, c, :], SL[:, c, :], PT[:, bt_at + c:bt_at + c + 1], OF[:, c, :],
                                                  ALU.mult, ALU.add))
                    for t in (SL, OF):
                        link(dve.tensor_scalar(t[:, c, 0:NL], t[:, c, 0:NL], S[4][:, c:c + 1], None, ALU.mult))
                        link(dve.tensor_scalar(t[:, c, NL:2 * NL], t[:, c, NL:2 * NL], S[7][:, c:c + 1], None, ALU.mult))
                for t in (SL, OF):
                    link(dve.tensor_scalar(t[:, :, NL:2 * NL], t[:, :, NL:2 * NL], -1.0, None, ALU.mult))
                link(dve.tensor_scalar(Wdh[:, :, :], Wd[:, :, :], 0.5, None, ALU.mult))
                dve.wait_ge(pe_setup, 5)
                link(dve.tensor_copy(wtT, PS[1][:, :]))
                mw = S[8][:, 0:1]
                link(dve.tensor_reduce(mw, wtT, AX.X, ALU.max))
                dve.tensor_copy(mw_spread, mw.to_broadcast([P, P])).then_inc(dve_setup, 1)
                link(dve.tensor_scalar(wtT, wtT, mw, None, ALU.subtract))
                link(dve.tensor_copy(WP[:, 0, :], wtT))
                link(dve.tensor_tensor(wres, wtT, WP[:, 0, :], ALU.subtract))
                link(dve.tensor_copy(WP[:, 1, :], wres))
                link(dve.tensor_tensor(wres, wres, WP[:, 1, :], ALU.subtract))
                link(dve.tensor_copy(WP[:, 2, :], wres))
                dve.wait_ge(pool_made, 7)
                link(dve.tensor_copy(identb[:, :], ident[:, :]))
                link(dve.tensor_copy(onesb[:, :], ones[:, :]))
                link(dve.tensor_scalar(colb[:, :], coli[:, :], 1.0, None, ALU.subtract))
                link(dve.tensor_tensor(tri[:, :], pidx[:, :], colb[:, :], ALU.is_lt))
                dve.wait_ge(pe_setup, 7)
                link(dve.tensor_copy(mwrow[:, :], PS[7][:, 0:P]))
                for h in range(2):
                    w = W2[:, 4 * h:4 * h + 4, :].rearrange("p e k -> p (e k)")
                    link(dve.tensor_tensor(w, PS[5 + h][:, :], w, ALU.mult))
                for i in range(3):
                    link(dve.tensor_scalar(third[:, i:i + 1], pidx[0:3, 0:1], float(i), None, ALU.is_equal))
                for i in range(3):
                    link(dve.tensor_copy(b3p[i], b3))
                    if i < 2:
                        link(dve.tensor_tensor(b3, b3, b3p[i], ALU.subtract))
                link(dve.tensor_scalar(b3sum, b3p[0], third[:, 0:1], None, ALU.mult))
                link(dve.scalar_tensor_tensor(b3sum, b3p[1], third[:, 1:2], b3sum, ALU.mult, ALU.add))
                for i in range(2):
                    link(dve.scalar_tensor_tensor(brows[:, :, 2 * i * P:2 * (i + 1) * P],
                                                  b3p[2].rearrange("p (w d) -> p w d", w=2), third[:, 2:3],
                                                  b3sum.rearrange("p (w d) -> p w d", w=2), ALU.mult, ALU.add))

        layer_norm_scales("ln1")

        def normalise(dve, dst, t):
            return dve.tensor_scalar(dst, X[:, bass.ds(t * P, P)], MEAN[:, bass.ds(t, 1)], RSTD[:, bass.ds(t, 1)],
                                     ALU.subtract, ALU.mult)

        def tile_stats(dve, t):
            return dve.bn_stats(STATS[:, bass.ds(t, 1), :].rearrange("p o s -> p (o s)"), X[:, bass.ds(t * P, P)])

        def exists(g):
            return not isinstance(g, int) or 0 <= g < NG

        def pipeline(eng, body):
            for g in range(-2, 2):
                body(g, g % 2)
            with eng.Fori(1, NG // 2 - 1) as i:
                body(i * 2, 0)
                body(i * 2 + 1, 1)
            for g in range(NG - 2, NG + 1):
                body(g, g % 2)

        def norms(act, g, xn, turned, ready):
            wait(act, turned, g - 1)
            for j in range(G4):
                t = g * G4 + j
                last = act.activation(xn[:, j * P:(j + 1) * P], X[:, bass.ds(t * P, P)], ACT.Identity,
                                      bias=NMR[:, bass.ds(t, 1)], scale=RSTD[:, bass.ds(t, 1)])
            last.then_inc(ready, 1)

        def per_tile(v):
            return v.rearrange("p (t d) -> p t d", t=G4)

        carve = Carve()
        adj_i = [carve(GW).bitcast(I32) for _ in range(2)]
        adj_f = [carve(GW) for _ in range(2)]
        xn = [carve(GW) for _ in range(2)]
        xT = [carve(GW) for _ in range(2)]
        hu = [carve(2 * GW) for _ in range(2)]
        tmp = [carve(GW) for _ in range(2)]
        deg = [carve(3 * G4) for _ in range(2)]
        with nc.Block() as block:
            adj_loaded = [sem("adj_loaded0"), sem("adj_loaded1")]
            adj_cast, adj_masked = sem("adj_cast"), sem("adj_masked")
            xn_ready, xn_turned, xT_ready = sem("p1_xn_ready"), sem("p1_xn_turned"), sem("p1_xT_ready")
            hu_summed, hu_ready, msg_summed, msg_used = sem("hu_summed"), sem("hu_ready"), sem("msg_summed"), sem("msg_used")
            deg_steps, added, x1_ready = sem("deg_steps"), sem("p1_added"), sem("x1_ready")
            BTURN, BDEG = PS[0], PS[1]
            BHU, BMSG = [PS[2:4], PS[4:6]], PS[6:8]

            @block.sync
            def _(sp):
                for p in range(2):
                    sp.dma_start(per_tile(adj_i[p]), a["adj"][p * G4:(p + 1) * G4].rearrange("t p j -> p t j")).then_inc(adj_loaded[p], 16)
                with sp.Fori(0, NG // 2 - 1) as i:
                    for p in range(2):
                        g = i * 2 + p
                        sp.wait_ge(adj_cast, g + 1)
                        sp.wait_ge(adj_masked, g + 1)
                        sp.dma_start(per_tile(adj_i[p]), a["adj"][bass.ds((g + 2) * G4, G4)].rearrange("t p j -> p t j")).then_inc(adj_loaded[p], 16)

            @block.tensor
            def _(pe):
                def turn(g, p):
                    pe.wait_ge(xn_ready, g + 1)
                    wait(pe, xT_ready, g)
                    for j in range(G4):
                        last = pe.transpose(BTURN[:, j * P:(j + 1) * P], xn[p][:, j * P:(j + 1) * P], ident[:, :])
                    last.then_inc(xn_turned, 1)

                def project(g, p):
                    pe.wait_ge(xT_ready, g + 1)
                    wait(pe, hu_ready, g * 2 - 2)
                    for h in range(2):
                        pe.matmul(BHU[p][h][:, :], onesb[0:3, :], brows[:, 0, :], start=True, stop=False, skip_group_check=True)
                        for j in range(2):
                            t = 2 * h + j
                            last = pe.matmul(BHU[p][h][:, 2 * j * P:2 * (j + 1) * P], xT[p][:, t * P:(t + 1) * P], WMU[:, :],
                                             start=False, stop=True, skip_group_check=True)
                        last.then_inc(hu_summed, 1)

                def gather(g, p):
                    pe.wait_ge(hu_ready, g * 2 + 2)
                    pe.wait_ge(adj_cast, g + 1)
                    wait(pe, msg_used, g - 1)
                    wait(pe, deg_steps, g * 3)
                    for j in range(G4):
                        at = adj_f[p][:, j * P:(j + 1) * P]
                        pe.matmul(BDEG[:, j:j + 1], at, ones[:, 0:1], start=True, stop=True)
                        last = pe.matmul(BMSG[p][:, j * P:(j + 1) * P], at, hu[p][:, 2 * j * P:(2 * j + 1) * P],
                                         start=True, stop=True)
                    last.then_inc(msg_summed, 1)

                def body(g, p):
                    if exists(g + 1):
                        turn(g + 1, 1 - p)
                    if exists(g):
                        project(g, p)
                    if exists(g - 1):
                        gather(g - 1, 1 - p)

                pipeline(pe, body)

            @block.scalar
            def _(act):
                def body(g, p):
                    if exists(g + 1):
                        act.wait_ge(xn_turned, g + 2)
                        wait(act, hu_summed, g * 2)
                        act.copy(xT[1 - p], BTURN[:, :]).then_inc(xT_ready, 1)
                    if exists(g + 2):
                        norms(act, g + 2, xn[p], xn_turned, xn_ready)
                    if exists(g):
                        if isinstance(g, int):
                            act.wait_ge(adj_loaded[p], g // 2 * 16 + 16)
                        else:
                            act.wait_ge(adj_loaded[p], (g - p) * 8 + 16)
                        wait(act, msg_summed, g - 1)
                        act.copy(adj_f[p], adj_i[p]).then_inc(adj_cast, 1)
                        for h in range(2):
                            act.wait_ge(hu_summed, g * 2 + h + 1)
                            wait(act, msg_used, g - 1)
                            act.copy(hu[p][:, h * GW:(h + 1) * GW], BHU[p][h][:, :]).then_inc(hu_ready, 1)

                pipeline(act, body)

            @block.vector
            def _(dve):
                def masks(g, p):
                    if isinstance(g, int):
                        dve.wait_ge(adj_loaded[p], g // 2 * 16 + 16)
                    else:
                        dve.wait_ge(adj_loaded[p], (g - p) * 8 + 16)
                    dve.tensor_scalar(M1[:, bass.ds(g * GW, GW)], adj_i[p], 1.0, None, ALU.is_equal)
                    dve.tensor_reduce(FLG[:, bass.ds(g * G4, G4)], per_tile(adj_i[p]), AX.X, ALU.max).then_inc(adj_masked, 1)

                def back(g, p):
                    m, n = BMSG[p], BDEG[:, 0:G4]
                    d = [deg[p][:, i * G4:(i + 1) * G4] for i in range(3)]
                    dve.wait_ge(msg_summed, g + 1)
                    dve.tensor_scalar(d[0], n, 1.0, None, ALU.max).then_inc(deg_steps, 1)
                    dve.wait_ge(deg_steps, g * 3 + 1)
                    dve.reciprocal(d[1], d[0]).then_inc(deg_steps, 1)
                    dve.wait_ge(deg_steps, g * 3 + 2)
                    dve.scalar_tensor_tensor(d[2], n, 0.0, d[1], ALU.is_gt, ALU.mult).then_inc(deg_steps, 1)
                    dve.wait_ge(deg_steps, g * 3 + 3)
                    for j in range(G4):
                        last = dve.scalar_tensor_tensor(tmp[p][:, j * P:(j + 1) * P], m[:, j * P:(j + 1) * P], d[2][:, j:j + 1],
                                                        hu[p][:, (2 * j + 1) * P:(2 * j + 2) * P], ALU.mult, ALU.add)
                    last.then_inc(msg_used, 1)
                    x = X[:, bass.ds(g * GW, GW)]
                    dve.wait_ge(msg_used, g + 1)
                    dve.scalar_tensor_tensor(x, tmp[p], 0.0, x, ALU.max, ALU.add).then_inc(added, 1)

                def stats(g):
                    dve.wait_ge(added, g + 1)
                    for j in range(G4):
                        last = tile_stats(dve, g * G4 + j)
                    last.then_inc(x1_ready, 1)

                def body(g, p):
                    if exists(g):
                        masks(g, p)
                    if exists(g - 1):
                        back(g - 1, 1 - p)
                        stats(g - 1)

                pipeline(dve, body)

        layer_norm_scales("ln2")

        carve = Carve()
        feat = [carve(P) for _ in range(4)]
        featT = carve(P)
        route = carve(64)
        spread = carve(E * P)
        c2diag = carve(E * E)
        wT = carve(P)
        C8 = carve(P)
        with nc.Block() as block:
            f_steps, f_sum = sem("f_steps"), [sem(f"f_sum{p}") for p in range(4)]
            r_pe, r_act, r_dve = sem("r_pe"), sem("r_act"), sem("r_dve")

            @block.vector
            def _(dve):
                link = Chain(dve, f_steps)
                for p in range(4):
                    dve.memset(feat[p], 0.0).then_inc(f_sum[p], 1)
                with dve.Fori(0, NT // 8) as i:
                    for j in range(8):
                        t, p = i * 8 + j, j % 4
                        dve.wait_ge(f_sum[p], i * 2 + j // 4 + 1)
                        dve.scalar_tensor_tensor(feat[p], X[:, bass.ds(t * P, P)], RSTD[:, bass.ds(t, 1)], feat[p],
                                                 ALU.mult, ALU.add).then_inc(f_sum[p], 1)
                for p in range(4):
                    dve.wait_ge(f_sum[p], NT // 4 + 1)
                link(dve.tensor_tensor(S[1], MEAN[:, :], RSTD[:, :], ALU.mult))
                link(dve.tensor_reduce(S[2][:, 0:1], S[1], AX.X, ALU.add))
                dve.tensor_tensor(feat[2], feat[2], feat[3], ALU.add).then_inc(f_sum[2], 1)
                link(dve.tensor_tensor(feat[0], feat[0], feat[1], ALU.add))
                dve.wait_ge(f_sum[2], NT // 4 + 2)
                link(dve.tensor_tensor(feat[0], feat[0], feat[2], ALU.add))
                link(dve.tensor_scalar(feat[0], feat[0], S[2][:, 0:1], 1.0 / NT, ALU.subtract, ALU.mult))
                dve.sem_inc(r_dve, 1)
                dve.wait_ge(r_pe, 2)
                logits, shifted, ex, w = (route[:, 8 * i:8 * i + 8] for i in range(4))
                link(dve.tensor_copy(logits, PS[1][:, 0:E]))
                link(dve.tensor_reduce(route[:, 40:41], logits, AX.X, ALU.max))
                link(dve.tensor_scalar(shifted, logits, route[:, 40:41], None, ALU.subtract))
                dve.sem_inc(r_dve, 1)
                dve.wait_ge(r_act, 2)
                link(dve.reciprocal(route[:, 42:43], route[:, 41:42]))
                link(dve.tensor_scalar(w, ex, route[:, 42:43], None, ALU.mult))
                link(dve.tensor_copy(spread.rearrange("p (e k) -> p e k", e=E), w.unsqueeze(2).to_broadcast([P, E, P])))
                link(dve.memset(c2diag, 0.0))
                link(dve.tensor_scalar(c2diag[:, 0:E * E:E + 1], nc2[:, :], -1.0, None, ALU.mult))
                dve.sem_inc(r_dve, 1)
                dve.wait_ge(r_pe, 5)
                for h in range(2):
                    link(dve.tensor_copy(WB[:, 4 * h:4 * h + 4, :].rearrange("p e k -> p (e k)"), PS[2 + h][:, :]))
                dve.wait_ge(r_pe, 6)
                link(dve.tensor_copy(CW[:, :], PS[6][:, 0:P]))
                link(dve.tensor_reduce(S[1][:, 0:1], FLG[:, :], AX.X, ALU.max))
                dve.sem_inc(r_dve, 1)
                dve.wait_ge(r_pe, 7)
                link(dve.tensor_reduce(S[2][0:1, 0:1], PS[7][0:1, 0:P], AX.X, ALU.max))
                link(dve.tensor_scalar(flag[0:1, 0:1], S[2][0:1, 0:1], 2.0, None, ALU.is_ge))

            @block.scalar
            def _(act):
                act.wait_ge(r_pe, 1)
                act.copy(featT, PS[0][:, 0:P]).then_inc(r_act, 1)
                act.wait_ge(r_dve, 2)
                act.activation(route[:, 16:24], route[:, 8:16], ACT.Exp, accum_out=route[:, 41:42]).then_inc(r_act, 1)
                act.wait_ge(r_pe, 3)
                act.copy(wT[0:E, :], PS[4][0:E, 0:P]).then_inc(r_act, 1)
                act.wait_ge(r_pe, 4)
                act.copy(C8[0:E, :], PS[5][0:E, 0:P]).then_inc(r_act, 1)

            @block.tensor
            def _(pe):
                pe.wait_ge(r_dve, 1)
                pe.transpose(PS[0][:, 0:P], feat[0], ident[:, :]).then_inc(r_pe, 1)
                pe.wait_ge(r_act, 1)
                pe.matmul(PS[1][:, 0:E], ones[0:1, :], brrow[:, :], start=True, stop=False)
                pe.matmul(PS[1][:, 0:E], featT, Wr[:, :], start=False, stop=True).then_inc(r_pe, 1)
                pe.wait_ge(r_dve, 3)
                pe.transpose(PS[4][0:E, 0:P], route[:, 24:32], ident[:, :]).then_inc(r_pe, 1)
                pe.matmul(PS[5][0:E, 0:P], ident[0:E, 0:E], bo[:, :], start=True, stop=False)
                for e in range(E):
                    last = pe.matmul(PS[5][0:E, 0:P], c2diag[:, e * E:(e + 1) * E], Wo[:, e, :], start=False, stop=(e == E - 1))
                last.then_inc(r_pe, 1)
                for e in range(E):
                    last = pe.matmul(PS[2 + e // 4][:, (e % 4) * P:(e % 4 + 1) * P], spread[:, e * P:(e + 1) * P], ident[:, :],
                                     start=True, stop=True)
                last.then_inc(r_pe, 1)
                pe.wait_ge(r_act, 4)
                pe.matmul(PS[6][:, 0:P], wT[0:E, :], C8[0:E, :], start=True, stop=True).then_inc(r_pe, 1)
                pe.wait_ge(r_dve, 4)
                pe.matmul(PS[7][0:1, 0:P], S[1][:, 0:1], ident[:, :], start=True, stop=True).then_inc(r_pe, 1)

        carve = Carve()
        xn4 = [carve(GW) for _ in range(2)]
        xT4 = [carve(GW) for _ in range(2)]
        h1 = [carve(GW) for _ in range(2)]
        h2 = [carve(GW) for _ in range(2)]
        e_da, e_db, e_far, e_u, e_eq, e_m = (carve(2 * NC * NL).rearrange("p (c l) -> p c l", l=NL) for _ in range(6))
        e_best = carve(2 * NC)
        sl = SL[:, :, :].rearrange("p c (s l) -> p (c s) l", s=2)
        of = OF[:, :, :].rearrange("p c (s l) -> p (c s) l", s=2)
        BEND_LINKS, FIRST_LINKS = 16, 5

        def per_line(v):
            return v.unsqueeze(2).to_broadcast([P, 2 * NC, NL])

        def piece(table, n):
            return table[:, bass.ds(n, 1), :].rearrange("p o c -> p (o c)")

        def largest(dve, link, dst, lines):
            dve.tensor_scalar(e_far, e_eq, 1.0, -FAR, ALU.subtract, ALU.mult)
            link(dve.tensor_tensor(e_m, lines, e_eq, ALU.mult))
            link(dve.tensor_tensor(e_m, e_m, e_far, ALU.add))
            link(dve.tensor_reduce(dst, e_m, AX.X, ALU.max))

        def highest(dve, link, n):
            link(dve.tensor_tensor(e_eq, sl, per_line(piece(CA, n)), ALU.is_equal))
            largest(dve, link, piece(CB, n), of)

        def first_piece(dve, link):
            link(dve.tensor_reduce(piece(CA, 0), sl, AX.X, ALU.min))
            highest(dve, link, 0)
            assert link.n == FIRST_LINKS

        def next_piece(dve, link, n, part):
            if part == 0:
                dve.tensor_tensor(e_db, of, per_line(piece(CB, n - 1)), ALU.subtract)
                link(dve.tensor_tensor(e_da, sl, per_line(piece(CA, n - 1)), ALU.subtract))
                dve.tensor_scalar(e_far, e_da, 0.0, -1e38, ALU.is_le, ALU.mult)
                link(dve.tensor_scalar(e_u, e_da, 1e-30, None, ALU.max))
                link(dve.reciprocal(e_u, e_u))
                link(dve.tensor_tensor(e_u, e_u, e_db, ALU.mult))
                link(dve.tensor_tensor(e_u, e_u, e_far, ALU.add))
                link(dve.tensor_reduce(e_best, e_u, AX.X, ALU.max))
            elif part == 1:
                link(dve.tensor_scalar(e_best, e_best, -1e37, None, ALU.max))
                link(dve.tensor_tensor(e_eq, e_u, per_line(e_best), ALU.is_ge))
                largest(dve, link, piece(CA, n), sl)
                link(dve.tensor_tensor(piece(CA, n), piece(CA, n), piece(CA, n - 1), ALU.max))
            else:
                highest(dve, link, n)
                assert link.n == BEND_LINKS

        def bends_of_pieces(dve, link):
            link(dve.tensor_tensor(BW[:, :, :], CA[:, 1:NL, :], CA[:, 0:BENDS, :], ALU.subtract))
            link(dve.tensor_tensor(BO[:, :, :], CB[:, 1:NL, :], CB[:, 0:BENDS, :], ALU.subtract))
            link(dve.tensor_tensor(A0[:, :], CA[:, 0, 0:2 * NC:2], CA[:, 0, 1:2 * NC:2], ALU.subtract))
            link(dve.tensor_tensor(K0[:, :], CB[:, 0, 0:2 * NC:2], CB[:, 0, 1:2 * NC:2], ALU.subtract))

        with nc.Block() as block:
            piece_steps = sem("piece_steps")
            xn_ready, xn_turned, xT_ready = sem("p2_xn_ready"), sem("p2_xn_turned"), sem("p2_xT_ready")
            h1_summed, h1_ready, h2_summed, h2_ready = sem("h1_summed"), sem("h1_ready"), sem("h2_summed"), sem("h2_ready")
            h2_used, y_summed = sem("h2_used"), sem("y_summed")
            cw_added, y_used, x2_ready = sem("cw_added"), sem("y_used"), sem("x2_ready")

            @block.gpsimd
            def _(pool):
                with pool.Fori(0, NG) as g:
                    pool.wait_ge(xn_ready, g * 4 + 4)
                    x = X[:, bass.ds(g * GW, GW)].rearrange("p (t d) -> p t d", d=P)
                    pool.tensor_tensor(x, x, CW[:, :].unsqueeze(1).to_broadcast([P, G4, P]), ALU.add).then_inc(cw_added, 1)

            @block.tensor
            def _(pe):
                def turn(g, p):
                    pe.wait_ge(xn_ready, g * 4 + 4)
                    wait(pe, xT_ready, g)
                    for j in range(G4):
                        last = pe.transpose(PS[0][:, j * P:(j + 1) * P], xn4[p][:, j * P:(j + 1) * P], ident[:, :])
                    last.then_inc(xn_turned, 1)

                def group(g, p, nxt):
                    def first(e):
                        if e == 0:
                            pe.wait_ge(xT_ready, g + 1)
                        wait(pe, h1_ready, g * E + e - 1)
                        pe.matmul(PS[1 + e % 2][:, :], W1[:, e, :], xT4[p], start=True, stop=True).then_inc(h1_summed, 1)

                    def second(e):
                        pe.wait_ge(h1_ready, g * E + e + 1)
                        wait(pe, h2_ready, g * E + e - 1)
                        pe.matmul(PS[3 + e % 2][:, :], W2[:, e, :], h1[e % 2], start=True, stop=True).then_inc(h2_summed, 1)

                    def third(e):
                        pe.wait_ge(h2_ready, g * E + e + 1)
                        if e == 0:
                            wait(pe, y_used, g)
                        for j in range(G4):
                            last = pe.matmul(PS[5 + p][:, j * P:(j + 1) * P], h2[e % 2][:, j * P:(j + 1) * P], Wo[:, e, :],
                                             start=(e == 0 and j == 0), stop=(e == E - 1), skip_group_check=True)
                        last.then_inc(h2_used, 1)

                    for e in range(E + 2):
                        if e < E:
                            first(e)
                        if e == 5 and nxt:
                            turn(*nxt)
                        if 1 <= e <= E:
                            second(e - 1)
                        if e >= 2:
                            third(e - 2)

                turn(0, 0)
                group(0, 0, (1, 1))
                with pe.Fori(0, NG // 2 - 1) as i:
                    group(i * 2 + 1, 1, (i * 2 + 2, 0))
                    group(i * 2 + 2, 0, (i * 2 + 3, 1))
                group(NG - 1, 1, None)

            @block.scalar
            def _(act):
                def copy_xT(g, p):
                    act.wait_ge(xn_turned, g + 1)
                    wait(act, h1_summed, (g - 1) * E)
                    act.copy(xT4[p], PS[0][:, :]).then_inc(xT_ready, 1)

                def group(g, p, nxt):
                    for e in range(E):
                        act.wait_ge(h1_summed, g * E + e + 1)
                        wait(act, h2_summed, g * E + e - 1)
                        act.activation(h1[e % 2], PS[1 + e % 2][:, :], ACT.Relu, bias=c1[:, e:e + 1],
                                       scale=sc1[:, e:e + 1]).then_inc(h1_ready, 1)
                        if e == 5 and nxt:
                            copy_xT(*nxt)

                copy_xT(0, 0)
                group(0, 0, (1, 1))
                with act.Fori(0, NG // 2 - 1) as i:
                    group(i * 2 + 1, 1, (i * 2 + 2, 0))
                    group(i * 2 + 2, 0, (i * 2 + 3, 1))
                group(NG - 1, 1, None)

            @block.vector
            def _(dve):
                def norms(g, p):
                    wait(dve, xn_turned, g - 1)
                    for j in range(G4):
                        normalise(dve, xn4[p][:, j * P:(j + 1) * P], g * G4 + j).then_inc(xn_ready, 1)

                def group(g, p, nxt, link=None, n=None):
                    for e in range(E):
                        dve.wait_ge(h2_summed, g * E + e + 1)
                        wait(dve, h2_used, g * E + e - 1)
                        dve.scalar_tensor_tensor(h2[e % 2].rearrange("p (t n) -> p t n", n=P),
                                                 PS[3 + e % 2][:, :].rearrange("p (t n) -> p t n", n=P),
                                                 nc2[:, e:e + 1], WB[:, e:e + 1, :].to_broadcast([P, G4, P]),
                                                 ALU.max, ALU.mult).then_inc(h2_ready, 1)
                        if e == 2 and nxt:
                            norms(*nxt)
                        if link is not None and e in (0, 4, 6):
                            next_piece(dve, link, n, (0, 4, 6).index(e))

                def finish(g, p):
                    dve.wait_ge(h2_used, g * E + E)
                    dve.wait_ge(cw_added, g + 1)
                    x = X[:, bass.ds(g * GW, GW)]
                    dve.tensor_tensor(x, PS[5 + p][:, :], x, ALU.add).then_inc(y_used, 1)
                    dve.wait_ge(y_used, g + 2)
                    for j in range(G4):
                        tile_stats(dve, g * G4 + j).then_inc(x2_ready, 1)

                dve.sem_inc(y_used, 1)
                norms(0, 0)
                first_piece(dve, Chain(dve, piece_steps))
                group(0, 0, (1, 1))
                finish(0, 0)
                assert BENDS == NG // 2 - 1
                with dve.Fori(0, BENDS) as i:
                    group(i * 2 + 1, 1, (i * 2 + 2, 0), Chain(dve, piece_steps, i * BEND_LINKS + FIRST_LINKS), i + 1)
                    finish(i * 2 + 1, 1)
                    group(i * 2 + 2, 0, (i * 2 + 3, 1))
                    finish(i * 2 + 2, 0)
                bends_of_pieces(dve, Chain(dve, piece_steps, BENDS * BEND_LINKS + FIRST_LINKS))
                group(NG - 1, 1, None)
                finish(NG - 1, 1)

        layer_norm_scales("ln3")

        carve = Carve()
        g_adj = carve(P).bitcast(I32)
        g_adjf, g_adjT, g_xn, g_xT = carve(P), carve(P), carve(P), carve(P)
        g_hg = carve(4 * P)
        g_rel = carve(1)
        g_sel, g_mf, g_mb = carve(P), carve(P), carve(P)
        g_sig, g_val = carve(2 * P), carve(2 * P)
        with nc.Block() as block:
            ga_loaded, ga_free, g_in = sem("ga_loaded"), sem("ga_free"), sem("g_in")
            g_turned, g_copied, g_proj, g_hgready = sem("g_turned"), sem("g_copied"), sem("g_proj"), sem("g_hgready")
            g_rset, g_mask, g_vsum, g_sigready, g_valready, g_acc, g_added = (
                sem("g_rset"), sem("g_mask"), sem("g_vsum"), sem("g_sigready"), sem("g_valready"), sem("g_acc"), sem("g_added"))

            def if_relations(eng):
                return eng.If(eng.value_load(flag[0:1, 0:1]) > 0)

            @block.sync
            def _(sp):
                with if_relations(sp):
                    with sp.Fori(0, NT) as t:
                        sp.wait_ge(ga_free, t + 1)
                        sp.dma_start(g_adj, a["adj"][bass.ds(t, 1)].rearrange("o p j -> (o p) j")).then_inc(ga_loaded, 16)

            @block.vector
            def _(dve):
                with if_relations(dve):
                    dve.sem_inc(ga_free, 1)
                    with dve.Fori(0, NT) as t:
                        dve.wait_ge(ga_loaded, t * 16 + 16)
                        dve.tensor_copy(g_adjf, g_adj).then_inc(ga_free, 1)
                        dve.memset(g_rel, 1.0).then_inc(g_rset, 1)
                        normalise(dve, g_xn, t).then_inc(g_in, 1)
                        with dve.Fori(0, NREL) as r:
                            n = t * NREL + r
                            dve.wait_ge(g_hgready, t + 1)
                            dve.wait_ge(ga_free, t + 2)
                            dve.wait_ge(g_rset, t * (NREL + 1) + r + 1)
                            dve.tensor_scalar(g_rel, g_rel, 1.0, None, ALU.add).then_inc(g_rset, 1)
                            dve.wait_ge(g_rset, t * (NREL + 1) + r + 2)
                            dve.tensor_scalar(g_sel, pidx[:, :], 2.0, g_rel, ALU.add, ALU.is_equal).then_inc(g_mask, 1)
                            dve.tensor_scalar(g_mf, g_adjT, g_rel, None, ALU.is_equal).then_inc(g_mask, 1)
                            dve.tensor_scalar(g_mb, g_adjf, g_rel, None, ALU.is_equal).then_inc(g_mask, 1)
                            dve.wait_ge(g_sigready, n * 2 + 2)
                            for h in range(2):
                                dve.tensor_tensor(g_val[:, h * P:(h + 1) * P], PS[2][:, 2 * h * P:(2 * h + 1) * P],
                                                  g_sig[:, h * P:(h + 1) * P], ALU.mult).then_inc(g_valready, 1)
                            dve.wait_ge(g_acc, n + 1)
                            ex = EX[:, bass.ds(t * P, P)]
                            dve.tensor_tensor(ex, PS[3][:, 0:P], ex, ALU.add).then_inc(g_added, 1)
                            dve.wait_ge(g_added, n + 1)

            @block.scalar
            def _(act):
                with if_relations(act):
                    with act.Fori(0, NT) as t:
                        act.wait_ge(g_turned, t + 1)
                        act.copy(g_adjT, PS[0][:, 0:P]).then_inc(g_copied, 1)
                        act.copy(g_xT, PS[0][:, P:2 * P]).then_inc(g_copied, 1)
                        act.wait_ge(g_proj, t + 1)
                        act.wait_ge(g_copied, t * 2 + 2)
                        act.copy(g_hg, PS[1][:, :]).then_inc(g_hgready, 1)
                        with act.Fori(0, NREL) as r:
                            act.wait_ge(g_vsum, t * NREL + r + 1)
                            for h in range(2):
                                act.activation(g_sig[:, h * P:(h + 1) * P], PS[2][:, (2 * h + 1) * P:(2 * h + 2) * P],
                                               ACT.Sigmoid).then_inc(g_sigready, 1)

            @block.tensor
            def _(pe):
                with if_relations(pe):
                    with pe.Fori(0, NT) as t:
                        pe.wait_ge(g_in, t + 1)
                        pe.wait_ge(ga_free, t + 2)
                        pe.transpose(PS[0][:, 0:P], g_adjf, ident[:, :])
                        pe.transpose(PS[0][:, P:2 * P], g_xn, ident[:, :]).then_inc(g_turned, 1)
                        pe.wait_ge(g_copied, t * 2 + 2)
                        pe.matmul(PS[1][:, :], g_xT, WHG[:, 0:2, :, :].rearrange("p i s d -> p (i s d)"),
                                  start=True, stop=True).then_inc(g_proj, 1)
                        with pe.Fori(0, NREL) as r:
                            n = t * NREL + r
                            pe.wait_ge(g_hgready, t + 1)
                            pe.wait_ge(g_mask, n * 3 + 3)
                            pe.matmul(PS[2][:, :], ident[:, :], g_hg, start=True, stop=False)
                            pe.matmul(PS[2][:, :], g_sel, B4[:, :], start=False, stop=True).then_inc(g_vsum, 1)
                            pe.wait_ge(g_valready, n * 2 + 2)
                            pe.matmul(PS[3][:, 0:P], g_mf, g_val[:, 0:P], start=True, stop=False)
                            pe.matmul(PS[3][:, 0:P], g_mb, g_val[:, P:2 * P], start=False, stop=True).then_inc(g_acc, 1)

        carve = Carve()
        xn = [carve(GW) for _ in range(2)]
        xT = [carve(GW) for _ in range(2)]
        m1f = [carve(GW) for _ in range(2)]
        sig = [carve(GW) for _ in range(2)]
        val = [carve(GW) for _ in range(2)]
        tmp = [carve(GW) for _ in range(2)]
        with nc.Block() as block:
            xn_ready, xn_turned, xT_ready = sem("p3_xn_ready"), sem("p3_xn_turned"), sem("p3_xT_ready")
            hg_summed, sig_ready, val_ready = sem("hg_summed"), sem("sig_ready"), sem("val_ready")
            m1_ready, agg_summed, agg_used, relu_done, x3_ready = (
                sem("m1_ready"), sem("agg_summed"), sem("agg_used"), sem("relu_done"), sem("x3_ready"))
            BTURN, BAGG = PS[0:2], PS[6:8]
            BHG = [PS[2:4], PS[4:6]]

            @block.gpsimd
            def _(pool):
                def body(g, p):
                    if exists(g + 1):
                        wait(pool, agg_summed, g)
                        pool.tensor_copy(m1f[1 - p], M1[:, bass.ds((g + 1) * GW, GW)]).then_inc(m1_ready, 1)

                pipeline(pool, body)

            @block.tensor
            def _(pe):
                def turn(g, p):
                    pe.wait_ge(xn_ready, g + 1)
                    wait(pe, xT_ready, g - 1)
                    for j in range(G4):
                        last = pe.transpose(BTURN[p][:, j * P:(j + 1) * P], xn[p][:, j * P:(j + 1) * P], ident[:, :])
                    last.then_inc(xn_turned, 1)

                def project(g, p):
                    pe.wait_ge(xT_ready, g + 1)
                    wait(pe, val_ready, g * 2 - 2)
                    for h in range(2):
                        pe.matmul(BHG[p][h][:, :], onesb[0:3, :], brows[:, 1, :], start=True, stop=False, skip_group_check=True)
                        for j in range(2):
                            t = 2 * h + j
                            last = pe.matmul(BHG[p][h][:, 2 * j * P:2 * (j + 1) * P], xT[p][:, t * P:(t + 1) * P],
                                             WHG[:, 2, :, :].rearrange("p s d -> p (s d)"),
                                             start=False, stop=True, skip_group_check=True)
                        last.then_inc(hg_summed, 1)

                def gather(g, p):
                    pe.wait_ge(val_ready, g * 2 + 2)
                    pe.wait_ge(m1_ready, g + 1)
                    wait(pe, agg_used, g - 1)
                    for j in range(G4):
                        last = pe.matmul(BAGG[p][:, j * P:(j + 1) * P], m1f[p][:, j * P:(j + 1) * P], val[p][:, j * P:(j + 1) * P],
                                         start=True, stop=True)
                    last.then_inc(agg_summed, 1)

                def body(g, p):
                    if exists(g + 1):
                        turn(g + 1, 1 - p)
                    if exists(g):
                        project(g, p)
                    if exists(g - 1):
                        gather(g - 1, 1 - p)

                pipeline(pe, body)

            @block.scalar
            def _(act):
                def body(g, p):
                    if exists(g + 2):
                        norms(act, g + 2, xn[p], xn_turned, xn_ready)
                    if exists(g + 1):
                        act.wait_ge(xn_turned, g + 2)
                        wait(act, hg_summed, g * 2)
                        act.copy(xT[1 - p], BTURN[1 - p][:, :]).then_inc(xT_ready, 1)
                    if exists(g):
                        for h in range(2):
                            act.wait_ge(hg_summed, g * 2 + h + 1)
                            wait(act, val_ready, g * 2 - 2)
                            act.activation(sig[p][:, 2 * h * P:2 * (h + 1) * P].rearrange("p (t d) -> p t d", t=2),
                                           BHG[p][h][:, :].rearrange("p (t s d) -> p t s d", t=2, s=2)[:, :, 1, :],
                                           ACT.Sigmoid).then_inc(sig_ready, 1)

                pipeline(act, body)

            @block.vector
            def _(dve):
                def products(g, p):
                    for h in range(2):
                        dve.wait_ge(sig_ready, g * 2 + h + 1)
                        wait(dve, agg_summed, g - 1)
                        halves = slice(2 * h * P, 2 * (h + 1) * P)
                        dve.tensor_tensor(val[p][:, halves].rearrange("p (t d) -> p t d", t=2),
                                          BHG[p][h][:, :].rearrange("p (t s d) -> p t s d", t=2, s=2)[:, :, 0, :],
                                          sig[p][:, halves].rearrange("p (t d) -> p t d", t=2), ALU.mult).then_inc(val_ready, 1)

                def back(g, p):
                    x = X[:, bass.ds(g * GW, GW)]
                    dve.wait_ge(agg_summed, g + 1)
                    dve.tensor_tensor(tmp[p], BAGG[p][:, :], EX[:, bass.ds(g * GW, GW)], ALU.add).then_inc(agg_used, 1)
                    dve.wait_ge(agg_used, g + 1)
                    dve.scalar_tensor_tensor(x, tmp[p], 0.0, x, ALU.max, ALU.add).then_inc(relu_done, 1)
                    dve.wait_ge(relu_done, g + 1)
                    for j in range(G4):
                        last = tile_stats(dve, g * G4 + j)
                    last.then_inc(x3_ready, 1)

                def body(g, p):
                    if exists(g):
                        products(g, p)
                    if exists(g - 1):
                        back(g - 1, 1 - p)

                pipeline(dve, body)

        layer_norm_scales("ln4")

        class Pwl:
            def __init__(self, tag):
                self.dbend_ready, self.pbend_ready = sem(tag + "_dbend_ready"), sem(tag + "_pbend_ready")
                self.acts_ready, self.fn_summed = sem(tag + "_acts_ready"), sem(tag + "_fn_summed")
                self.stepped, self.pbend_added = sem(tag + "_stepped"), sem(tag + "_pbend_added")
                self.out_summed, self.out_made, self.out_stored = (
                    sem(tag + "_out_summed"), sem(tag + "_out_made"), sem(tag + "_out_stored"))

        at_ex = [0]

        def carve_ex(n):
            v = EX[:, at_ex[0]:at_ex[0] + n]
            at_ex[0] += n
            assert at_ex[0] <= NT * P
            return v

        carve = Carve()
        Zall = carve_ex(NC * GW)
        Z = [Zall[:, c * GW:(c + 1) * GW] for c in range(NC)]
        T = [carve_ex(NH) for _ in range(G4)]
        ring_d = [carve_ex(GW) for _ in range(RING_D)]
        ring_p = [carve_ex(GW) for _ in range(RING_P)]
        TO = carve(NH)
        YE = carve(G4 * YW).rearrange("p (j w) -> p j w", j=G4)
        YO = carve(YW)
        slotm = [carve(P) for _ in range(G4)]
        slotT = carve(G4 * P)
        xna, xT4 = carve(GW), carve(GW)
        OH = [carve(8 * P // 2).bitcast(BF16) for _ in range(2)]
        OHT = [carve(8 * P // 2).bitcast(BF16) for _ in range(2)]
        gelu = [carve(GW) for _ in range(2)]
        gate, acc = carve(GW), carve(GW)
        F = [carve(GW) for _ in range(2)]
        outs = carve(GW)
        top = [carve(8) for _ in range(2)]
        topo = carve(R2)
        rest = carve(8 * G4)
        resto = carve(8)
        taken = carve(2)
        index = carve(8).bitcast(U32)
        padded = carve(4).bitcast(BF16)
        opened = padded[:, G4 - 1:2 * G4 - 1]
        closed = carve(G4)
        slot = carve(G4)
        sel = [carve(P) for _ in range(2)]
        dcount = carve(1)
        BM, BFN, BBEND, BOUT = PS[4], PS[5], PS[6], PS[7]

        def act_bend_d(act, s, m, c, k):
            n, col = (0, 2 * c) if k == 0 else (k - 1, 2 * c + 1)
            before = m * STEPS + k - RING_D if k >= RING_D else (m - 1) * STEPS + DVE_TERMS + k - RING_D
            wait(act, s.stepped, before + 1)
            act.activation(ring_d[k % RING_D], Z[c], ACT.Relu, bias=BO[:, n, col:col + 1],
                           scale=BW[:, n, col:col + 1]).then_inc(s.dbend_ready, 1)

        def act_bend_p(act, s, m, c, k):
            wait(act, s.pbend_added, m * PE_TERMS + k - RING_P + 1)
            act.activation(ring_p[k % RING_P], Z[c], ACT.Relu, bias=BO[:, k + 1, 2 * c:2 * c + 1],
                           scale=BW[:, k + 1, 2 * c:2 * c + 1]).then_inc(s.pbend_ready, 1)

        def act_gelu(act, s, m, c):
            act.wait_ge(s.fn_summed, m * 2 + 1)
            wait(act, s.out_summed, m - 1)
            act.activation(gelu[c % 2], BFN[:, :], ACT.Gelu, bias=PT[:, bc_at + c:bc_at + c + 1]).then_inc(s.acts_ready, 1)

        def act_gate(act, s, m, c):
            act.wait_ge(s.fn_summed, m * 2 + 2)
            wait(act, s.stepped, m * STEPS)
            act.activation(gate, BFN[:, :], ACT.Tanh, bias=bgh[:, c:c + 1], scale=0.5).then_inc(s.acts_ready, 1)

        def act_first(act, s, m, c):
            for k in range(3):
                act_bend_d(act, s, m, c, k)
                act_bend_p(act, s, m, c, k)
            act_bend_d(act, s, m, c, 3)

        def act_second(act, s, m, c):
            act_bend_d(act, s, m, c, 4)
            act_bend_p(act, s, m, c, 3)
            act_gelu(act, s, m, c)

        def act_third(act, s, m, c):
            act_bend_d(act, s, m, c, 5)
            act_bend_p(act, s, m, c, 4)
            act_bend_d(act, s, m, c, 6)
            act_bend_p(act, s, m, c, 5)
            act_bend_d(act, s, m, c, 7)
            act_gate(act, s, m, c)

        def dve_step(dve, s, m, c, n):
            after = m * STEPS + n
            wait(dve, s.stepped, after)
            if n < DVE_TERMS:
                dve.wait_ge(s.dbend_ready, m * DVE_TERMS + n + 1)
                bend = ring_d[n % RING_D]
                if n == 0:
                    dve.scalar_tensor_tensor(acc, Z[c], A0[:, c:c + 1], bend, ALU.mult, ALU.add).then_inc(s.stepped, 1)
                else:
                    dve.tensor_tensor(acc, acc, bend, ALU.subtract).then_inc(s.stepped, 1)
            elif n == DVE_TERMS:
                dve.wait_ge(s.pbend_added, m * PE_TERMS + PE_TERMS)
                dve.tensor_tensor(acc, BBEND[:, :], acc, ALU.add).then_inc(s.stepped, 1)
            elif n == DVE_TERMS + 1:
                dve.wait_ge(s.acts_ready, m * 2 + 1)
                dve.scalar_tensor_tensor(acc, acc, K0[:, c:c + 1], gelu[c % 2], ALU.add, ALU.subtract).then_inc(s.stepped, 1)
            else:
                dve.wait_ge(s.acts_ready, m * 2 + 2)
                wait(dve, s.out_summed, m - 1)
                dve.scalar_tensor_tensor(F[c % 2], gate, 1.0, acc, ALU.add, ALU.mult).then_inc(s.stepped, 1)

        def pe_bend(pe, s, m, c, k):
            pe.wait_ge(s.pbend_ready, m * PE_TERMS + k + 1)
            if k == 0:
                wait(pe, s.stepped, (m - 1) * STEPS + DVE_TERMS + 1)
            pe.matmul(BBEND[:, :], ident[:, :], ring_p[k % RING_P], start=(k == 0), stop=(k == PE_TERMS - 1)).then_inc(s.pbend_added, 1)

        def pe_function(pe, s, m, c, f):
            wait(pe, s.acts_ready, m * 2 + f)
            pe.matmul(BFN[:, :], (Wc, Wg)[f][:, c * P:(c + 1) * P], xT4, start=True, stop=True).then_inc(s.fn_summed, 1)

        def pe_out(pe, s, m, c, g):
            pe.wait_ge(s.stepped, m * STEPS + STEPS)
            if c == 0:
                wait(pe, s.out_made, g)
                pe.matmul(BOUT[:, :], ones[0:1, :], bdrow[:, :], start=True, stop=False, skip_group_check=True)
            for j in range(G4):
                tile = slice(j * P, (j + 1) * P)
                pe.matmul(BOUT[:, tile], gelu[c % 2][:, tile], Wd[:, c, :], start=False, stop=False, skip_group_check=True)
                last = pe.matmul(BOUT[:, tile], F[c % 2][:, tile], Wdh[:, c, :],
                                 start=False, stop=(c == NC - 1), skip_group_check=True)
            last.then_inc(s.out_summed, 1)

        def dve_finish(dve, s, g):
            dve.wait_ge(s.out_summed, g * NC + NC)
            dve.wait_ge(s.out_stored, g * 16 + 16)
            dve.tensor_tensor(outs, BOUT[:, :], X[:, bass.ds(g * GW, GW)], ALU.add).then_inc(s.out_made, 1)

        def store_groups(sp, s):
            sp.sem_inc(s.out_stored, 16)
            with sp.Fori(0, NG) as g:
                sp.wait_ge(s.out_made, g + 1)
                sp.dma_start(out[bass.ds(g * G4, G4)].rearrange("t p d -> p t d"),
                             outs.rearrange("p (t d) -> p t d", d=P)).then_inc(s.out_stored, 16)
            sp.wait_ge(s.out_stored, NG * 16 + 16)

        def all_groups(eng, iteration):
            iteration(0)
            iteration(1)
            with eng.Fori(2, NG - 1) as g:
                iteration(g)
            iteration(NG - 1)
            iteration(NG)

        def has_tiles(g):
            return not isinstance(g, int) or g < NG

        def has_next(g):
            return not isinstance(g, int) or g < NG - 1

        def has_pwl(g):
            return not isinstance(g, int) or g >= 1

        def has_finish(g):
            return not isinstance(g, int) or g >= 2

        s4 = Pwl("p4")
        ones_made, y_steps, oh_ready, oh_turned, oht_ready = (
            sem("ones_made"), sem("y_steps"), sem("oh_ready"), sem("oh_turned"), sem("oht_ready"))
        cand_summed, cand_used = sem("cand_summed"), sem("cand_used")
        min_ready, open_ready, slots_given, slotm_ready = sem("min_ready"), sem("open_ready"), sem("slots_given"), sem("slotm_ready")
        bm_filled, bm_read = sem("bm_filled"), sem("bm_read")
        z_turned, z_ready = sem("z_turned"), sem("z_ready")
        OPEN_KNOWN, ROWS_TURNED = 30.5, 31.5
        xna_ready = sem("xna_ready")
        BENDS_AFTER = [[2, 3, 4, 5, 6, 7], [15, 17, 18, 20, 21, 22], [29, 30, 30, OPEN_KNOWN, OPEN_KNOWN, 31], [37, 38, 39, 40, 41, 42]]
        GELU_AFTER, GATE_AFTER, OUT_AFTER = [2, 15, 30, ROWS_TURNED], [6, 20, 31, 41], [16, ROWS_TURNED, 47]
        F_SLOT, F_ROWS, F_SLOTT, F_XT = 0, 1, 2, 3
        BZ = [BFN, BBEND, BM, BFN]
        with nc.Block() as block:
            @block.sync
            def _(sp):
                store_groups(sp, s4)

            @block.tensor
            def _(pe):
                def turn_onehots(q, slot_):
                    pe.wait_ge(oh_ready, q + 1)
                    wait(pe, oht_ready, q)
                    for k in range(8):
                        last = pe.transpose(BM[:, :].bitcast(BF16)[:, k * P:(k + 1) * P], OH[slot_][:, k * P:(k + 1) * P],
                                            identb[:, :])
                    last.then_inc(oh_turned, 1)

                def beside(g, u):
                    m0 = (g - 1) * NC
                    if u == 0 and has_pwl(g):
                        pe.wait_ge(z_ready, g * G4)
                    if u == 7 and has_finish(g):
                        pe_out(pe, s4, m0 - 1, NC - 1, g - 2)
                    if has_pwl(g):
                        for c in range(NC):
                            for k in range(PE_TERMS):
                                if BENDS_AFTER[c][k] == u:
                                    pe_bend(pe, s4, m0 + c, c, k)
                            if GELU_AFTER[c] == u:
                                pe_function(pe, s4, m0 + c, c, 0)
                            if GATE_AFTER[c] == u:
                                pe_function(pe, s4, m0 + c, c, 1)
                            if c < NC - 1 and OUT_AFTER[c] == u:
                                pe_out(pe, s4, m0 + c, c, g - 1)

                def candidates(q, slot_, g, u0, turn_next=None):
                    pe.wait_ge(oht_ready, q + 1)
                    for k in range(8):
                        u = u0 + k
                        wait(pe, cand_used, g * USES + u - CB4 + 1)
                        for part in range(3):
                            last = pe.matmul(PS[u % CB4][:, :], OHT[slot_][:, k * P:(k + 1) * P], WP[:, part, :],
                                             start=(part == 0), stop=(part == 2))
                        last.then_inc(cand_summed, 1)
                        if u != G4 * R1 - 1:
                            beside(g, u)
                        if k == turn_next:
                            turn_onehots(q + 1, 1 - slot_)

                def fill(g, f):
                    wait(pe, bm_read, g * FILLS + f)

                def iteration(g):
                    q0, m0 = g * ROUNDS, (g - 1) * NC
                    if not has_tiles(g):
                        for u in range(G4 * R1 + R2):
                            if u == G4 * R1 - 1:
                                beside(g, OPEN_KNOWN)
                            beside(g, u)
                            if u == G4 * R1 - 1:
                                beside(g, ROWS_TURNED)
                        pe_out(pe, s4, m0 + 3, 3, g - 1)
                        return
                    for j in range(G4):
                        candidates(q0 + j, j % 2, g, j * R1, turn_next=6 if j + 1 < G4 else None)
                    beside(g, OPEN_KNOWN)
                    fill(g, F_SLOT)
                    pe.wait_ge(open_ready, g + 1)
                    pe.matmul(BM[:, 0:G4], tri[:, :], opened, start=True, stop=False)
                    for j in range(1, G4):
                        last = pe.matmul(BM[:, 0:G4], onesb[:, :], padded[:, G4 - 1 - j:2 * G4 - 1 - j],
                                         start=False, stop=(j == G4 - 1))
                    last.then_inc(bm_filled, 1)
                    beside(g, G4 * R1 - 1)
                    fill(g, F_ROWS)
                    pe.wait_ge(slotm_ready, g * G4 + G4)
                    for j in range(G4):
                        last = pe.matmul(BM[:, 0:YW], slotm[j], YE[:, j, :], start=(j == 0), stop=(j == G4 - 1))
                    last.then_inc(bm_filled, 1)
                    fill(g, F_SLOTT)
                    for j in range(G4):
                        last = pe.transpose(BM[:, j * P:(j + 1) * P], slotm[j], ident[:, :])
                    last.then_inc(bm_filled, 1)
                    beside(g, ROWS_TURNED)
                    pe.wait_ge(bm_read, g * FILLS + F_SLOTT + 1)
                    turn_onehots(q0 + 4, 0)
                    candidates(q0 + 4, 0, g, G4 * R1, turn_next=1)
                    candidates(q0 + 5, 1, g, G4 * R1 + 8, turn_next=3 if has_next(g) else None)
                    fill(g, F_XT)
                    if has_next(g):
                        pe.wait_ge(oht_ready, q0 + ROUNDS + 1)
                    pe.wait_ge(xna_ready, g * G4 + G4)
                    for j in range(G4):
                        last = pe.transpose(BM[:, j * P:(j + 1) * P], xna[:, j * P:(j + 1) * P], ident[:, :])
                    last.then_inc(bm_filled, 1)
                    pe.wait_ge(cand_used, g * USES + G4 * R1 + R2)
                    for j in range(G4):
                        u = G4 * R1 + R2 + j
                        pe.wait_ge(cand_used, g * USES + u - CB4 + 1)
                        pe.matmul(PS[u % CB4][:, :], slotT[:, j * P:(j + 1) * P], TO, start=True, stop=True).then_inc(cand_summed, 1)
                    for j in range(G4):
                        pe.wait_ge(cand_used, g * USES + G4 * R1 + R2 + j + 1)
                        if j == 0:
                            wait(pe, s4.acts_ready, g * NC * 2)
                        elif j == 1:
                            wait(pe, s4.stepped, g * NC * STEPS - STEPS + DVE_TERMS + 1)
                        elif j == 2:
                            pe.wait_ge(bm_read, (g + 1) * FILLS)
                        else:
                            pe.wait_ge(z_ready, g * G4 + 1)
                        for c in range(NC):
                            last = pe.transpose(BZ[j][:, c * P:(c + 1) * P], T[j][:, c * P:(c + 1) * P], ident[:, :])
                        last.then_inc(z_turned, 1)

                turn_onehots(0, 0)
                all_groups(pe, iteration)

            @block.scalar
            def _(act):
                def copy_onehots(q, slot_):
                    act.wait_ge(oh_turned, q + 1)
                    act.copy(OHT[slot_], BM[:, :].bitcast(BF16)).then_inc(oht_ready, 1)

                def onehot_free(g, j):
                    wait(act, cand_summed, g * USES + (j - 1) * 8 if j >= 2 else (g - 1) * USES + G4 * R1 + (j + 1) * 8)

                def iteration(g):
                    q0, m0 = g * ROUNDS, (g - 1) * NC

                    def onehots(j):
                        if has_tiles(g):
                            onehot_free(g, j)
                            copy_onehots(q0 + j, j % 2)

                    def chunk(c, part):
                        if has_pwl(g):
                            part(act, s4, m0 + c, c)

                    if has_pwl(g):
                        act.wait_ge(z_ready, g * G4)
                    for part in (act_first, act_second, act_third):
                        chunk(0, part)
                    onehots(1)
                    chunk(1, act_first)
                    onehots(2)
                    chunk(1, act_second)
                    chunk(1, act_third)
                    onehots(3)
                    for part in (act_first, act_second, act_third):
                        chunk(2, part)
                    if has_tiles(g):
                        act.wait_ge(bm_filled, g * FILLS + F_ROWS + 1)
                        act.copy(YO, BM[:, 0:YW]).then_inc(bm_read, 1)
                        act.wait_ge(bm_filled, g * FILLS + F_SLOTT + 1)
                        act.copy(slotT, BM[:, :]).then_inc(bm_read, 1)
                    chunk(3, act_first)
                    onehots(4)
                    onehots(5)
                    chunk(3, act_second)
                    chunk(3, act_third)
                    if has_tiles(g):
                        wait(act, bm_filled, (g - 1) * FILLS + F_XT + 1)
                        for j in range(G4):
                            t = g * G4 + j
                            act.activation(xna[:, j * P:(j + 1) * P], X[:, bass.ds(t * P, P)], ACT.Identity,
                                           bias=NMR[:, bass.ds(t, 1)], scale=RSTD[:, bass.ds(t, 1)]).then_inc(xna_ready, 1)
                        if has_next(g):
                            onehot_free(g + 1, 0)
                            copy_onehots(q0 + ROUNDS, 0)
                        act.wait_ge(bm_filled, g * FILLS + F_XT + 1)
                        wait(act, s4.fn_summed, g * NC * 2)
                        act.copy(xT4, BM[:, :]).then_inc(bm_read, 1)
                        wait(act, s4.stepped, g * NC * STEPS - STEPS + 1)
                        for j in range(G4):
                            act.wait_ge(z_turned, g * G4 + j + 1)
                            act.copy(Zall.rearrange("p (c t n) -> p c t n", c=NC, t=G4)[:, :, j, :],
                                     BZ[j][:, :].rearrange("p (c n) -> p c n", c=NC)).then_inc(z_ready, 1)

                copy_onehots(0, 0)
                all_groups(act, iteration)

            @block.vector
            def _(dve):
                def find8(src, dst):
                    dve.drain()
                    dve.max(dst, src)

                def locate8(src, dst):
                    dve.drain()
                    dve.max_index(index, dst, src)
                    dve.match_replace(src, dst, src, FAR)
                    dve.drain()

                def onehots(q, slot_):
                    wait(dve, oh_turned, q - 1)
                    dve.tensor_tensor(OH[slot_].rearrange("p (k f) -> p k f", k=8),
                                      colb[:, :].unsqueeze(1).to_broadcast([P, 8, P]),
                                      index.unsqueeze(2).to_broadcast([P, 8, P]), ALU.is_equal).then_inc(oh_ready, 1)

                SELECT_PARTS = 4

                def select(g, j, part):
                    t, y = g * G4 + j, YE[:, j, 0:P]
                    if part == 0:
                        wait(dve, bm_filled, (g - 1) * FILLS + F_ROWS + 1)
                        dve.tensor_scalar(y, X[:, bass.ds(t * P, P)], MEAN[:, bass.ds(t, 1)], RSTD[:, bass.ds(t, 1)],
                                          ALU.subtract, ALU.mult).then_inc(y_steps, 1)
                        dve.wait_ge(y_steps, t + 1)
                        dve.tensor_tensor(y, y, mwrow[:, :], ALU.add)
                        find8(y, top[j % 2])
                    elif part == 1:
                        locate8(y, top[j % 2])
                    elif part == 2:
                        onehots(g * ROUNDS + j, j % 2)
                    else:
                        dve.max(rest[:, 8 * j:8 * j + 8], y)

                def maximum(g, u, dst, bound, first=False):
                    dve.wait_ge(cand_summed, g * USES + u + 1)
                    if first:
                        dve.tensor_scalar(dst, PS[u % CB4][:, :], bound, None, ALU.add).then_inc(cand_used, 1)
                    else:
                        dve.wait_ge(cand_used, g * USES + u)
                        dve.scalar_tensor_tensor(dst, PS[u % CB4][:, :], bound, dst, ALU.add, ALU.max).then_inc(cand_used, 1)

                def steps(g, first, count):
                    if has_pwl(g):
                        for w in range(first, first + count):
                            dve_step(dve, s4, (g - 1) * NC + w // STEPS, w // STEPS, w % STEPS)

                def iteration(g):
                    if not has_tiles(g):
                        steps(g, 0, 6)
                        dve_finish(dve, s4, g - 2)
                        steps(g, 6, NC * STEPS - 6)
                        dve_finish(dve, s4, g - 1)
                        return
                    for j in range(G4):
                        wait(dve, z_turned, (g - 1) * G4 + j + 1)
                        for k in range(R1):
                            maximum(g, j * R1 + k, T[j], top[j % 2][:, k:k + 1], first=(k == 0))
                            if j + 1 < G4 and k < SELECT_PARTS:
                                select(g, j + 1, k)
                            if k < 6:
                                steps(g, 6 * j + k, 1)
                            if j == 1 and k == 2 and has_finish(g):
                                dve_finish(dve, s4, g - 2)
                        dve.wait_ge(cand_used, g * USES + (j + 1) * R1)
                        dve.tensor_reduce(YE[:, j, P + 1:P + 2], T[j], AX.X, ALU.min).then_inc(min_ready, 1)
                    dve.wait_ge(min_ready, g * G4 + G4)
                    dve.tensor_tensor(opened, rest.rearrange("p (j k) -> p j k", j=G4)[:, :, 0], YE[:, :, P + 1],
                                      ALU.is_gt).then_inc(open_ready, 1)
                    dve.wait_ge(open_ready, g + 1)
                    dve.tensor_scalar(closed, opened, 1.0, -FAR, ALU.subtract, ALU.mult)
                    steps(g, 24, 2)
                    dve.wait_ge(bm_filled, g * FILLS + F_SLOT + 1)
                    dve.scalar_tensor_tensor(slot, BM[:, 0:G4], 1.0, opened, ALU.add, ALU.mult).then_inc(bm_read, 1)
                    dve.wait_ge(bm_read, g * FILLS + F_SLOT + 1)
                    dve.tensor_copy(PMALL[:, bass.ds(g * G4, G4)], slot)
                    for j in range(G4):
                        dve.tensor_scalar(slotm[j], coli[:, :], slot[:, j:j + 1], None, ALU.is_equal).then_inc(slotm_ready, 1)
                    steps(g, 26, 4)
                    dve.wait_ge(bm_read, g * FILLS + F_ROWS + 1)
                    dve.tensor_copy(taken, YO[:, P:P + 2])
                    for r in range(R2 // 8):
                        find8(YO[:, 0:P], topo[:, 8 * r:8 * r + 8])
                        locate8(YO[:, 0:P], topo[:, 8 * r:8 * r + 8])
                        onehots(g * ROUNDS + G4 + r, r)
                    dve.max(resto, YO[:, 0:P])
                    dve.drain()
                    dve.scalar_tensor_tensor(OPEN[:, bass.ds(g, 1)], resto[:, 0:1], taken[:, 1:2], taken[:, 0:1],
                                             ALU.is_gt, ALU.mult)
                    if has_next(g):
                        for part in range(SELECT_PARTS):
                            select(g + 1, 0, part)
                    for k in range(R2):
                        maximum(g, G4 * R1 + k, TO, topo[:, k:k + 1], first=(k == 0))
                        if k < 10:
                            steps(g, 30 + k, 1)
                    steps(g, 40, 2)
                    for j in range(G4):
                        maximum(g, G4 * R1 + R2 + j, T[j], closed[:, j:j + 1])
                        if j < 2:
                            steps(g, 42 + j, 1)

                dve.memset(YE[:, :, P], 1.0).then_inc(ones_made, 1)
                dve.memset(padded, 0.0).then_inc(ones_made, 1)
                dve.wait_ge(ones_made, 2)
                for part in range(SELECT_PARTS):
                    select(0, 0, part)
                all_groups(dve, iteration)

        with nc.Block() as block:
            o_steps, o_sum = sem("o_steps"), sem("o_sum")

            @block.vector
            def _(dve):
                link = Chain(dve, o_steps)
                link(dve.tensor_scalar(S[0], PMALL[:, :], float(P), None, ALU.is_gt))
                link(dve.tensor_reduce(S[1][:, 0:1], S[0], AX.X, ALU.max))
                link(dve.tensor_reduce(S[1][:, 1:2], OPEN[:, :], AX.X, ALU.max))
                link(dve.tensor_tensor(S[2][:, 0:1], S[1][:, 0:1], S[1][:, 1:2], ALU.max))
                dve.wait_ge(o_sum, 1)
                link(dve.tensor_reduce(S[3][0:1, 0:1], PS[0][0:1, 0:P], AX.X, ALU.max))
                link(dve.tensor_scalar(flag2[0:1, 0:1], S[3][0:1, 0:1], 0.0, None, ALU.is_gt))

            @block.tensor
            def _(pe):
                pe.wait_ge(o_steps, 4)
                pe.matmul(PS[0][0:1, 0:P], S[2][:, 0:1], ident[:, :], start=True, stop=True).then_inc(o_sum, 1)

        s5 = Pwl("p5")
        xn4 = xna
        with nc.Block() as block:
            d_xn, d_turned, d_xT = sem("d_xn"), sem("d_turned"), sem("d_xT")
            z_set, d_sel, d_row, d_max = sem("z_set"), sem("d_sel"), sem("d_row"), sem("d_max")
            d_cnt = sem("d_cnt")

            def if_open(eng):
                return eng.If(eng.value_load(flag2[0:1, 0:1]) > 0)

            @block.sync
            def _(sp):
                with if_open(sp):
                    store_groups(sp, s5)

            @block.tensor
            def _(pe):
                def group(g):
                    pe.wait_ge(d_xn, g * 4 + 4)
                    for j in range(G4):
                        last = pe.transpose(PS[0][:, j * P:(j + 1) * P], xn4[:, j * P:(j + 1) * P], ident[:, :])
                    last.then_inc(d_turned, 1)
                    with pe.Fori(0, P // 2) as d:
                        for p in range(2):
                            n = g * P + d * 2 + p
                            pe.wait_ge(d_xT, g + 1)
                            pe.wait_ge(d_sel, n + 1)
                            pe.matmul(PS[1 + p][:, :], sel[p], xT4, start=True, stop=True).then_inc(d_row, 1)
                    for c in range(NC):
                        m = g * NC + c
                        pe_function(pe, s5, m, c, 0)
                        for k in range(PE_TERMS):
                            pe_bend(pe, s5, m, c, k)
                        pe_function(pe, s5, m, c, 1)
                        pe_out(pe, s5, m, c, g)

                with if_open(pe):
                    group(0)
                    with pe.Fori(1, NG) as g:
                        group(g)

            @block.scalar
            def _(act):
                def group(g):
                    act.wait_ge(d_turned, g + 1)
                    act.copy(xT4, PS[0][:, :]).then_inc(d_xT, 1)
                    act.wait_ge(d_max, (g * P + P) * NC + NC)
                    for c in range(NC):
                        for part in (act_first, act_second, act_third):
                            part(act, s5, g * NC + c, c)

                with if_open(act):
                    group(0)
                    with act.Fori(1, NG) as g:
                        group(g)

            @block.vector
            def _(dve):
                def group(g):
                    for j in range(G4):
                        normalise(dve, xn4[:, j * P:(j + 1) * P], g * G4 + j).then_inc(d_xn, 1)
                    dve.memset(dcount, -1.0).then_inc(z_set, 1)
                    for c in range(NC):
                        dve.memset(Z[c], LOWEST).then_inc(z_set, 1)
                    with dve.Fori(0, P // 2) as d:
                        for p in range(2):
                            n = g * P + d * 2 + p
                            dve.wait_ge(z_set, g * (NC + 1) + NC + 1)
                            dve.tensor_scalar(dcount, dcount, 1.0, None, ALU.add).then_inc(d_cnt, 1)
                            dve.wait_ge(d_cnt, n + 1)
                            dve.tensor_scalar(sel[p], pidx[:, :], dcount, None, ALU.is_equal).then_inc(d_sel, 1)
                        for p in range(2):
                            n = g * P + d * 2 + p
                            dve.wait_ge(d_row, n + 1)
                            for c in range(NC):
                                dve.wait_ge(d_max, n * NC + c + 1)
                                dve.scalar_tensor_tensor(Z[c], PS[1 + p][:, :], WtS[:, c, bass.ds(d * 2 + p, 1)], Z[c],
                                                         ALU.add, ALU.max).then_inc(d_max, 1)
                    for c in range(NC):
                        for n in range(STEPS):
                            dve_step(dve, s5, g * NC + c, c, n)
                    dve_finish(dve, s5, g)

                with if_open(dve):
                    dve.sem_inc(d_max, NC)
                    group(0)
                    with dve.Fori(1, NG) as g:
                        group(g)


_INS = ['x', 'adj', 'L0_gnn_W_msg', 'L0_gnn_W_upd', 'L0_gnn_bias', 'L0_ffn_Wr', 'L0_ffn_br', 'L0_ffn_W1', 'L0_ffn_b1',
        'L0_ffn_g1', 'L0_ffn_be1', 'L0_ffn_m1', 'L0_ffn_v1', 'L0_ffn_W2', 'L0_ffn_b2', 'L0_ffn_g2', 'L0_ffn_be2',
        'L0_ffn_m2', 'L0_ffn_v2', 'L0_ffn_Wo', 'L0_ffn_bo', 'L1_gnn_W_fwd', 'L1_gnn_W_bwd', 'L1_gnn_W_loop',
        'L1_gnn_Wg_fwd', 'L1_gnn_Wg_bwd', 'L1_gnn_Wg_loop', 'L1_gnn_b_fwd', 'L1_gnn_b_bwd', 'L1_gnn_b_loop',
        'L1_gnn_bg_fwd', 'L1_gnn_bg_bwd', 'L1_gnn_bg_loop', 'L1_ffn_Wt', 'L1_ffn_bt', 'L1_ffn_sl_cvx', 'L1_ffn_of_cvx',
        'L1_ffn_sl_ccv', 'L1_ffn_of_ccv', 'L1_ffn_alpha', 'L1_ffn_Wc', 'L1_ffn_bc', 'L1_ffn_Wg', 'L1_ffn_bg',
        'L1_ffn_Wd', 'L1_ffn_bd']


def kernel(**inputs):
    import numpy as _np
    import concourse.bacc as _bacc
    from concourse import mybir as _mybir
    from concourse.bass_utils import run_bass_kernel_spmd as _run

    nc = _bacc.Bacc("TRN2", target_bir_lowering=False, num_devices=1)
    arrays, args = {}, {}
    for name in _INS:
        arr = _np.ascontiguousarray(inputs[name])
        arrays[f"in_{name}_dram"] = arr
        args[name] = nc.dram_tensor(f"in_{name}_dram", arr.shape, _mybir.dt.from_np(arr.dtype), kind="ExternalInput").ap()
    out = nc.dram_tensor("out_0_dram", (NT, P, P), _mybir.dt.float32, kind="ExternalOutput").ap()
    build(nc, args, out)
    r = _run(nc, [arrays], core_ids=[0])
    return r.results[0]["out_0_dram"]
```
